# Optimizing a Trainium2 kernel written in Bass

```python
import numpy as np
import jax
import jax.numpy as jnp

def _softmax(x, axis=-1):
    return jax.nn.softmax(x, axis=axis)

def _gelu(x):
    return jax.nn.gelu(x, approximate=True)

def _silu(x):
    return jax.nn.silu(x)

def _sigmoid(x):
    return jax.nn.sigmoid(x)

def _layernorm(x, axis=-1, eps=1e-05):
    m = jnp.mean(x, axis=axis, keepdims=True)
    v = jnp.var(x, axis=axis, keepdims=True)
    return (x - m) / jnp.sqrt(v + eps)

def _scatter_add(tgt, idx, src, axis=0):
    return tgt.at[idx].add(src)

def _segment_sum(src, seg, n):
    return jax.ops.segment_sum(src, seg, n)
kernel_name = 'mk_vit_tower_d1_tok_img256_r4_731083'

def setup_inputs(seed: int=0):
    np.random.seed(seed)
    _w = jnp.asarray

    def _rec_inputs():
        import jax
        import jax.numpy as jnp
        _rk = jax.random.key(seed)
        x = -0.0003702 + 0.999946 * jax.random.normal(jax.random.fold_in(_rk, 1), (64, 1, 224, 224), jnp.float32)
        return x
    x = _rec_inputs()

    def _L0_tok_setup():
        import jax, jax.numpy as jnp
        import numpy as np
        PH, PW = (64, 25)
        SH, SW = (64, 12)

        def _unfold(x, ph, pw, sh, sw):
            B, C, H, W = x.shape
            nh = (H - ph) // sh + 1
            nw = (W - pw) // sw + 1
            rows = jnp.arange(nh)[:, None] * sh + jnp.arange(ph)[None, :]
            cols = jnp.arange(nw)[:, None] * sw + jnp.arange(pw)[None, :]
            p = x[:, :, rows, :]
            p = p[:, :, :, :, cols]
            p = jnp.transpose(p, (0, 2, 4, 1, 3, 5))
            return p.reshape(B, nh * nw, C * ph * pw)
        key = jax.random.key(seed)
        kx, kw = jax.random.split(key, 2)
        x = jax.random.normal(kx, (64, 1, 64, 1000), dtype=jnp.float32)
        in_dim = 1 * PH * PW
        weight = jax.random.normal(kw, (in_dim, 64), dtype=jnp.float32) / np.sqrt(in_dim).astype(np.float32)
        bias = jnp.zeros((64,), dtype=jnp.float32)
        return {'x': x, 'weight': weight, 'bias': bias}
    _L0_tok_all = _L0_tok_setup()
    _L0_tok_in = {k: v for k, v in _L0_tok_all.items() if k in ('weight', 'bias')}
    del _L0_tok_all

    def _L0_attn_setup():
        import jax, jax.numpy as jnp
        import numpy as np
        B, N, C, H = (4, 256, 64, 8)
        HD = C // H
        BN_EPS = 1e-05
        key = jax.random.key(seed)
        ks = jax.random.split(key, 6)

        def w(k, shape, sc=0.02):
            return jax.random.normal(k, shape, jnp.float32) * sc
        return {'x': jax.random.normal(ks[0], (B, N, C), jnp.float32), 'w_qkv': w(ks[1], (3 * C, C)), 'b_qkv': jnp.zeros((3 * C,), jnp.float32), 'w_proj': w(ks[2], (C, C)), 'b_proj': jnp.zeros((C,), jnp.float32), 'scale': jnp.float32(HD ** (-0.5)), 'riem_scale': jnp.float32(HD ** (-0.5)), 'grassman_scale': jnp.float32(HD ** (-0.5)), 'bn_gamma': jnp.ones((3 * H,), jnp.float32), 'bn_beta': jnp.zeros((3 * H,), jnp.float32), 'bn_mean': jnp.zeros((3 * H,), jnp.float32), 'bn_var': jnp.ones((3 * H,), jnp.float32), 'conv_w': w(ks[3], (H, 3 * H)), 'conv_b': jnp.zeros((H,), jnp.float32)}
    _L0_attn_all = _L0_attn_setup()
    _L0_attn_in = {k: v for k, v in _L0_attn_all.items() if k in ('w_qkv', 'b_qkv', 'w_proj', 'b_proj', 'scale', 'riem_scale', 'grassman_scale', 'bn_gamma', 'bn_beta', 'bn_mean', 'bn_var', 'conv_w', 'conv_b')}
    del _L0_attn_all

    def _L0_ffn_setup():
        import jax, jax.numpy as jnp
        import numpy as np
        E, D, H, TOP_K = (6, 64, 64, 2)
        ROUTER_H = D // 2
        key = jax.random.key(seed)
        ks = jax.random.split(key, 12)
        s = 1.0 / np.sqrt(D)
        sh = 1.0 / np.sqrt(H)
        sr = 1.0 / np.sqrt(ROUTER_H)
        return {'features': jax.random.normal(ks[0], (8, 1024, D), dtype=jnp.float32), 'router_w1': jax.random.uniform(ks[1], (D, ROUTER_H), jnp.float32, -s, s), 'router_b1': jnp.zeros((ROUTER_H,), jnp.float32), 'router_w2': jax.random.uniform(ks[2], (ROUTER_H, E), jnp.float32, -sr, sr), 'router_b2': jnp.zeros((E,), jnp.float32), 'expert_w1': jax.random.uniform(ks[3], (E, D, H), jnp.float32, -s, s), 'expert_b1': jnp.zeros((E, H), jnp.float32), 'expert_w2': jax.random.uniform(ks[4], (E, H, H), jnp.float32, -sh, sh), 'expert_b2': jnp.zeros((E, H), jnp.float32), 'expert_w3': jax.random.uniform(ks[5], (E, H, D), jnp.float32, -sh, sh), 'expert_b3': jnp.zeros((E, D), jnp.float32)}
    _L0_ffn_all = _L0_ffn_setup()
    _L0_ffn_in = {k: v for k, v in _L0_ffn_all.items() if k in ('router_w1', 'router_b1', 'router_w2', 'router_b2', 'expert_w1', 'expert_b1', 'expert_w2', 'expert_b2', 'expert_w3', 'expert_b3')}
    del _L0_ffn_all
    return {'x': x, 'L0_tok_weight': _L0_tok_in['weight'], 'L0_tok_bias': _L0_tok_in['bias'], 'L0_attn_w_qkv': _L0_attn_in['w_qkv'], 'L0_attn_b_qkv': _L0_attn_in['b_qkv'], 'L0_attn_w_proj': _L0_attn_in['w_proj'], 'L0_attn_b_proj': _L0_attn_in['b_proj'], 'L0_attn_scale': _L0_attn_in['scale'], 'L0_attn_riem_scale': _L0_attn_in['riem_scale'], 'L0_attn_grassman_scale': _L0_attn_in['grassman_scale'], 'L0_attn_bn_gamma': _L0_attn_in['bn_gamma'], 'L0_attn_bn_beta': _L0_attn_in['bn_beta'], 'L0_attn_bn_mean': _L0_attn_in['bn_mean'], 'L0_attn_bn_var': _L0_attn_in['bn_var'], 'L0_attn_conv_w': _L0_attn_in['conv_w'], 'L0_attn_conv_b': _L0_attn_in['conv_b'], 'L0_ffn_router_w1': _L0_ffn_in['router_w1'], 'L0_ffn_router_b1': _L0_ffn_in['router_b1'], 'L0_ffn_router_w2': _L0_ffn_in['router_w2'], 'L0_ffn_router_b2': _L0_ffn_in['router_b2'], 'L0_ffn_expert_w1': _L0_ffn_in['expert_w1'], 'L0_ffn_expert_b1': _L0_ffn_in['expert_b1'], 'L0_ffn_expert_w2': _L0_ffn_in['expert_w2'], 'L0_ffn_expert_b2': _L0_ffn_in['expert_b2'], 'L0_ffn_expert_w3': _L0_ffn_in['expert_w3'], 'L0_ffn_expert_b3': _L0_ffn_in['expert_b3']}

def reference(x, L0_tok_weight, L0_tok_bias, L0_attn_w_qkv, L0_attn_b_qkv, L0_attn_w_proj, L0_attn_b_proj, L0_attn_scale, L0_attn_riem_scale, L0_attn_grassman_scale, L0_attn_bn_gamma, L0_attn_bn_beta, L0_attn_bn_mean, L0_attn_bn_var, L0_attn_conv_w, L0_attn_conv_b, L0_ffn_router_w1, L0_ffn_router_b1, L0_ffn_router_w2, L0_ffn_router_b2, L0_ffn_expert_w1, L0_ffn_expert_b1, L0_ffn_expert_w2, L0_ffn_expert_b2, L0_ffn_expert_w3, L0_ffn_expert_b3):
    import jax
    import jax.numpy as jnp

    def _L0_tok_ref(x, weight, bias):
        import jax, jax.numpy as jnp
        import numpy as np
        PH, PW = (64, 25)
        SH, SW = (64, 12)

        def _unfold(x, ph, pw, sh, sw):
            B, C, H, W = x.shape
            nh = (H - ph) // sh + 1
            nw = (W - pw) // sw + 1
            rows = jnp.arange(nh)[:, None] * sh + jnp.arange(ph)[None, :]
            cols = jnp.arange(nw)[:, None] * sw + jnp.arange(pw)[None, :]
            p = x[:, :, rows, :]
            p = p[:, :, :, :, cols]
            p = jnp.transpose(p, (0, 2, 4, 1, 3, 5))
            return p.reshape(B, nh * nw, C * ph * pw)
        p = _unfold(x, PH, PW, SH, SW)
        return jax.nn.gelu(jnp.einsum('bnk,kd->bnd', p, weight) + bias, approximate=False)

    def _L0_attn_ref(x, w_qkv, b_qkv, w_proj, b_proj, scale, riem_scale, grassman_scale, bn_gamma, bn_beta, bn_mean, bn_var, conv_w, conv_b):
        import jax, jax.numpy as jnp
        import numpy as np
        B, N, C, H = (4, 256, 64, 8)
        HD = C // H
        BN_EPS = 1e-05
        b, n, c = x.shape
        h, hd = (H, c // H)
        qkv = (x @ w_qkv.T + b_qkv).reshape(b, n, 3, h, hd).transpose(2, 0, 3, 1, 4)
        q, k, v = (qkv[0], qkv[1], qkv[2])
        qgr, _ = jnp.linalg.qr(q)
        kgr, _ = jnp.linalg.qr(k)
        attn_grass = jnp.einsum('bhnd,bhmd->bhnm', qgr, kgr) ** 2 * grassman_scale
        dots = jnp.einsum('bhnd,bhmd->bhnm', q, k)
        attn_eucl = dots * scale
        attn_riem = dots ** 2 * riem_scale
        a = jnp.concatenate([attn_eucl, attn_riem, attn_grass], axis=1)
        inv = (bn_gamma * jax.lax.rsqrt(bn_var + BN_EPS))[:, None, None]
        a = (a - bn_mean[:, None, None]) * inv + bn_beta[:, None, None]
        a = jnp.einsum('oc,bcnm->bonm', conv_w, a) + conv_b[None, :, None, None]
        a = jax.nn.softmax(a, axis=-1)
        out = jnp.einsum('bhnm,bhmd->bhnd', a, v)
        out = out.transpose(0, 2, 1, 3).reshape(b, n, c)
        return out @ w_proj.T + b_proj

    def _L0_ffn_ref(features, router_w1, router_b1, router_w2, router_b2, expert_w1, expert_b1, expert_w2, expert_b2, expert_w3, expert_b3):
        import jax, jax.numpy as jnp
        import numpy as np
        E, D, H, TOP_K = (6, 64, 64, 2)
        ROUTER_H = D // 2
        rh = jax.nn.relu(features @ router_w1 + router_b1)
        expert_logits = jax.nn.softmax(rh @ router_w2 + router_b2, axis=-1)
        top_w, top_i = jax.lax.top_k(expert_logits, TOP_K)
        routing_weights = jax.nn.softmax(top_w, axis=-1)
        h1 = jax.nn.relu(jnp.einsum('bsd,edh->bseh', features, expert_w1) + expert_b1)
        h2 = jax.nn.relu(jnp.einsum('bseh,ehf->bsef', h1, expert_w2) + expert_b2)
        expert_out = jnp.einsum('bsef,efo->bseo', h2, expert_w3) + expert_b3
        sel = jnp.take_along_axis(expert_out, top_i[:, :, :, None], axis=2)
        combined = jnp.sum(sel * routing_weights[..., None], axis=2)
        return combined
    h = _L0_tok_ref(x, L0_tok_weight, L0_tok_bias)
    h = h + _L0_attn_ref(_layernorm(h, axis=-1), L0_attn_w_qkv, L0_attn_b_qkv, L0_attn_w_proj, L0_attn_b_proj, L0_attn_scale, L0_attn_riem_scale, L0_attn_grassman_scale, L0_attn_bn_gamma, L0_attn_bn_beta, L0_attn_bn_mean, L0_attn_bn_var, L0_attn_conv_w, L0_attn_conv_b)
    h = h + _L0_ffn_ref(_layernorm(h, axis=-1), L0_ffn_router_w1, L0_ffn_router_b1, L0_ffn_router_w2, L0_ffn_router_b2, L0_ffn_expert_w1, L0_ffn_expert_b1, L0_ffn_expert_w2, L0_ffn_expert_b2, L0_ffn_expert_w3, L0_ffn_expert_b3)
    return h

_drawn_inputs = setup_inputs


def setup_inputs(seed=0):
    import zlib

    import numpy as np

    out = dict(_drawn_inputs(seed))
    spreads = {'L0_tok_bias': (0.0, 0.1),
     'L0_attn_b_qkv': (0.0, 0.1),
     'L0_attn_b_proj': (0.0, 0.1),
     'L0_attn_bn_gamma': (1.0, 0.6),
     'L0_attn_bn_beta': (0.0, 0.8),
     'L0_attn_bn_mean': (0.0, 0.8),
     'L0_attn_bn_var': (1.0, 0.6),
     'L0_attn_conv_b': (0.0, 0.8),
     'L0_ffn_router_b1': (0.0, 0.1),
     'L0_ffn_router_b2': (0.0, 0.1),
     'L0_ffn_expert_b1': (0.0, 0.463),
     'L0_ffn_expert_b2': (0.0, 0.1),
     'L0_ffn_expert_b3': (0.0, 0.1)}
    factors = {'L0_attn_w_qkv': 4.177, 'L0_attn_conv_w': 8.0}
    for name, (base, spread) in spreads.items():
        noise = np.random.default_rng([zlib.crc32(name.encode()), seed]).standard_normal(out[name].shape)
        drawn = base * np.exp(spread * noise) if base else spread * noise
        out[name] = jnp.asarray(drawn.astype(out[name].dtype))
    for name, factor in factors.items():
        out[name] = (out[name] * factor).astype(out[name].dtype)
    return out
```

```python
from contextlib import ExitStack

import concourse.bass as bass
from concourse import mybir

B, IMG = 64, 224
PH, PW, SH, SW = 64, 25, 64, 12
NH = (IMG - PH) // SH + 1
NW = (IMG - PW) // SW + 1
N = NH * NW
C, H = 64, 8
D = C // H
E, RH = 6, 32
EPS = 1e-5

PAIRS = B // 2
COLS = PAIRS * N
GROUPS = 4
GP = PAIRS // GROUPS
GN = GP * N
NC4 = 4
NI = 13
HI = H * NI
XW = SW * (NW - 1) + PW + 1
XG = GP * NH * XW
WO = (PW + 1) // 2
TT = 2 * N
T2 = PAIRS // 2

ROUTE_LOGITS = 3
ROUTE_TOP = ROUTE_LOGITS + 3 + 3 * (E - 1) + 2
ROUTE_ALL = ROUTE_TOP + 5

def _columns():
    at, where = 0, {}
    for name, n in [("tok_a", WO * C), ("tok_b", WO * C), ("vec", 32),
                    ("ident", 128), ("center", 128), ("avg", 128), ("headmask", H), ("eye8", D * D),
                    ("wq", 128), ("wk", 128), ("wqkv_a", 3 * C), ("wqkv_b", 3 * C), ("bqk", 2 * C),
                    ("conv", 3 * HI), ("wproj", 128), ("wr1", 2 * RH), ("wr2", 2 * E), ("b3", 128),
                    ("w1", 6 * 128), ("w2", 3 * 128), ("w3", 3 * 128)]:
        where[name] = (at, at + n)
        at += n
    return where, at


COL, NCOLS = _columns()
VEC = {n: i for i, n in enumerate(
    ["tok_bias", "bq", "bk", "bv", "bproj", "br1", "br2", "b1_0", "b1_1", "b1_2", "b2_0", "b2_1", "b2_2",
     "gamma_0", "gamma_1", "gamma_2", "beta_0", "beta_1", "beta_2", "mean_0", "mean_1", "mean_2",
     "var_0", "var_1", "var_2", "conv_b", "scale_0", "scale_1", "scale_2", "eps"])}


def vit_tower_kernel(nc, x, wpack, out):
    f32 = mybir.dt.float32
    ALU = mybir.AluOpType
    ACT = mybir.ActivationFunctionType
    AX = mybir.AxisListType.X
    ds = bass.ds

    with ExitStack() as ctx:
        def sb(name, shape):
            return ctx.enter_context(nc.sbuf_tensor(name, shape, f32))

        def sem(name):
            return ctx.enter_context(nc.semaphore(name))

        bank = [ctx.enter_context(nc.psum_tensor(f"bank{i}", [128, 512], f32)) for i in range(8)]

        W = sb("weights", [128, NCOLS])

        def w(name, rows=128):
            a, b = COL[name]
            return W[0:rows, a:b]

        def vec(name, rows=128, n=1):
            a = COL["vec"][0] + VEC[name]
            return W[0:rows, a:a + n]

        ident = w("ident")
        h_sb = sb("h", [128, COLS])
        q_sb = sb("q", [128, COLS + 4])
        k_sb = sb("k", [128, COLS])
        n_sb = sb("normed", [128, COLS])
        KBD = sb("kbd", [128, PAIRS * 4 * N])
        VBD = sb("vbd", [128, PAIRS * H * 2 * (D + 1)])
        big = sb("big", [128, 4 * XG])
        kbd = KBD[:, :].rearrange("p (a g k n) -> p a g k n", a=PAIRS, g=2, k=2)
        vbd = VBD[:, :].rearrange("p (a h g d) -> p a h g d", a=PAIRS, h=H, g=2)

        pix = [[big[:, (2 * b + half) * XG:(2 * b + half + 1) * XG].rearrange("p (a c) -> p a c", c=XW)
                for half in range(2)] for b in range(2)]

        at = [0]

        def part(n):
            a = at[0]
            at[0] += n
            assert at[0] <= 4 * XG
            return big[:, a:a + n]

        xc = part(COLS)
        sq = part(COLS)
        rstd = part(COLS)
        qk_tok = [part(2 * 4 * C) for _ in range(2)]
        gmask = [part(4 * C) for _ in range(2)]
        cgram = part(PAIRS * 2 * D)
        aug = part(H * D * 3 * D)
        etmp = part(H * D * 2 * D)
        small = part(H * D * 8)
        iq = part(4 * D * D)
        ik = part(4 * D * D)
        prods = part(D * 4 * D * D)
        mmat = part(4 * D * D)
        bdm = part(PAIRS * 128)
        at[0] = 0
        er = [part(3 * 2 * NC4 * N) for _ in range(2)]
        tb = [part(2 * NC4 * N) for _ in range(2)]
        pts = [part(NC4 * HI) for _ in range(2)]
        rmax = [part(8) for _ in range(2)]
        rmaxc = [part(8) for _ in range(2)]
        rsum = [part(16) for _ in range(2)]
        assert at[0] <= 3 * COLS + 4 * 4 * C + 8 * C
        convw = sb("convw", [HI, 3 * HI])
        mixc = sb("mixc", [HI, 16])
        qbd = [sb(f"qbd{u}", [128, NC4 * HI]) for u in range(2)]
        on = [sb(f"heads{u}", [96, 128]) for u in range(2)]
        pr = [sb(f"probs{u}", [HI, NC4 * 128]) for u in range(2)]

        at[0] = 0
        xc2, sq2, rstd2 = part(COLS), part(COLS), part(COLS)
        rh = part(COLS)
        lg = part(COLS)
        wt = part(COLS)
        h1 = [part(GN) for _ in range(2)]
        h2 = [part(3 * GN) for _ in range(2)]
        hb = [part(GN) for _ in range(2)]
        osb = part(B // 2 * C)
        rt = [part(2 * E * T2) for _ in range(7)]
        r1 = [part(2 * T2) for _ in range(4)]

        S = {n: sem(n) for n in """
            w_embed w_rest pix0 pix1 pix2 pix3 shifted embed gelu_done
            xc_done sq_done var_mm std_done rcp_done xn_done
            zero_kbd zero_vbd q_mm k_mm q_done k_done kbd_k
            tok_mm qk_tok_done v_tok_done gram_mm gmask_done cgram_done
            atop_mm g_mm aug_done elim lu mstep z_mm bd_done kp_mm kp_done
            prep zero_tok pad_q cvec_mm cvec sqv
            qbd_ready dots sq3 mix rmax_s rmaxc_s sub_s exp_s tr_s pt_s av_s rsum_s on_s ot_s o_done
            proj_mm h_attn cen_mm
            xc2_done sq2_done var2_mm std2_done rcp2_done xn2_done cen2_mm
            rh_mm rh_done lg_mm lg_done lt_mm route wt_mm wt_done
            l1 h1_done l2 h2_done b3_mm hb_done l3 comb stored route_exp
            """.split()}

        block = ctx.enter_context(nc.Block())

        outf = out[:, :, :].rearrange("b n c -> (b n) c")

        def pixels(half, g, i):
            b0 = half * PAIRS + g * GP
            return x[b0:b0 + GP, 0, i * SH:i * SH + PH, 0:XW].rearrange("b r c -> r b c")

        @block.sync
        def _(sp):
            a, b = COL["tok_a"][0], COL["vec"][1]
            sp.dma_start(W[:, a:b], wpack[:, a:b]).then_inc(S["w_embed"], 16)
            for g in range(GROUPS):
                for half in range(2):
                    if g >= 2:
                        sp.wait_ge(S["embed"], g - 1)
                    dst = pix[g % 2][half][64 * half:64 * half + 64, :, :]
                    for i in range(NH):
                        sp.dma_start(dst[:, i:GP * NH:NH, :], pixels(half, g, i)).then_inc(S[f"pix{g}"], 16)
                if g == 0:
                    sp.dma_start(W[:, b:NCOLS], wpack[:, b:NCOLS]).then_inc(S["w_rest"], 16)
            for g in range(GROUPS):
                for half in range(2):
                    sp.wait_ge(S["comb"], 4 * (2 * g + half + 1))
                    r0 = half * COLS + g * GN
                    sp.dma_start(outf[r0:r0 + GN, :].rearrange("(t p) c -> p t c", p=TT),
                                 osb[0:TT, (half * T2 + 4 * g) * C:(half * T2 + 4 * g + 4) * C]
                                 .rearrange("p (t c) -> p t c", c=C)).then_inc(S["stored"], 16)
            sp.wait_ge(S["stored"], 16 * 2 * GROUPS)

        @block.gpsimd
        def _(pool):
            pool.memset(KBD[:, :], 0.0).then_inc(S["zero_kbd"], 1)
            pool.memset(VBD[:, :], 0.0).then_inc(S["zero_vbd"], 1)
            for u in range(2):
                pool.memset(pr[u][:, :], 0.0).then_inc(S["pad_q"], 1)
                pool.memset(on[u][:, :], 0.0).then_inc(S["pad_q"], 1)
            pool.memset(q_sb[:, COLS:COLS + 4], 0.0).then_inc(S["pad_q"], 1)
            pool.wait_ge(S["pad_q"], 5)
            for half in range(2):
                pool.wait_ge(S["zero_vbd"], 1 + half)
                pool.memset(vbd[64 * half:64 * half + N, :, :, half, D:D + 1], 1.0).then_inc(S["zero_vbd"], 1)
            pool.wait_ge(S["embed"], 4)
            pool.wait_ge(S["zero_vbd"], 3)
            for u in range(2):
                pool.memset(qk_tok[u], 0.0).then_inc(S["zero_tok"], 1)
            for g in range(GROUPS):
                pool.wait_ge(S["k_done"], g + 1)
                pool.wait_ge(S["zero_kbd"], 1)
                pool.wait_ge(S["zero_tok"], 2)
                for half in range(2):
                    if g + half > 0:
                        pool.wait_ge(S["kbd_k"], 2 * g + half)
                    pool.tensor_copy(kbd[64 * half:64 * half + 64, g * GP:(g + 1) * GP, half, 0, :],
                                     k_sb[64 * half:64 * half + 64, g * GN:(g + 1) * GN]
                                     .rearrange("p (a n) -> p a n", n=N)).then_inc(S["kbd_k"], 1)

            def block_queries(s, u, wait):
                if wait:
                    pool.wait_ge(S["dots"], 2 * s - 2)
                qv = q_sb[:, ds(s * N, NC4 * NI)].rearrange("p (c i) -> p c i", i=NI)
                pool.tensor_tensor(qbd[u][:, :].rearrange("p (c h i) -> p c h i", c=NC4, h=H),
                                   qv.unsqueeze(2).to_broadcast([128, NC4, H, NI]),
                                   w("headmask").unsqueeze(1).unsqueeze(3).to_broadcast([128, NC4, H, NI]),
                                   ALU.mult).then_inc(S["qbd_ready"], 1)

            pool.wait_ge(S["kbd_k"], 2 * GROUPS)
            pool.wait_ge(S["q_done"], GROUPS)
            pool.wait_ge(S["w_rest"], 16)
            pool.wait_ge(S["pad_q"], 5)
            for s in range(2):
                block_queries(s, s, False)
            with pool.Fori(0, (PAIRS - 2) // 2) as i:
                for u in range(2):
                    block_queries(2 * i + (2 + u), u, True)

        def act_norm(act, tag, xcb, sqb, rsb):
            for g in range(GROUPS + 1):
                if g < GROUPS:
                    act.wait_ge(S["xc" + tag + "_done"], g + 1)
                    nc.scalar.activation(sqb[:, g * GN:(g + 1) * GN], xcb[:, g * GN:(g + 1) * GN],
                                         ACT.Square).then_inc(S["sq" + tag + "_done"], 1)
                if g >= 1:
                    act.wait_ge(S["var" + tag + "_mm"], g)
                    nc.scalar.activation(rsb[:, (g - 1) * GN:g * GN], bank[4 + (g - 1) % 2][:, 0:GN], ACT.Sqrt,
                                         bias=vec("eps")).then_inc(S["std" + tag + "_done"], 1)

        @block.scalar
        def _(act):
            act.wait_ge(S["w_embed"], 16)
            nc.scalar.activation(mixc[0:HI, 0:3], vec("var_0", HI, 3), ACT.Sqrt, bias=vec("eps", HI)).then_inc(S["sqv"], 1)
            for g in range(GROUPS):
                act.wait_ge(S["embed"], g + 1)
                nc.scalar.activation(h_sb[:, g * GN:(g + 1) * GN], bank[g % 2][:, 0:GN], ACT.Gelu,
                                     bias=vec("tok_bias")).then_inc(S["gelu_done"], 1)
            act_norm(act, "", xc, sq, rstd)
            for g in range(GROUPS):
                act.wait_ge(S["q_mm"], g + 1)
                nc.scalar.activation(q_sb[:, g * GN:(g + 1) * GN], bank[6][:, 0:GN], ACT.Identity,
                                     bias=vec("bq")).then_inc(S["q_done"], 1)
                act.wait_ge(S["k_mm"], g + 1)
                nc.scalar.activation(k_sb[:, g * GN:(g + 1) * GN], bank[7][:, 0:GN], ACT.Identity,
                                     bias=vec("bk")).then_inc(S["k_done"], 1)
            act.wait_ge(S["zero_vbd"], 3)
            for t in range(T2):
                act.wait_ge(S["qk_tok_done"], 2 * (t + 1))
                for half in range(2):
                    r = slice(64 * half, 64 * half + N)
                    v = bank[t % 2][r, 0:6 * C].rearrange("p (a c) -> p a c", a=2)[:, :, 2 * C:3 * C]
                    nc.scalar.activation(vbd[r, 2 * t:2 * t + 2, :, half, 0:D],
                                         v.rearrange("p a (h d) -> p a h d", d=D),
                                         ACT.Copy).then_inc(S["v_tok_done"], 1)
            act.wait_ge(S["elim"], 4 * (D - 1) + 1)
            nc.scalar.activation(small[:, 64:128], small[:, 0:64], ACT.Sqrt).then_inc(S["elim"], 1)
            for g in range(GROUPS):
                act.wait_ge(S["kp_mm"], g + 1)
                for half in range(2):
                    r = slice(64 * half, 64 * half + 64)
                    nc.scalar.activation(kbd[r, g * GP:(g + 1) * GP, half, 1, :],
                                         bank[1 + g % 2][r, 0:GN].rearrange("p (a n) -> p a n", n=N),
                                         ACT.Copy).then_inc(S["kp_done"], 1)

            def squares(s, u, wait):
                if wait:
                    act.wait_ge(S["mix"], s - 1)
                for b in range(2):
                    act.wait_ge(S["dots"], 2 * s + (b + 1))
                    src = bank[b][0:HI, 0:8 * N].rearrange("p (a k n) -> p a k n", a=4, k=2)
                    e = er[u][0:HI, 4 * b * N:4 * (b + 1) * N].rearrange("p (a n) -> p a n", a=4)
                    r = er[u][0:HI, (8 + 8 * b) * N:(16 + 8 * b) * N]
                    nc.scalar.activation(e, src[:, :, 0, :], ACT.Copy).then_inc(S["sq3"], 1)
                    nc.scalar.activation(r, bank[b][0:HI, 0:8 * N], ACT.Square).then_inc(S["sq3"], 1)

            def exponentials(s, u, wait):
                act.wait_ge(S["sub_s"], s + 1)
                if wait:
                    act.wait_ge(S["tr_s"], s - 1)
                dst = pr[u][:, :].rearrange("p (c g n) -> p (c g) n", g=2, n=64)[:, :, 0:N]
                nc.scalar.activation(dst, tb[u][0:HI, :].rearrange("p (a n) -> p a n", n=N),
                                     ACT.Exp).then_inc(S["exp_s"], 1)

            def heads_out(s):
                act.wait_ge(S["ot_s"], s + 1)
                nc.scalar.activation(n_sb[:, ds(s * N, N)], bank[5][:, 0:N], ACT.Identity,
                                     bias=vec("bv")).then_inc(S["o_done"], 1)

            def step(s, u, steady):
                if steady or 2 <= s < PAIRS + 2:
                    exponentials(s - 2, u, steady or s >= 4)
                if steady or s < PAIRS:
                    squares(s, u, steady or s >= 2)
                if steady or s >= 3:
                    heads_out(s - 3)

            for s in range(4):
                step(s, s % 2, False)
            with act.Fori(0, (PAIRS - 4) // 2) as i:
                for u in range(2):
                    step(2 * i + (4 + u), u, True)
            for s in range(PAIRS, PAIRS + 3):
                step(s, s % 2, False)

            act_norm(act, "2", xc2, sq2, rstd2)
            for g in range(GROUPS):
                act.wait_ge(S["rh_mm"], g + 1)
                nc.scalar.activation(rh[0:2 * RH, g * GN:(g + 1) * GN], bank[6][0:2 * RH, 0:GN], ACT.Relu,
                                     bias=vec("br1", 2 * RH)).then_inc(S["rh_done"], 1)
                act.wait_ge(S["lg_mm"], g + 1)
                nc.scalar.activation(lg[0:2 * E, g * GN:(g + 1) * GN], bank[7][0:2 * E, 0:GN], ACT.Identity,
                                     bias=vec("br2", 2 * E)).then_inc(S["lg_done"], 1)
            act.wait_ge(S["route"], ROUTE_LOGITS)
            nc.scalar.activation(rt[1][0:TT, :], rt[0][0:TT, :], ACT.Exp).then_inc(S["route_exp"], 1)
            act.wait_ge(S["route"], ROUTE_TOP)
            nc.scalar.activation(rt[5][0:TT, :], rt[4][0:TT, :], ACT.Exp).then_inc(S["route_exp"], 1)
            for g in range(GROUPS):
                act.wait_ge(S["wt_mm"], g + 1)
                nc.scalar.activation(wt[0:2 * E, g * GN:(g + 1) * GN], bank[2 + g % 2][0:2 * E, 0:GN],
                                     ACT.Copy).then_inc(S["wt_done"], 1)
            for n in range(2 * GROUPS):
                for j in range(3):
                    m = 3 * n + j
                    if m >= 2:
                        act.wait_ge(S["l2"], m - 1)
                    act.wait_ge(S["l1"], m + 1)
                    nc.scalar.activation(h1[m % 2], bank[m % 2][:, 0:GN], ACT.Relu,
                                         bias=vec(f"b1_{j}")).then_inc(S["h1_done"], 1)

        def dve_norm(dve, tag, cen, src_banks, xcb, rsb, dst):
            for g in range(GROUPS + 1):
                if g < GROUPS:
                    dve.wait_ge(S[cen], g + 1)
                    nc.vector.tensor_copy(xcb[:, g * GN:(g + 1) * GN],
                                          bank[2 + g % 2][:, 0:GN]).then_inc(S["xc" + tag + "_done"], 1)
                if g >= 1:
                    c = slice((g - 1) * GN, g * GN)
                    dve.wait_ge(S["std" + tag + "_done"], g)
                    nc.vector.reciprocal(rsb[:, c], rsb[:, c]).then_inc(S["rcp" + tag + "_done"], 1)
                    dve.wait_ge(S["rcp" + tag + "_done"], g)
                    dve.wait_ge(S["xc" + tag + "_done"], g)
                    nc.vector.tensor_tensor(dst[:, c], xcb[:, c], rsb[:, c], ALU.mult).then_inc(S["xn" + tag + "_done"], 1)

        @block.vector
        def _(dve):
            for g in range(GROUPS):
                dve.wait_ge(S[f"pix{g}"], 16 * 2 * NH)
                if g >= 2:
                    dve.wait_ge(S["embed"], g - 1)
                for half in range(2):
                    src = pix[g % 2][half][64 * half:64 * half + 64, :, 1:XW]
                    nc.vector.tensor_copy(pix[g % 2][half][64 * (1 - half):64 * (1 - half) + 64, :, 0:XW - 1],
                                          src).then_inc(S["shifted"], 1)
            prep = [0]

            def link(ins, name="prep", box=prep):
                box[0] += 1
                ins.then_inc(S[name], 1)
                dve.wait_ge(S[name], box[0])

            dve.wait_ge(S["sqv"], 1)
            dve.wait_ge(S["w_rest"], 16)
            link(nc.vector.reciprocal(mixc[0:HI, 3:6], mixc[0:HI, 0:3]))
            link(nc.vector.tensor_tensor(mixc[0:HI, 6:9], mixc[0:HI, 3:6], vec("gamma_0", HI, 3), ALU.mult))
            link(nc.vector.tensor_tensor(mixc[0:HI, 9:12], mixc[0:HI, 6:9], vec("scale_0", HI, 3), ALU.mult))
            link(nc.vector.tensor_tensor(mixc[0:HI, 12:15], mixc[0:HI, 6:9], vec("mean_0", HI, 3), ALU.mult))
            link(nc.vector.tensor_tensor(mixc[0:HI, 0:3], vec("beta_0", HI, 3), mixc[0:HI, 12:15], ALU.subtract))
            for k in range(3):
                cw = w("conv", HI)[:, k * HI:(k + 1) * HI]
                link(nc.vector.tensor_scalar(convw[0:HI, k * HI:(k + 1) * HI], cw, mixc[0:HI, 9 + k:10 + k], None, ALU.mult))
            dve_norm(dve, "", "cen_mm", None, xc, rstd, n_sb)
            dve.wait_ge(S["cvec_mm"], 1)
            nc.vector.tensor_tensor(mixc[0:HI, 15:16], bank[4][0:HI, 0:1], vec("conv_b", HI), ALU.add).then_inc(S["cvec"], 1)

            def gram_blocks(t):
                dve.wait_ge(S["gram_mm"], t + 1)
                gm = gmask[t % 2][:, :].rearrange("p (a h d) -> p a h d", a=4, h=H)
                if t >= 2:
                    dve.wait_ge(S["cgram_done"], t - 1)
                for half in range(2):
                    r = slice(64 * half, 64 * half + 64)
                    src = bank[6 + t % 2][r, :].rearrange("p (a c) -> p a c", a=4)[:, :, 64 * half:64 * half + 64]
                    nc.vector.tensor_tensor(gm[r], src.rearrange("p a (h d) -> p a h d", d=D),
                                            w("headmask")[r].unsqueeze(1).unsqueeze(3).to_broadcast([64, 4, H, D]),
                                            ALU.mult).then_inc(S["gmask_done"], 1)
                dve.wait_ge(S["gmask_done"], 2 * (t + 1))
                nc.vector.tensor_reduce(cgram[:, t * 32:(t + 1) * 32].rearrange("p (a d) -> p a d", a=4),
                                        gm.rearrange("p a h d -> p a d h"), AX, ALU.add).then_inc(S["cgram_done"], 1)

            dve.wait_ge(S["zero_tok"], 2)
            for t in range(T2):
                dve.wait_ge(S["tok_mm"], t + 1)
                if t >= 2:
                    dve.wait_ge(S["gram_mm"], t - 1)
                for half in range(2):
                    r = slice(64 * half, 64 * half + N)
                    src = bank[t % 2][r, 0:6 * C].rearrange("p (a c) -> p a c", a=2)[:, :, 0:2 * C]
                    dst = qk_tok[t % 2][r, :].rearrange("p (a k g c) -> p a k g c", a=2, k=2, g=2)[:, :, :, half, :]
                    nc.vector.tensor_tensor(dst, src.rearrange("p a (k c) -> p a k c", k=2),
                                            w("bqk")[r].rearrange("p (k c) -> p k c", k=2).unsqueeze(1)
                                            .to_broadcast([N, 2, 2, C]), ALU.add).then_inc(S["qk_tok_done"], 1)
                if t >= 1:
                    gram_blocks(t - 1)
            gram_blocks(T2 - 1)

            A = aug.rearrange("p (h d c) -> p h d c", h=H, d=D)
            dve.wait_ge(S["w_rest"], 16)
            nc.vector.tensor_copy(A[:, :, :, 2 * D:3 * D],
                                  w("eye8").rearrange("p (d c) -> p d c", d=D).unsqueeze(1)
                                  .to_broadcast([128, H, D, D])).then_inc(S["aug_done"], 1)
            dve.wait_ge(S["atop_mm"], 1)
            nc.vector.tensor_copy(A[:, :, :, D:2 * D],
                                  bank[5][:, :].rearrange("p (n h d) -> p h d n", n=D, h=H)).then_inc(S["aug_done"], 1)
            dve.wait_ge(S["g_mm"], 1)
            nc.vector.tensor_copy(A[:, :, :, 0:D],
                                  bank[4][:, :].rearrange("p (n h d) -> p h d n", n=D, h=H)).then_inc(S["aug_done"], 1)
            dve.wait_ge(S["aug_done"], 3)
            el = [0]

            def link_e(ins):
                link(ins, "elim", el)

            rc = small[:, 128:136]
            lrow = small[:, 136:192].rearrange("p (h i) -> p h i", h=H)
            for j in range(D - 1):
                m = D - 1 - j
                link_e(nc.vector.reciprocal(rc, A[:, :, j, j]))
                link_e(nc.vector.tensor_tensor(lrow[:, :, 0:m], A[:, :, j, j + 1:D],
                                               rc.unsqueeze(2).to_broadcast([128, H, m]), ALU.mult))
                tmp = etmp[:, 0:H * m * 16].rearrange("p (h i c) -> p h i c", h=H, i=m)
                link_e(nc.vector.tensor_tensor(tmp, lrow[:, :, 0:m].unsqueeze(3).to_broadcast([128, H, m, 16]),
                                               A[:, :, j:j + 1, j + 1:j + 17].to_broadcast([128, H, m, 16]), ALU.mult))
                rows = A[:, :, j + 1:D, j + 1:j + 17]
                link_e(nc.vector.tensor_tensor(rows, rows, tmp, ALU.subtract))
            diag = aug.rearrange("p (h r) -> p h r", h=H)[:, :, 0:D * 3 * D:3 * D + 1]
            piv = small[:, 0:64].rearrange("p (h d) -> p h d", h=H)
            link_e(nc.vector.tensor_copy(piv, diag))
            el[0] += 1
            dve.wait_ge(S["elim"], el[0])
            link_e(nc.vector.reciprocal(small[:, 64:128], small[:, 64:128]))
            rs = small[:, 64:128].rearrange("p (h d) -> p h d", h=H)
            both = A[:, :, :, D:3 * D]
            link_e(nc.vector.tensor_tensor(both, both, rs.unsqueeze(3).to_broadcast([128, H, D, 2 * D]), ALU.mult))
            lu = [0]

            def link_l(ins):
                link(ins, "lu", lu)

            u_ = small[:, 192:256].rearrange("p (h d) -> p h d", h=H)
            npv = small[:, 256:264]
            nrc = small[:, 264:272]
            lc = small[:, 272:336].rearrange("p (h i) -> p h i", h=H)
            for j in range(D):
                tjj = A[:, :, j, D + j]
                link_l(nc.vector.tensor_scalar(u_[:, :, j], tjj, 0.0, -2.0, ALU.is_ge, ALU.mult))
                if j == D - 1:
                    break
                m = D - 1 - j
                link_l(nc.vector.scalar_tensor_tensor(npv, u_[:, :, j], 1.0, tjj, ALU.add, ALU.subtract))
                link_l(nc.vector.reciprocal(nrc, npv))
                link_l(nc.vector.tensor_tensor(lc[:, :, 0:m], A[:, :, j, D + j + 1:2 * D],
                                               nrc.unsqueeze(2).to_broadcast([128, H, m]), ALU.mult))
                tmp = etmp[:, 0:H * m * m].rearrange("p (h k i) -> p h k i", h=H, k=m)
                link_l(nc.vector.tensor_tensor(tmp, A[:, :, j + 1:D, D + j].unsqueeze(3).to_broadcast([128, H, m, m]),
                                               lc[:, :, 0:m].unsqueeze(2).to_broadcast([128, H, m, m]), ALU.mult))
                tr = A[:, :, j + 1:D, D + j + 1:2 * D]
                link_l(nc.vector.tensor_tensor(tr, tr, tmp, ALU.add))
            sg = small[:, 336:400]
            link_l(nc.vector.tensor_scalar(sg, small[:, 192:256], 1.0, None, ALU.add))
            sgv = sg.rearrange("p (h d) -> p h d", h=H)
            for dst, src_half in ((iq, 0), (ik, 1)):
                for hg in range(2):
                    r = slice(64 * src_half, 64 * src_half + 64)
                    hh = slice(4 * hg, 4 * hg + 4)
                    nc.vector.tensor_tensor(dst[64 * hg:64 * hg + 64, :].rearrange("p (h j c) -> p h j c", h=4, j=D),
                                            A[r, hh, :, 2 * D:3 * D],
                                            sgv[r, hh, :].unsqueeze(3).to_broadcast([64, 4, D, D]),
                                            ALU.mult).then_inc(S["mstep"], 1)
            dve.wait_ge(S["mstep"], 4)
            iqv = iq.rearrange("p (h j c) -> p h j c", h=4, j=D)
            ikv = ik.rearrange("p (h j c) -> p h j c", h=4, j=D)
            for j in range(D):
                nc.vector.tensor_tensor(prods[:, j * 256:(j + 1) * 256].rearrange("p (h c a) -> p h c a", h=4, c=D),
                                        iqv[:, :, j, :].unsqueeze(3).to_broadcast([128, 4, D, D]),
                                        ikv[:, :, j, :].unsqueeze(2).to_broadcast([128, 4, D, D]),
                                        ALU.mult).then_inc(S["mstep"], 1)
            dve.wait_ge(S["mstep"], 12)
            nc.vector.tensor_tensor(prods[:, 0:1024], prods[:, 0:1024], prods[:, 1024:2048], ALU.add).then_inc(S["mstep"], 1)
            dve.wait_ge(S["mstep"], 13)
            nc.vector.tensor_tensor(prods[:, 0:512], prods[:, 0:512], prods[:, 512:1024], ALU.add).then_inc(S["mstep"], 1)
            dve.wait_ge(S["mstep"], 14)
            nc.vector.tensor_tensor(mmat.rearrange("p (c h a) -> p h c a", c=D, h=4),
                                    prods[:, 0:256].rearrange("p (h c a) -> p h c a", h=4, c=D),
                                    prods[:, 256:512].rearrange("p (h c a) -> p h c a", h=4, c=D),
                                    ALU.add).then_inc(S["mstep"], 1)
            nc.vector.memset(bdm, 0.0).then_inc(S["bd_done"], 1)
            dve.wait_ge(S["bd_done"], 1)
            dve.wait_ge(S["z_mm"], 1)
            z = bank[0][:, 0:256].rearrange("p (c a) -> p a c", c=D)
            for g in range(GROUPS):
                for half in range(2):
                    r = slice(64 * half, 64 * half + 64)
                    dst = bdm[r, g * GP * 128:(g + 1) * GP * 128].rearrange("p (a c) -> p a c", c=128)
                    nc.vector.tensor_tensor(dst[:, :, 64 * half:64 * half + 64].rearrange("p a (h c) -> p a h c", c=D),
                                            z[r, g * GP:(g + 1) * GP, :].unsqueeze(2).to_broadcast([64, GP, H, D]),
                                            w("headmask")[r].unsqueeze(1).unsqueeze(3).to_broadcast([64, GP, H, D]),
                                            ALU.mult).then_inc(S["bd_done"], 1)

            dve.wait_ge(S["cvec"], 1)
            cvec = mixc[0:HI, 15:16]

            def keys_out(s, u, wait):
                dve.wait_ge(S["tr_s"], s + 1)
                if wait:
                    dve.wait_ge(S["av_s"], s - 1)
                nc.vector.tensor_copy(pts[u][0:64 + N, :].rearrange("p (h c i) -> p c h i", h=H, c=NC4),
                                      bank[3][0:64 + N, 0:NC4 * HI].rearrange("p (c h i) -> p c h i", c=NC4, h=H)).then_inc(S["pt_s"], 1)

            def row_max(s, u, wait):
                dve.wait_ge(S["mix"], s + 1)
                if wait:
                    dve.wait_ge(S["exp_s"], s - 1)
                a = bank[2][0:HI, 0:8 * N].rearrange("p (a n) -> p a n", n=N)
                nc.vector.reduce_max(rmax[u][0:HI, :], a, AX).then_inc(S["rmax_s"], 1)
                dve.wait_ge(S["rmax_s"], s + 1)
                nc.vector.tensor_scalar(rmaxc[u][0:HI, :], rmax[u][0:HI, :], cvec, None, ALU.add).then_inc(S["rmaxc_s"], 1)
                dve.wait_ge(S["rmaxc_s"], s + 1)
                nc.vector.scalar_tensor_tensor(tb[u][0:HI, :].rearrange("p (a n) -> p a n", n=N), a, cvec,
                                               rmaxc[u][0:HI, :].unsqueeze(2).to_broadcast([HI, 8, N]),
                                               ALU.add, ALU.subtract).then_inc(S["sub_s"], 1)

            def normalise(s, u, wait):
                dve.wait_ge(S["av_s"], s + 1)
                if wait:
                    dve.wait_ge(S["ot_s"], s - 1)
                o = bank[4][0:NC4 * NI, 0:H * 2 * (D + 1)].rearrange("p (h g d) -> p g h d", h=H, g=2)
                rv = rsum[u][0:NC4 * NI, :].rearrange("p (g h) -> p g h", g=2)
                nc.vector.reciprocal(rv, o[:, :, :, D]).then_inc(S["rsum_s"], 1)
                dve.wait_ge(S["rsum_s"], s + 1)
                nc.vector.tensor_tensor(on[u][0:NC4 * NI, :].rearrange("p (g h d) -> p g h d", g=2, h=H),
                                        o[:, :, :, 0:D], rv.unsqueeze(3).to_broadcast([NC4 * NI, 2, H, D]),
                                        ALU.mult).then_inc(S["on_s"], 1)

            def step(s, u, steady):
                if steady or 2 <= s < PAIRS + 2:
                    keys_out(s - 2, u, steady or s >= 4)
                if steady or 1 <= s < PAIRS + 1:
                    row_max(s - 1, 1 - u, steady or s >= 3)
                if steady or 2 <= s < PAIRS + 2:
                    normalise(s - 2, u, steady or s >= 4)

            for s in range(4):
                step(s, s % 2, False)
            with dve.Fori(0, (PAIRS - 4) // 2) as i:
                for u in range(2):
                    step(2 * i + (4 + u), u, True)
            for s in range(PAIRS, PAIRS + 2):
                step(s, s % 2, False)

            for g in range(GROUPS):
                dve.wait_ge(S["proj_mm"], g + 1)
                c = slice(g * GN, (g + 1) * GN)
                nc.vector.scalar_tensor_tensor(k_sb[:, c], bank[6 + g % 2][:, 0:GN], vec("bproj"), h_sb[:, c],
                                               ALU.add, ALU.add).then_inc(S["h_attn"], 1)
            dve_norm(dve, "2", "cen2_mm", None, xc2, rstd2, q_sb)

            r_ = [0]

            def link_r(ins):
                link(ins, "route", r_)

            def v3(a):
                return a[0:TT, :].rearrange("p (t e) -> p t e", e=E)

            def bc(a):
                return a[0:TT, :].unsqueeze(2).to_broadcast([TT, 2 * T2, E])

            lt = bank[1][0:TT, 0:2 * E * T2].rearrange("p (t e) -> p t e", e=E)
            dve.wait_ge(S["lt_mm"], 1)
            link_r(nc.vector.reduce_max(r1[0][0:TT, :], lt, AX))
            link_r(nc.vector.tensor_tensor(v3(rt[0]), lt, bc(r1[0]), ALU.subtract))
            link_r(nc.vector.memset(rt[3][0:TT, :], 0.0))
            assert r_[0] == ROUTE_LOGITS
            dve.wait_ge(S["route_exp"], 1)
            link_r(nc.vector.reduce_sum(r1[1][0:TT, :], v3(rt[1]), AX))
            link_r(nc.vector.reciprocal(r1[1][0:TT, :], r1[1][0:TT, :]))
            link_r(nc.vector.tensor_tensor(v3(rt[2]), v3(rt[1]), bc(r1[1]), ALU.mult))
            pv, rank, ge = v3(rt[2]), v3(rt[3]), v3(rt[6])
            for s in range(1, E):
                link_r(nc.vector.tensor_tensor(ge[:, :, s:E], pv[:, :, 0:E - s], pv[:, :, s:E], ALU.is_ge))
                link_r(nc.vector.tensor_tensor(rank[:, :, s:E], rank[:, :, s:E], ge[:, :, s:E], ALU.add))
                link_r(nc.vector.scalar_tensor_tensor(rank[:, :, 0:E - s], rank[:, :, 0:E - s], 1.0,
                                                      ge[:, :, s:E], ALU.add, ALU.subtract))
            link_r(nc.vector.reduce_max(r1[2][0:TT, :], pv, AX))
            link_r(nc.vector.tensor_tensor(v3(rt[4]), pv, bc(r1[2]), ALU.subtract))
            assert r_[0] == ROUTE_TOP
            link_r(nc.vector.tensor_scalar(rt[3][0:TT, :], rt[3][0:TT, :], 2.0, None, ALU.is_lt))
            dve.wait_ge(S["route_exp"], 2)
            link_r(nc.vector.tensor_tensor(rt[6][0:TT, :], rt[5][0:TT, :], rt[3][0:TT, :], ALU.mult))
            link_r(nc.vector.reduce_sum(r1[3][0:TT, :], v3(rt[6]), AX))
            link_r(nc.vector.reciprocal(r1[0][0:TT, :], r1[3][0:TT, :]))
            link_r(nc.vector.tensor_tensor(v3(rt[0]), v3(rt[6]), bc(r1[0]), ALU.mult))
            assert r_[0] == ROUTE_ALL

            def second_layer(n):
                for j in range(3):
                    m = 3 * n + j
                    dve.wait_ge(S["l2"], m + 1)
                    if n >= 2:
                        dve.wait_ge(S["l3"], 4 * (n - 1))
                    nc.vector.tensor_scalar(h2[n % 2][:, j * GN:(j + 1) * GN], bank[2 + m % 2][:, 0:GN],
                                            vec(f"b2_{j}"), 0.0, ALU.add, ALU.max).then_inc(S["h2_done"], 1)

            def bias_and_residual(g):
                dve.wait_ge(S["b3_mm"], g + 1)
                if g >= 2:
                    dve.wait_ge(S["l3"], 8 * (g - 1))
                nc.vector.tensor_tensor(hb[g % 2], bank[4][:, 0:GN], k_sb[:, g * GN:(g + 1) * GN],
                                        ALU.add).then_inc(S["hb_done"], 1)

            cc = [0]

            def combine(n):
                g, half = divmod(n, 2)
                for t in range(4):
                    tile = half * T2 + 4 * g + t
                    src = bank[5 + (4 * n + t) % 3][0:TT, :]
                    o = osb[0:TT, tile * C:(tile + 1) * C]
                    dve.wait_ge(S["l3"], 4 * n + t + 1)
                    col = (4 * g + t) * 2 * E + half * E
                    nc.vector.tensor_copy(o, src[:, 384:448]).then_inc(S["lu"], 1)
                    cc[0] += 1
                    for e in range(E):
                        dve.wait_ge(S["lu"], lu[0] + cc[0])
                        ins = nc.vector.scalar_tensor_tensor(o, src[:, e * C:(e + 1) * C], rt[0][0:TT, col + e:col + e + 1],
                                                             o, ALU.mult, ALU.add)
                        if e < E - 1:
                            ins.then_inc(S["lu"], 1)
                            cc[0] += 1
                        else:
                            ins.then_inc(S["comb"], 1)

            for n in range(2 * GROUPS + 1):
                if n < 2 * GROUPS:
                    if n % 2 == 0:
                        bias_and_residual(n // 2)
                    second_layer(n)
                if n >= 1:
                    combine(n - 1)

        def pe_norm(pe, tag, ready, cen, src):
            for g in range(GROUPS + 1):
                if g < GROUPS:
                    pe.wait_ge(S[ready], g + 1)
                    if g >= 2:
                        pe.wait_ge(S["xc" + tag + "_done"], g - 1)
                    nc.tensor.matmul(bank[2 + g % 2][:, 0:GN], w("center"), src[:, g * GN:(g + 1) * GN],
                                     start=True, stop=True).then_inc(S[cen], 1)
                if g >= 1:
                    pe.wait_ge(S["sq" + tag + "_done"], g)
                    if g >= 3:
                        pe.wait_ge(S["std" + tag + "_done"], g - 2)
                    sqb = sq if tag == "" else sq2
                    nc.tensor.matmul(bank[4 + (g - 1) % 2][:, 0:GN], w("avg"), sqb[:, (g - 1) * GN:g * GN],
                                     start=True, stop=True).then_inc(S["var" + tag + "_mm"], 1)

        @block.tensor
        def _(pe):
            pe.wait_ge(S["w_embed"], 16)
            for g in range(GROUPS):
                pe.wait_ge(S["shifted"], 2 * (g + 1))
                if g >= 2:
                    pe.wait_ge(S["gelu_done"], g - 1)
                for v in range(WO):
                    for half in range(2):
                        wt_ = w("tok_a" if half == 0 else "tok_b")[:, v * C:(v + 1) * C]
                        src = pix[g % 2][half][:, :, 2 * v:2 * v + SW * (NW - 1) + 1:SW]
                        last = nc.tensor.matmul(bank[g % 2][64 * half:64 * half + 64, 0:GN], wt_, src,
                                                start=(v == 0), stop=(v == WO - 1))
                last.then_inc(S["embed"], 1)
            pe.wait_ge(S["w_rest"], 16)
            pe_norm(pe, "", "gelu_done", "cen_mm", h_sb)
            pe.wait_ge(S["prep"], 8)
            pe.wait_ge(S["std_done"], 4)
            for k in range(3):
                last = nc.tensor.matmul(bank[4][0:HI, 0:1], w("conv", HI)[:, k * HI:(k + 1) * HI], mixc[0:HI, k:k + 1],
                                        start=(k == 0), stop=(k == 2))
            last.then_inc(S["cvec_mm"], 1)
            for g in range(GROUPS):
                pe.wait_ge(S["xn_done"], g + 1)
                if g >= 1:
                    pe.wait_ge(S["q_done"], g)
                nc.tensor.matmul(bank[6][:, 0:GN], w("wq"), n_sb[:, g * GN:(g + 1) * GN],
                                 start=True, stop=True).then_inc(S["q_mm"], 1)
                if g >= 1:
                    pe.wait_ge(S["k_done"], g)
                nc.tensor.matmul(bank[7][:, 0:GN], w("wk"), n_sb[:, g * GN:(g + 1) * GN],
                                 start=True, stop=True).then_inc(S["k_mm"], 1)

            def gram(t):
                pe.wait_ge(S["qk_tok_done"], 2 * (t + 1))
                if t >= 2:
                    pe.wait_ge(S["gmask_done"], 2 * (t - 1))
                for a in range(2):
                    for k in range(2):
                        blk = qk_tok[t % 2][0:64 + N, (2 * a + k) * 128:(2 * a + k + 1) * 128]
                        last = nc.tensor.matmul(bank[6 + t % 2][:, (2 * a + k) * 128:(2 * a + k + 1) * 128], blk, blk,
                                                start=True, stop=True)
                last.then_inc(S["gram_mm"], 1)

            for t in range(T2):
                if t >= 2:
                    pe.wait_ge(S["v_tok_done"], 2 * (t - 1))
                for a in range(2):
                    p = 2 * t + a
                    for half in range(2):
                        last = nc.tensor.matmul(bank[t % 2][64 * half:64 * half + N, a * 3 * C:(a + 1) * 3 * C],
                                                n_sb[:, p * N:(p + 1) * N], w("wqkv_a" if half == 0 else "wqkv_b"),
                                                start=True, stop=True)
                last.then_inc(S["tok_mm"], 1)
                if t == 0:
                    pe.wait_ge(S["k_done"], GROUPS)
                    pe.wait_ge(S["q_done"], GROUPS)
                if t >= 1:
                    gram(t - 1)
            gram(T2 - 1)

            def to_rows(dst, src):
                for half in range(2):
                    for k in range(2):
                        last = nc.tensor.matmul(dst[64 * k + 32 * half:64 * k + 32 * half + 32, :], src(k),
                                                ident[:, 64 * half:64 * half + 64], start=True, stop=True)
                return last

            for n in range(D):
                last = to_rows(bank[5][:, n * 64:(n + 1) * 64],
                               lambda k: (q_sb, k_sb)[k][:, n:n + (PAIRS - 1) * N + 1:N])
            last.then_inc(S["atop_mm"], 1)
            pe.wait_ge(S["cgram_done"], T2)
            pe.wait_ge(S["cvec"], 1)
            cg = cgram.rearrange("p (a k d) -> p a k d", a=PAIRS, k=2)
            for n in range(D):
                last = to_rows(bank[4][:, n * 64:(n + 1) * 64], lambda k: cg[:, :, k, n])
            last.then_inc(S["g_mm"], 1)
            pe.wait_ge(S["mstep"], 15)
            for c in range(D):
                for half in range(2):
                    for hg in range(2):
                        r0 = 64 * half + 32 * hg
                        last = nc.tensor.matmul(bank[0][r0:r0 + 32, c * 32:(c + 1) * 32], mmat[:, c * 32:(c + 1) * 32],
                                                ident[:, 64 * hg + 32 * half:64 * hg + 32 * half + 32],
                                                start=True, stop=True)
            last.then_inc(S["z_mm"], 1)
            for g in range(GROUPS):
                pe.wait_ge(S["bd_done"], 1 + 2 * (g + 1))
                if g >= 2:
                    pe.wait_ge(S["kp_done"], 2 * (g - 1))
                for a in range(GP):
                    p = g * GP + a
                    last = nc.tensor.matmul(bank[1 + g % 2][:, a * N:(a + 1) * N], bdm[:, p * 128:(p + 1) * 128],
                                            k_sb[:, p * N:(p + 1) * N], start=True, stop=True)
                last.then_inc(S["kp_mm"], 1)

            pe.wait_ge(S["kp_done"], 2 * GROUPS)
            pe.wait_ge(S["kbd_k"], 2 * GROUPS)

            def all_dots(s, u, wait):
                pe.wait_ge(S["qbd_ready"], s + 1)
                for b in range(2):
                    if wait:
                        pe.wait_ge(S["sq3"], 4 * s - (2 - 2 * b))
                    for c in range(2):
                        ch = 2 * b + c
                        last = nc.tensor.matmul(bank[b][0:HI, c * 4 * N:(c + 1) * 4 * N],
                                                qbd[u][:, ch * HI:(ch + 1) * HI], KBD[:, ds(s * 4 * N, 4 * N)],
                                                start=True, stop=True)
                    last.then_inc(S["dots"], 1)

            def mixing(s, u, wait):
                pe.wait_ge(S["sq3"], 4 * s + 4)
                if wait:
                    pe.wait_ge(S["sub_s"], s)
                r = er[u][0:HI, 8 * N:24 * N].rearrange("p (a k n) -> p a k n", a=8, k=2)
                for k, src in enumerate((er[u][0:HI, 0:8 * N], r[:, :, 0, :], r[:, :, 1, :])):
                    last = nc.tensor.matmul(bank[2][0:HI, 0:8 * N], convw[0:HI, k * HI:(k + 1) * HI], src,
                                            start=(k == 0), stop=(k == 2))
                last.then_inc(S["mix"], 1)

            def transposes(s, u, wait):
                pe.wait_ge(S["exp_s"], s + 1)
                if wait:
                    pe.wait_ge(S["pt_s"], s)
                for c in range(NC4):
                    last = nc.tensor.transpose(bank[3][0:64 + N, c * HI:(c + 1) * HI], pr[u][:, c * 128:c * 128 + 64 + N],
                                               ident[0:HI, 0:HI])
                last.then_inc(S["tr_s"], 1)

            def values(s, u, wait):
                pe.wait_ge(S["pt_s"], s + 1)
                if wait:
                    pe.wait_ge(S["on_s"], s)
                V9 = 2 * (D + 1)
                for h in range(H):
                    last = nc.tensor.matmul(bank[4][0:NC4 * NI, h * V9:(h + 1) * V9], pts[u][0:64 + N, h * NC4 * NI:(h + 1) * NC4 * NI],
                                            VBD[0:64 + N, ds(s * (H * V9) + h * V9, V9)], start=True, stop=True)
                last.then_inc(S["av_s"], 1)

            def out_transposes(s, u, wait):
                pe.wait_ge(S["on_s"], s + 1)
                if wait:
                    pe.wait_ge(S["o_done"], s)
                nc.tensor.transpose(bank[5][:, 0:96], on[u][:, :], ident[0:96, 0:96]).then_inc(S["ot_s"], 1)

            def step(s, u, steady):
                if steady or s < PAIRS:
                    all_dots(s, u, steady or s >= 1)
                if steady or 2 <= s < PAIRS + 2:
                    transposes(s - 2, u, steady or s >= 3)
                if steady or 1 <= s < PAIRS + 1:
                    mixing(s - 1, 1 - u, steady or s >= 2)
                if steady or 2 <= s < PAIRS + 2:
                    values(s - 2, u, steady or s >= 3)
                if steady or s >= 3:
                    out_transposes(s - 3, 1 - u, steady or s >= 4)

            for s in range(4):
                step(s, s % 2, False)
            with pe.Fori(0, (PAIRS - 4) // 2) as i:
                for u in range(2):
                    step(2 * i + (4 + u), u, True)
            for s in range(PAIRS, PAIRS + 3):
                step(s, s % 2, False)

            pe.wait_ge(S["o_done"], PAIRS)
            for g in range(GROUPS):
                if g >= 2:
                    pe.wait_ge(S["h_attn"], g - 1)
                nc.tensor.matmul(bank[6 + g % 2][:, 0:GN], w("wproj"), n_sb[:, g * GN:(g + 1) * GN],
                                 start=True, stop=True).then_inc(S["proj_mm"], 1)
            pe_norm(pe, "2", "h_attn", "cen2_mm", k_sb)
            pe.wait_ge(S["h_attn"], GROUPS)
            for g in range(GROUPS):
                pe.wait_ge(S["xn2_done"], g + 1)
                if g >= 1:
                    pe.wait_ge(S["rh_done"], g)
                nc.tensor.matmul(bank[6][0:2 * RH, 0:GN], w("wr1"), q_sb[:, g * GN:(g + 1) * GN],
                                 start=True, stop=True).then_inc(S["rh_mm"], 1)
                pe.wait_ge(S["rh_done"], g + 1)
                if g >= 1:
                    pe.wait_ge(S["lg_done"], g)
                nc.tensor.matmul(bank[7][0:2 * E, 0:GN], w("wr2", 2 * RH), rh[0:2 * RH, g * GN:(g + 1) * GN],
                                 start=True, stop=True).then_inc(S["lg_mm"], 1)
            pe.wait_ge(S["lg_done"], GROUPS)
            for t in range(T2):
                last = nc.tensor.transpose(bank[1][0:TT, t * 2 * E:(t + 1) * 2 * E], lg[0:2 * E, t * TT:(t + 1) * TT],
                                           ident[0:2 * E, 0:2 * E])
            last.then_inc(S["lt_mm"], 1)
            pe.wait_ge(S["route"], ROUTE_ALL)
            for g in range(GROUPS):
                if g >= 2:
                    pe.wait_ge(S["wt_done"], g - 1)
                for t in range(4):
                    tt = 4 * g + t
                    last = nc.tensor.transpose(bank[2 + g % 2][0:2 * E, t * TT:(t + 1) * TT],
                                               rt[0][0:TT, tt * 2 * E:(tt + 1) * 2 * E], ident[0:TT, 0:TT])
                last.then_inc(S["wt_mm"], 1)
            pe.wait_ge(S["wt_done"], GROUPS)

            def third_layer(n):
                g, half = divmod(n, 2)
                pe.wait_ge(S["h2_done"], 3 * (n + 1))
                pe.wait_ge(S["hb_done"], g + 1)
                for t in range(4):
                    i = 4 * n + t
                    bk = bank[5 + i % 3]
                    if i >= 3:
                        pe.wait_ge(S["comb"], i - 2)
                    for j in range(3):
                        nc.tensor.matmul(bk[0:TT, j * 128:(j + 1) * 128], h2[n % 2][:, j * GN + t * TT:j * GN + (t + 1) * TT],
                                         w("w3")[:, j * 128:(j + 1) * 128], start=True, stop=True)
                    nc.tensor.matmul(bk[0:TT, 384:448], hb[g % 2][:, t * TT:(t + 1) * TT],
                                     ident[:, 64 * half:64 * half + 64], start=True, stop=True).then_inc(S["l3"], 1)

            for n in range(2 * GROUPS + 1):
                if n < 2 * GROUPS:
                    g, half = divmod(n, 2)
                    if half == 0:
                        if g >= 1:
                            pe.wait_ge(S["hb_done"], g)
                        nc.tensor.matmul(bank[4][:, 0:GN], w("b3", 2 * E), wt[0:2 * E, g * GN:(g + 1) * GN],
                                         start=True, stop=True).then_inc(S["b3_mm"], 1)
                    for j in range(4):
                        if j < 3:
                            m = 3 * n + j
                            if m >= 2:
                                pe.wait_ge(S["h1_done"], m - 1)
                            col = COL["w1"][0] + (3 * half + j) * 128
                            nc.tensor.matmul(bank[m % 2][:, 0:GN], W[:, col:col + 128], q_sb[:, g * GN:(g + 1) * GN],
                                             start=True, stop=True).then_inc(S["l1"], 1)
                        if j >= 1:
                            m = 3 * n + j - 1
                            pe.wait_ge(S["h1_done"], m + 1)
                            if m >= 2:
                                pe.wait_ge(S["h2_done"], m - 1)
                            nc.tensor.matmul(bank[2 + m % 2][:, 0:GN], w("w2")[:, (j - 1) * 128:j * 128], h1[m % 2],
                                             start=True, stop=True).then_inc(S["l2"], 1)
                if n >= 1:
                    third_layer(n - 1)


def _pack(np, f):
    P = np.zeros((128, NCOLS), np.float32)

    def at(name):
        a, b = COL[name]
        return P[:, a:b]

    tok = f["L0_tok_weight"].reshape(PH, PW, C)
    ta, tb = at("tok_a").reshape(128, WO, C), at("tok_b").reshape(128, WO, C)
    for w in range(PW):
        v, par = divmod(w, 2)
        ta[64 * par:64 * par + 64, v] = tok[:, w]
        tb[64 * (1 - par):64 * (1 - par) + 64, v] = tok[:, w]
    P[:, COL["tok_a"][0]:COL["tok_a"][1]] = ta.reshape(128, -1)
    P[:, COL["tok_b"][0]:COL["tok_b"][1]] = tb.reshape(128, -1)

    V = at("vec")

    def rep(a, times):
        return np.concatenate([a] * times)

    bqkv = f["L0_attn_b_qkv"]
    V[:, VEC["tok_bias"]] = rep(f["L0_tok_bias"], 2)
    for i, n in enumerate(("bq", "bk", "bv")):
        V[:, VEC[n]] = rep(bqkv[i * C:(i + 1) * C], 2)
    V[:, VEC["bproj"]] = rep(f["L0_attn_b_proj"], 2)
    V[0:2 * RH, VEC["br1"]] = rep(f["L0_ffn_router_b1"], 2)
    V[0:2 * E, VEC["br2"]] = rep(f["L0_ffn_router_b2"], 2)
    for j in range(3):
        V[:, VEC[f"b1_{j}"]] = f["L0_ffn_expert_b1"][2 * j:2 * j + 2].reshape(-1)
        V[:, VEC[f"b2_{j}"]] = f["L0_ffn_expert_b2"][2 * j:2 * j + 2].reshape(-1)
    for k in range(3):
        for src, n in (("gamma", "gamma"), ("beta", "beta"), ("mean", "mean"), ("var", "var")):
            V[0:HI, VEC[f"{n}_{k}"]] = np.repeat(f[f"L0_attn_bn_{src}"][k * H:(k + 1) * H], NI)
        V[:, VEC[f"scale_{k}"]] = f[("L0_attn_scale", "L0_attn_riem_scale", "L0_attn_grassman_scale")[k]]
    V[0:HI, VEC["conv_b"]] = np.repeat(f["L0_attn_conv_b"], NI)
    V[:, VEC["eps"]] = EPS

    at("ident")[:] = np.eye(128)
    for half in range(2):
        s = slice(64 * half, 64 * half + 64)
        at("center")[s, s] = np.eye(64) - 1.0 / 64
        at("avg")[s, s] = 1.0 / 64
        for h in range(H):
            at("headmask")[64 * half + D * h:64 * half + D * h + D, h] = 1.0
        at("wq")[s, s] = f["L0_attn_w_qkv"][0:C].T
        at("wk")[s, s] = f["L0_attn_w_qkv"][C:2 * C].T
        at(("wqkv_a", "wqkv_b")[half])[s, :] = f["L0_attn_w_qkv"].T
        at("wproj")[s, s] = f["L0_attn_w_proj"].T
        at("wr1")[s, RH * half:RH * half + RH] = f["L0_ffn_router_w1"]
        at("wr2")[RH * half:RH * half + RH, E * half:E * half + E] = f["L0_ffn_router_w2"]
        at("b3")[E * half:E * half + E, s] = f["L0_ffn_expert_b3"]
        for e in range(E):
            c0 = (3 * half + e // 2) * 128 + 64 * (e % 2)
            at("w1")[s, c0:c0 + 64] = f["L0_ffn_expert_w1"][e]
    for e in range(E):
        r = 64 * (e % 2)
        c0 = (e // 2) * 128 + r
        at("w2")[r:r + 64, c0:c0 + 64] = f["L0_ffn_expert_w2"][e]
        at("w3")[r:r + 64, c0:c0 + 64] = f["L0_ffn_expert_w3"][e]
    at("eye8")[:] = np.eye(D).reshape(-1)
    at("bqk")[:] = bqkv[0:2 * C]
    for k in range(3):
        for i in range(NI):
            rows = at("conv")[i:HI:NI]
            rows[:, k * HI + i:(k + 1) * HI:NI] = f["L0_attn_conv_w"][:, k * H:(k + 1) * H].T
    return P


def kernel(**inputs):
    import numpy as _np
    import concourse.bacc as _bacc
    from concourse.bass_utils import run_bass_kernel_spmd as _run

    f = {k: _np.asarray(v) for k, v in inputs.items()}
    arrays = {"in_x_dram": _np.ascontiguousarray(f["x"]), "in_w_dram": _pack(_np, f)}
    nc = _bacc.Bacc("TRN2", target_bir_lowering=False, num_devices=1)
    f32 = mybir.dt.float32
    x = nc.dram_tensor("in_x_dram", (B, 1, IMG, IMG), f32, kind="ExternalInput").ap()
    wp = nc.dram_tensor("in_w_dram", (128, NCOLS), f32, kind="ExternalInput").ap()
    out = nc.dram_tensor("out_0_dram", (B, N, C), f32, kind="ExternalOutput").ap()
    vit_tower_kernel(nc, x, wp, out)
    r = _run(nc, [arrays], core_ids=[0])
    return r.results[0]["out_0_dram"]
```

```python
from contextlib import ExitStack

import concourse.bass as bass
from concourse import mybir

B, IMG = 64, 224
PH, PW, SH, SW = 64, 25, 64, 12
NH = (IMG - PH) // SH + 1
NW = (IMG - PW) // SW + 1
N = NH * NW
C, H = 64, 8
D = C // H
E, RH = 6, 32
EPS = 1e-5

PAIRS = B // 2
COLS = PAIRS * N
GROUPS = 4
GP = PAIRS // GROUPS
GN = GP * N
NC4 = 4
NI = 13
HI = H * NI
XW = SW * (NW - 1) + PW + 1
SP = GP // 2
SN = SP * N
STEPS = 2 * GROUPS
XG = SP * NH * XW
WO = (PW + 1) // 2
TT = 2 * N
T2 = PAIRS // 2
BP = PAIRS // 2
BT = T2 // 2
E1 = E + 1

ROUTE_LOGITS = 3
ROUTE_TOP = ROUTE_LOGITS + 3 + 3 * (E - 1) + 2
ROUTE_ALL = ROUTE_TOP + 6

def _columns():
    at, where = 0, {}
    for name, n in [("tok", WO * C), ("vec", 32),
                    ("ident", 128), ("eye64", 64), ("center", 128), ("avg", 128), ("headmask", H), ("eye8", D * D),
                    ("wq", 128), ("wk", 128), ("wv_a", C), ("wv_b", C),
                    ("conv", 3 * HI), ("wproj", 128), ("wr1", 2 * RH), ("wr2", 2 * E), ("b3", 128),
                    ("w1", 6 * 128), ("w2", 3 * 128), ("w3", 3 * 128)]:
        where[name] = (at, at + n)
        at += n
    return where, at


COL, NCOLS = _columns()
VEC = {n: i for i, n in enumerate(
    ["tok_bias", "bq", "bk", "bv", "bproj", "br1", "br2", "b1_0", "b1_1", "b1_2", "b2_0", "b2_1", "b2_2",
     "gamma_0", "gamma_1", "gamma_2", "beta_0", "beta_1", "beta_2", "mean_0", "mean_1", "mean_2",
     "var_0", "var_1", "var_2", "conv_b", "scale_0", "scale_1", "scale_2", "eps"])}


def vit_tower_kernel(nc, x, wpack, out):
    f32 = mybir.dt.float32
    ALU = mybir.AluOpType
    ACT = mybir.ActivationFunctionType
    AX = mybir.AxisListType.X
    ds = bass.ds

    with ExitStack() as ctx:
        def sb(name, shape):
            return ctx.enter_context(nc.sbuf_tensor(name, shape, f32))

        bank = [ctx.enter_context(nc.psum_tensor(f"bank{i}", [128, 512], f32)) for i in range(8)]

        W = sb("weights", [128, NCOLS])

        def w(name, rows=128):
            a, b = COL[name]
            return W[0:rows, a:b]

        def vec(name, rows=128, n=1):
            a = COL["vec"][0] + VEC[name]
            return W[0:rows, a:a + n]

        ident = w("ident")
        h_sb = sb("h", [128, COLS])
        q_sb = sb("q", [128, COLS + 4])
        k_sb = sb("k", [128, COLS])
        n_sb = sb("normed", [128, COLS])
        KBD = sb("kbd", [128, PAIRS * 4 * N])
        VBD = sb("vbd", [128, PAIRS * H * 2 * (D + 1)])
        xc = sb("centered", [128, 2 * GN])
        sq = sb("square", [128, 2 * GN])
        rstd = sb("rstd", [128, 2 * GN])
        convw = sb("convw", [HI, 3 * HI])
        mixc = sb("mixc", [HI, 16])
        qbd = [sb(f"qbd{u}", [128, NC4 * HI]) for u in range(2)]
        on = [sb(f"heads{u}", [96, 128]) for u in range(2)]
        pr = [sb(f"probs{u}", [HI, NC4 * 128]) for u in range(2)]
        pixels_sb = [sb(f"pixels{b}", [128, 4 * XG]) for b in range(2)]
        kbd = KBD[:, :].rearrange("p (a g k n) -> p a g k n", a=PAIRS, g=2, k=2)
        vbd = VBD[:, :].rearrange("p (a h g d) -> p a h g d", a=PAIRS, h=H, g=2)
        pix = [[pixels_sb[i // 2][:, (2 * (i % 2) + half) * XG:(2 * (i % 2) + half + 1) * XG]
                .rearrange("p (a c) -> p a c", c=XW) for half in range(2)] for i in range(4)]

        at = [0]

        def part(b, n):
            a = at[0]
            at[0] += n
            assert at[0] <= 4 * XG
            return pixels_sb[b][:, a:a + n]

        qk_tok = [part(0, 4 * 128) for _ in range(2)]
        gmask = [part(0, 4 * C) for _ in range(2)]
        cgram = part(0, D * 32)
        atop = part(0, D * 32)
        aug = part(0, 4 * D * 3 * D)
        etmp = part(0, 4 * D * 2 * D)
        small = part(0, 256)
        linv = part(0, 4 * D * D)
        ik = part(0, 2 * D * D)
        prods = part(0, D // 2 * 4 * D * D)
        mmat = part(0, 4 * D * D)
        bdm = part(0, BP * 128)
        at[0] = 0
        h1 = [part(0, GN) for _ in range(2)]
        h2 = [part(0, 3 * GN) for _ in range(2)]
        hb = [part(0, GN) for _ in range(2)]
        osb = part(0, B // 2 * C)
        wout = [part(0, E1 * C) for _ in range(2)]
        at[0] = 0
        er = [part(1, 3 * 2 * NC4 * N) for _ in range(2)]
        tb = [part(1, 2 * NC4 * N) for _ in range(2)]
        pts = [part(1, NC4 * HI) for _ in range(2)]
        rmax = [part(1, 8) for _ in range(2)]
        rmaxc = [part(1, 8) for _ in range(2)]
        rsum = [part(1, 16) for _ in range(2)]
        rh = part(1, 2 * GN)
        lg = part(1, 2 * GN)
        wt = part(1, 2 * GN)
        w7 = part(1, 2 * T2 * E1)
        NR = 2 * E * BT
        rt = [part(1, NR) for _ in range(7)]
        r1 = [part(1, 2 * BT) for _ in range(4)]

        S = {n: ctx.enter_context(nc.semaphore(n)) for n in """
            w_embed w_rest pix0 pix1 pix2 pix3 pix4 pix5 pix6 pix7 shifted0 shifted1 embed gelu_done prep sqv
            xc_done sq_done cen_mm var_mm std_done rcp_done xn_done
            zero_kbd zero_vbd zero_tok zero_bdm pads
            q_mm k_mm q_done k_done kbd_k tok_tr v_mm qk_tok_done v_tok_done
            gram_mm gmask_done cgram_done atop_cp atop_mm g_mm aug_done elim pivots sqrt_done lu linv_done sel_mm
            mstep z_mm bd_done kp_mm kp_done cvec_mm cvec
            qbd_ready dots sq3 mix rmax_s rmaxc_s sub_s exp_s tr_s pt_s av_s rsum_s on_s ot_s o_done
            proj_mm h_attn xc2_done sq2_done cen2_mm var2_mm std2_done rcp2_done xn2_done
            rh_mm rh_done lg_mm lg_done lt_mm route route_exp wt_mm wt_done
            l1 h1_done l2 h2_done b3_mm hb_done l3 wout_done comb stored
            """.split()}

        block = ctx.enter_context(nc.Block())
        outf = out[:, :, :].rearrange("b n c -> (b n) c")

        def gcols(g):
            return slice(g * GN, (g + 1) * GN)

        def slot(buf, g):
            return buf[:, (g % 2) * GN:(g % 2 + 1) * GN]

        @block.sync
        def _(sp):
            b = COL["vec"][1]
            sp.dma_start(W[:, 0:b], wpack[:, 0:b]).then_inc(S["w_embed"], 16)
            for e in range(STEPS):
                if e >= 4:
                    sp.wait_ge(S["embed"], e - 3)
                for half in range(2):
                    dst = pix[e % 4][half][64 * half:64 * half + 64, :, :]
                    b0 = half * PAIRS + e * SP
                    for i in range(NH):
                        src = x[b0:b0 + SP, 0, i * SH:i * SH + PH, 0:XW].rearrange("b r c -> r b c")
                        sp.dma_start(dst[:, i:SP * NH:NH, :], src).then_inc(S[f"pix{e}"], 16)
                if e == 2:
                    sp.dma_start(W[:, b:NCOLS], wpack[:, b:NCOLS]).then_inc(S["w_rest"], 16)
            for g in range(GROUPS):
                for half in range(2):
                    sp.wait_ge(S["comb"], 4 * (2 * g + half + 1))
                    r0 = half * COLS + g * GN
                    sp.dma_start(outf[r0:r0 + GN, :].rearrange("(t p) c -> p t c", p=TT),
                                 osb[0:TT, (half * T2 + 4 * g) * C:(half * T2 + 4 * g + 4) * C]
                                 .rearrange("p (t c) -> p t c", c=C)).then_inc(S["stored"], 16)
            sp.wait_ge(S["stored"], 16 * 2 * GROUPS)

        @block.gpsimd
        def _(pool):
            pool.memset(VBD[:, :], 0.0).then_inc(S["zero_vbd"], 1)
            pool.memset(KBD[:, :], 0.0).then_inc(S["zero_kbd"], 1)
            for u in range(2):
                pool.memset(pr[u][:, :], 0.0).then_inc(S["pads"], 1)
                pool.memset(on[u][:, :], 0.0).then_inc(S["pads"], 1)
            pool.memset(q_sb[:, COLS:COLS + 4], 0.0).then_inc(S["pads"], 1)
            pool.wait_ge(S["pads"], 5)
            for half in range(2):
                pool.wait_ge(S["zero_vbd"], 1 + half)
                pool.memset(vbd[64 * half:64 * half + N, :, :, half, D:D + 1], 1.0).then_inc(S["zero_vbd"], 1)
            pool.wait_ge(S["zero_vbd"], 3)
            pool.wait_ge(S["embed"], 6)
            for u in range(2):
                pool.memset(qk_tok[u], 0.0).then_inc(S["zero_tok"], 1)
            pool.memset(bdm, 0.0).then_inc(S["zero_bdm"], 1)

            def keys(b):
                for g in (2 * b, 2 * b + 1):
                    pool.wait_ge(S["k_done"], g + 1)
                pool.wait_ge(S["q_done"], 2 * b + 2)
                pool.wait_ge(S["zero_kbd"], 1)
                pool.wait_ge(S["zero_bdm"], 1)
                if b == 1:
                    pool.wait_ge(S["kbd_k"], 4)
                    pool.wait_ge(S["atop_mm"], 1)
                for k, src in enumerate((q_sb, k_sb)):
                    pool.tensor_copy(atop.rearrange("p (n a k) -> p a n k", n=D, k=2)[:, :, :, k],
                                     src[:, b * 2 * GN:(b + 1) * 2 * GN].rearrange("p (a n) -> p a n", n=N)[:, :, 0:D])\
                        .then_inc(S["atop_cp"], 1)
                pool.wait_ge(S["atop_cp"], 2 * b + 2)
                for g in (2 * b, 2 * b + 1):
                    for half in range(2):
                        if g + half > 0:
                            pool.wait_ge(S["kbd_k"], 2 * g + half)
                        pool.tensor_copy(kbd[64 * half:64 * half + 64, g * GP:(g + 1) * GP, half, 0, :],
                                         k_sb[64 * half:64 * half + 64, gcols(g)]
                                         .rearrange("p (a n) -> p a n", n=N)).then_inc(S["kbd_k"], 1)

            def block_queries(s, u, wait):
                if wait:
                    pool.wait_ge(S["dots"], 2 * s - 2)
                qv = q_sb[:, ds(s * N, NC4 * NI)].rearrange("p (c i) -> p c i", i=NI)
                pool.tensor_tensor(qbd[u][:, :].rearrange("p (c h i) -> p c h i", c=NC4, h=H),
                                   qv.unsqueeze(2).to_broadcast([128, NC4, H, NI]),
                                   w("headmask").unsqueeze(1).unsqueeze(3).to_broadcast([128, NC4, H, NI]),
                                   ALU.mult).then_inc(S["qbd_ready"], 1)

            keys(0)
            keys(1)
            pool.wait_ge(S["kbd_k"], 2 * GROUPS)
            pool.wait_ge(S["w_rest"], 16)
            for s in range(2):
                block_queries(s, s, False)
            with pool.Fori(0, (PAIRS - 2) // 2) as i:
                for u in range(2):
                    block_queries(2 * i + (2 + u), u, True)

        def pairs(eng, step, lo, hi):
            assert (hi - lo) % 2 == 0 and lo % 2 == 0
            with eng.Fori(0, (hi - lo) // 2) as i:
                for u in range(2):
                    step(2 * i + (lo + u), u, True)

        @block.scalar
        def _(act):
            def squares_ln(g, tag=""):
                act.wait_ge(S[f"xc{tag}_done"], g + 1)
                if g >= 2:
                    act.wait_ge(S[f"var{tag}_mm"], g - 1)
                nc.scalar.activation(slot(sq, g), slot(xc, g), ACT.Square).then_inc(S[f"sq{tag}_done"], 1)

            def std_ln(g, first_bank, tag=""):
                act.wait_ge(S[f"var{tag}_mm"], g + 1)
                if g >= 2:
                    act.wait_ge(S[f"xn{tag}_done"], g - 1)
                nc.scalar.activation(slot(rstd, g), bank[first_bank + g % 2][:, 0:GN], ACT.Sqrt,
                                     bias=vec("eps")).then_inc(S[f"std{tag}_done"], 1)

            def shift(e):
                act.wait_ge(S[f"pix{e}"], 16 * 2 * NH)
                nc.scalar.activation(pix[e % 4][1][0:64, :, 1:XW:2], pix[e % 4][1][64:128, :, 0:XW - 1:2],
                                     ACT.Copy).then_inc(S["shifted1"], 1)

            def gelu(g):
                act.wait_ge(S["embed"], 2 * g + 2)
                nc.scalar.activation(h_sb[:, gcols(g)], bank[g % 2][:, 0:GN], ACT.Gelu,
                                     bias=vec("tok_bias")).then_inc(S["gelu_done"], 1)

            def q_and_k(g):
                act.wait_ge(S["q_mm"], g + 1)
                nc.scalar.activation(q_sb[:, gcols(g)], bank[6][:, 0:GN], ACT.Identity,
                                     bias=vec("bq")).then_inc(S["q_done"], 1)
                act.wait_ge(S["k_mm"], g + 1)
                nc.scalar.activation(k_sb[:, gcols(g)], bank[7][:, 0:GN], ACT.Identity,
                                     bias=vec("bk")).then_inc(S["k_done"], 1)

            def tokens(t):
                act.wait_ge(S["tok_tr"], t + 1)
                if t >= 2:
                    act.wait_ge(S["gram_mm"], t - 1)
                nc.scalar.activation(qk_tok[t % 2][0:N, :], bank[t % 2][0:N, :], ACT.Copy).then_inc(S["qk_tok_done"], 1)
                act.wait_ge(S["v_mm"], t + 1)
                for half in range(2):
                    r = slice(64 * half, 64 * half + N)
                    nc.scalar.activation(vbd[r, 2 * t:2 * t + 2, :, half, 0:D],
                                         bank[2 + t % 2][r, 0:2 * C].rearrange("p (a h d) -> p a h d", a=2, d=D),
                                         ACT.Copy).then_inc(S["v_tok_done"], 1)

            def pivot_roots(b):
                act.wait_ge(S["pivots"], b + 1)
                nc.scalar.activation(small[:, 32:64], small[:, 0:32], ACT.Sqrt).then_inc(S["sqrt_done"], 1)

            def grass_keys(b):
                for g in (2 * b, 2 * b + 1):
                    act.wait_ge(S["kp_mm"], g + 1)
                    for half in range(2):
                        r = slice(64 * half, 64 * half + 64)
                        nc.scalar.activation(kbd[r, g * GP:(g + 1) * GP, half, 1, :],
                                             bank[4 + 2 * b + g % 2][r, 0:GN].rearrange("p (a n) -> p a n", n=N),
                                             ACT.Copy).then_inc(S["kp_done"], 1)

            act.wait_ge(S["w_embed"], 16)
            nc.scalar.activation(mixc[0:HI, 0:3], vec("var_0", HI, 3), ACT.Sqrt, bias=vec("eps", HI)).then_inc(S["sqv"], 1)
            shift(0)
            shift(1)
            shift(2)
            gelu(0)
            shift(3)
            squares_ln(0)
            std_ln(0, 4)
            gelu(1)
            shift(4)
            squares_ln(1)
            shift(5)
            std_ln(1, 4)
            q_and_k(0)
            gelu(2)
            squares_ln(2)
            q_and_k(1)
            std_ln(2, 4)
            shift(6)
            act.wait_ge(S["zero_vbd"], 3)
            act.wait_ge(S["zero_tok"], 2)
            for t in range(BT):
                tokens(t)
                if t == 2:
                    shift(7)
            q_and_k(2)
            pivot_roots(0)
            gelu(3)
            squares_ln(3)
            std_ln(3, 4)
            q_and_k(3)
            for t in range(BT, T2):
                tokens(t)
                if t == BT + 6:
                    grass_keys(0)

            def squares(s, u, wait):
                if wait:
                    act.wait_ge(S["mix"], s - 1)
                for b in range(2):
                    act.wait_ge(S["dots"], 2 * s + (b + 1))
                    src = bank[b][0:HI, 0:8 * N].rearrange("p (a k n) -> p a k n", a=4, k=2)
                    e = er[u][0:HI, 4 * b * N:4 * (b + 1) * N].rearrange("p (a n) -> p a n", a=4)
                    r = er[u][0:HI, (8 + 8 * b) * N:(16 + 8 * b) * N]
                    nc.scalar.activation(e, src[:, :, 0, :], ACT.Copy).then_inc(S["sq3"], 1)
                    nc.scalar.activation(r, bank[b][0:HI, 0:8 * N], ACT.Square).then_inc(S["sq3"], 1)

            def exponentials(s, u, wait):
                act.wait_ge(S["sub_s"], s + 1)
                if wait:
                    act.wait_ge(S["tr_s"], s - 1)
                dst = pr[u][:, :].rearrange("p (c g n) -> p (c g) n", g=2, n=64)[:, :, 0:N]
                nc.scalar.activation(dst, tb[u][0:HI, :].rearrange("p (a n) -> p a n", n=N),
                                     ACT.Exp).then_inc(S["exp_s"], 1)

            def heads_out(s):
                act.wait_ge(S["ot_s"], s + 1)
                nc.scalar.activation(n_sb[:, ds(s * N, N)], bank[5][:, 0:N], ACT.Identity,
                                     bias=vec("bv")).then_inc(S["o_done"], 1)

            def step(s, u, steady=False):
                if steady or 2 <= s < PAIRS + 2:
                    exponentials(s - 2, u, steady or s >= 4)
                if steady or s < PAIRS:
                    squares(s, u, steady or s >= 2)
                if steady or s >= 4:
                    heads_out(s - 4)

            def router_hidden(b):
                for g in (2 * b, 2 * b + 1):
                    act.wait_ge(S["rh_mm"], g + 1)
                    nc.scalar.activation(slot(rh, g)[0:2 * RH], bank[6 + g % 2][0:2 * RH, 0:GN], ACT.Relu,
                                         bias=vec("br1", 2 * RH)).then_inc(S["rh_done"], 1)

            def router_logits(b):
                for g in (2 * b, 2 * b + 1):
                    act.wait_ge(S["lg_mm"], g + 1)
                    if g >= 2:
                        act.wait_ge(S["lt_mm"], 1)
                    nc.scalar.activation(slot(lg, g)[0:2 * E], bank[6 + g % 2][0:2 * E, 0:GN], ACT.Identity,
                                         bias=vec("br2", 2 * E)).then_inc(S["lg_done"], 1)

            def router_exp(b, k):
                act.wait_ge(S["route"], b * ROUTE_ALL + (ROUTE_LOGITS, ROUTE_TOP)[k])
                nc.scalar.activation(rt[(1, 5)[k]][0:TT, :], rt[(0, 4)[k]][0:TT, :], ACT.Exp).then_inc(S["route_exp"], 1)

            def weights_out(b):
                for g in (2 * b, 2 * b + 1):
                    act.wait_ge(S["wt_mm"], g + 1)
                    if g >= 2:
                        act.wait_ge(S["b3_mm"], g - 1)
                    nc.scalar.activation(slot(wt, g)[0:2 * E1], bank[6 + g % 2][0:2 * E1, 0:GN],
                                         ACT.Copy).then_inc(S["wt_done"], 1)

            def expert_part(n, j):
                if j < 3:
                    m = 3 * n + j
                    act.wait_ge(S["l1"], m + 1)
                    if m >= 2:
                        act.wait_ge(S["l2"], m - 1)
                    nc.scalar.activation(h1[m % 2], bank[m % 2][:, 0:GN], ACT.Relu,
                                         bias=vec(f"b1_{j}")).then_inc(S["h1_done"], 1)
                if j >= 1:
                    m = 3 * n + j - 1
                    act.wait_ge(S["l2"], m + 1)
                    if n >= 2:
                        act.wait_ge(S["l3"], 4 * (n - 1))
                    nc.scalar.activation(h2[n % 2][:, (j - 1) * GN:j * GN], bank[2 + m % 2][:, 0:GN], ACT.Relu,
                                         bias=vec(f"b2_{j - 1}")).then_inc(S["h2_done"], 1)

            for s in range(6):
                step(s, s % 2)
                if s == 4:
                    pivot_roots(1)
            pairs(act, step, 6, 14)
            grass_keys(1)
            pairs(act, step, 14, 20)
            for s in range(20, PAIRS + 4):
                step(s, s % 2)
                if s == 21:
                    squares_ln(0, "2")
                    squares_ln(1, "2")
                elif s == 22:
                    std_ln(0, 6, "2")
                    std_ln(1, 6, "2")
                elif s == 24:
                    router_hidden(0)
                elif s == 25:
                    router_logits(0)
                elif s == 27:
                    router_exp(0, 0)
                elif s == 29:
                    router_exp(0, 1)
                elif s == 31:
                    weights_out(0)
                elif s == PAIRS + 2:
                    for j in range(4):
                        expert_part(0, j)

            for n in range(1, 8):
                for j in range(4):
                    expert_part(n, j)
                    if (n, j) == (1, 1):
                        squares_ln(2, "2")
                        squares_ln(3, "2")
                    elif (n, j) == (1, 3):
                        std_ln(2, 6, "2")
                        std_ln(3, 6, "2")
                    elif (n, j) == (3, 1):
                        router_hidden(1)
                    elif (n, j) == (3, 2):
                        router_logits(1)
                if n == 4:
                    router_exp(1, 0)
                elif n == 5:
                    router_exp(1, 1)
                    weights_out(1)

        @block.vector
        def _(dve):
            count = {}

            def link(ins, name):
                count[name] = count.get(name, 0) + 1
                ins.then_inc(S[name], 1)
                dve.wait_ge(S[name], count[name])

            def shift(e):
                dve.wait_ge(S[f"pix{e}"], 16 * 2 * NH)
                nc.vector.tensor_copy(pix[e % 4][0][64:128, :, 0:XW:2], pix[e % 4][0][0:64, :, 1:XW:2])\
                    .then_inc(S["shifted0"], 1)

            def center(g, first_bank, tag=""):
                dve.wait_ge(S[f"cen{tag}_mm"], g + 1)
                if g >= 2:
                    dve.wait_ge(S[f"xn{tag}_done"], g - 1)
                    dve.wait_ge(S[f"sq{tag}_done"], g - 1)
                nc.vector.tensor_copy(slot(xc, g), bank[first_bank + g % 2][:, 0:GN]).then_inc(S[f"xc{tag}_done"], 1)

            def normalise_ln(g, dst, tag=""):
                dve.wait_ge(S[f"std{tag}_done"], g + 1)
                nc.vector.reciprocal(slot(rstd, g), slot(rstd, g)).then_inc(S[f"rcp{tag}_done"], 1)
                dve.wait_ge(S[f"rcp{tag}_done"], g + 1)
                nc.vector.tensor_tensor(dst[:, gcols(g)], slot(xc, g), slot(rstd, g), ALU.mult).then_inc(S[f"xn{tag}_done"], 1)

            def gram_blocks(t):
                dve.wait_ge(S["gram_mm"], t + 1)
                gm = gmask[t % 2][:, :].rearrange("p (a h d) -> p a h d", a=4, h=H)
                if t >= 2:
                    dve.wait_ge(S["cgram_done"], t - 1)
                for half in range(2):
                    r = slice(64 * half, 64 * half + 64)
                    src = bank[6 + t % 2][r, :].rearrange("p (a c) -> p a c", a=4)[:, :, 64 * half:64 * half + 64]
                    nc.vector.tensor_tensor(gm[r], src.rearrange("p a (h d) -> p a h d", d=D),
                                            w("headmask")[r].unsqueeze(1).unsqueeze(3).to_broadcast([64, 4, H, D]),
                                            ALU.mult).then_inc(S["gmask_done"], 1)
                dve.wait_ge(S["gmask_done"], 2 * (t + 1))
                if t == BT:
                    dve.wait_ge(S["g_mm"], 1)
                c = 4 * (t % BT)
                nc.vector.tensor_reduce(cgram.rearrange("p (d a) -> p a d", d=D)[:, c:c + 4, :],
                                        gm.rearrange("p a h d -> p a d h"), AX, ALU.add).then_inc(S["cgram_done"], 1)

            A = aug.rearrange("p (h d c) -> p h d c", h=4, d=D)
            rc = small[:, 64:68]
            lrow = small[:, 68:96].rearrange("p (h i) -> p h i", h=4)
            u_ = small[:, 96:128].rearrange("p (h d) -> p h d", h=4)
            npv = small[:, 128:132]
            nrc = small[:, 132:136]
            lc = small[:, 136:164].rearrange("p (h i) -> p h i", h=4)
            sg = small[:, 164:196]

            def qr_load(b):
                if b == 0:
                    dve.wait_ge(S["w_rest"], 16)
                nc.vector.tensor_copy(A[:, :, :, 2 * D:3 * D],
                                      w("eye8").rearrange("p (d c) -> p d c", d=D).unsqueeze(1)
                                      .to_broadcast([128, 4, D, D])).then_inc(S["aug_done"], 1)
                dve.wait_ge(S["atop_mm"], b + 1)
                nc.vector.tensor_copy(A[:, :, :, D:2 * D],
                                      bank[5 + 2 * b][:, 0:256].rearrange("p (n h d) -> p h d n", n=D, h=4)).then_inc(S["aug_done"], 1)
                dve.wait_ge(S["g_mm"], b + 1)
                nc.vector.tensor_copy(A[:, :, :, 0:D],
                                      bank[4 + 2 * b][:, 0:256].rearrange("p (n h d) -> p h d n", n=D, h=4)).then_inc(S["aug_done"], 1)
                dve.wait_ge(S["aug_done"], 3 * (b + 1))

            def eliminate(j):
                m = D - 1 - j
                link(nc.vector.reciprocal(rc, A[:, :, j, j]), "elim")
                link(nc.vector.tensor_tensor(lrow[:, :, 0:m], A[:, :, j, j + 1:D],
                                             rc.unsqueeze(2).to_broadcast([128, 4, m]), ALU.mult), "elim")
                tmp = etmp[:, 0:4 * m * 16].rearrange("p (h i c) -> p h i c", h=4, i=m)
                link(nc.vector.tensor_tensor(tmp, lrow[:, :, 0:m].unsqueeze(3).to_broadcast([128, 4, m, 16]),
                                             A[:, :, j:j + 1, j + 1:j + 17].to_broadcast([128, 4, m, 16]), ALU.mult), "elim")
                rows = A[:, :, j + 1:D, j + 1:j + 17]
                link(nc.vector.tensor_tensor(rows, rows, tmp, ALU.subtract), "elim")

            def qr_scale(b):
                diag = aug.rearrange("p (h r) -> p h r", h=4)[:, :, 0:D * 3 * D:3 * D + 1]
                piv = small[:, 0:32].rearrange("p (h d) -> p h d", h=4)
                nc.vector.tensor_copy(piv, diag).then_inc(S["pivots"], 1)
                dve.wait_ge(S["sqrt_done"], b + 1)
                link(nc.vector.reciprocal(small[:, 32:64], small[:, 32:64]), "elim")
                rs = small[:, 32:64].rearrange("p (h d) -> p h d", h=4)
                both = A[:, :, :, D:3 * D]
                link(nc.vector.tensor_tensor(both, both, rs.unsqueeze(3).to_broadcast([128, 4, D, 2 * D]), ALU.mult), "elim")

            def signs(j):
                tjj = A[:, :, j, D + j]
                link(nc.vector.tensor_scalar(u_[:, :, j], tjj, 0.0, -2.0, ALU.is_ge, ALU.mult), "lu")
                if j == D - 1:
                    return
                m = D - 1 - j
                link(nc.vector.scalar_tensor_tensor(npv, u_[:, :, j], 1.0, tjj, ALU.add, ALU.subtract), "lu")
                link(nc.vector.reciprocal(nrc, npv), "lu")
                link(nc.vector.tensor_tensor(lc[:, :, 0:m], A[:, :, j, D + j + 1:2 * D],
                                             nrc.unsqueeze(2).to_broadcast([128, 4, m]), ALU.mult), "lu")
                tmp = etmp[:, 0:4 * m * m].rearrange("p (h k i) -> p h k i", h=4, k=m)
                link(nc.vector.tensor_tensor(tmp, A[:, :, j + 1:D, D + j].unsqueeze(3).to_broadcast([128, 4, m, m]),
                                             lc[:, :, 0:m].unsqueeze(2).to_broadcast([128, 4, m, m]), ALU.mult), "lu")
                tr = A[:, :, j + 1:D, D + j + 1:2 * D]
                link(nc.vector.tensor_tensor(tr, tr, tmp, ALU.add), "lu")

            def signed_inverse(b):
                link(nc.vector.tensor_scalar(sg, small[:, 96:128], 1.0, None, ALU.add), "lu")
                if b == 1:
                    dve.wait_ge(S["sel_mm"], 1)
                nc.vector.tensor_tensor(linv.rearrange("p (h j c) -> p h j c", h=4, j=D), A[:, :, :, 2 * D:3 * D],
                                        sg.rearrange("p (h d) -> p h d", h=4).unsqueeze(3).to_broadcast([128, 4, D, D]),
                                        ALU.mult).then_inc(S["linv_done"], 1)

            def q_times_k(b):
                dve.wait_ge(S["sel_mm"], b + 1)
                if b == 1:
                    dve.wait_ge(S["z_mm"], 1)
                J = D // 2
                link(nc.vector.tensor_copy(ik, bank[4 + 2 * b][:, 128:256]), "mstep")
                iqv = bank[4 + 2 * b][:, 0:128].rearrange("p (h j c) -> p h j c", h=4, j=J)
                ikv = ik.rearrange("p (h j c) -> p h j c", h=4, j=J)
                for j in range(J):
                    nc.vector.tensor_tensor(prods[:, j * 256:(j + 1) * 256].rearrange("p (h c a) -> p h c a", h=4, c=D),
                                            iqv[:, :, j, :].unsqueeze(3).to_broadcast([128, 4, D, D]),
                                            ikv[:, :, j, :].unsqueeze(2).to_broadcast([128, 4, D, D]),
                                            ALU.mult).then_inc(S["mstep"], 1)
                count["mstep"] += J
                dve.wait_ge(S["mstep"], count["mstep"])
                link(nc.vector.tensor_tensor(prods[:, 0:512], prods[:, 0:512], prods[:, 512:1024], ALU.add), "mstep")
                link(nc.vector.tensor_tensor(mmat.rearrange("p (c h a) -> p h c a", c=D, h=4),
                                             prods[:, 0:256].rearrange("p (h c a) -> p h c a", h=4, c=D),
                                             prods[:, 256:512].rearrange("p (h c a) -> p h c a", h=4, c=D),
                                             ALU.add), "mstep")

            def block_m(b):
                dve.wait_ge(S["z_mm"], b + 1)
                dve.wait_ge(S["zero_bdm"], 1)
                if b == 1:
                    dve.wait_ge(S["kp_mm"], 2)
                z = bank[5 + 2 * b][:, 0:D * BP].rearrange("p (c a) -> p a c", c=D)
                for g in range(2):
                    for half in range(2):
                        r = slice(64 * half, 64 * half + 64)
                        dst = bdm[r, g * GP * 128:(g + 1) * GP * 128].rearrange("p (a c) -> p a c", c=128)
                        nc.vector.tensor_tensor(dst[:, :, 64 * half:64 * half + 64].rearrange("p a (h c) -> p a h c", c=D),
                                                z[r, g * GP:(g + 1) * GP, :].unsqueeze(2).to_broadcast([64, GP, H, D]),
                                                w("headmask")[r].unsqueeze(1).unsqueeze(3).to_broadcast([64, GP, H, D]),
                                                ALU.mult).then_inc(S["bd_done"], 1)

            shift(0)
            shift(1)
            shift(2)
            center(0, 2)
            shift(3)
            shift(4)
            normalise_ln(0, n_sb)
            center(1, 2)
            shift(5)
            dve.wait_ge(S["sqv"], 1)
            dve.wait_ge(S["w_rest"], 16)
            link(nc.vector.reciprocal(mixc[0:HI, 3:6], mixc[0:HI, 0:3]), "prep")
            link(nc.vector.tensor_tensor(mixc[0:HI, 6:9], mixc[0:HI, 3:6], vec("gamma_0", HI, 3), ALU.mult), "prep")
            link(nc.vector.tensor_tensor(mixc[0:HI, 9:12], mixc[0:HI, 6:9], vec("scale_0", HI, 3), ALU.mult), "prep")
            link(nc.vector.tensor_tensor(mixc[0:HI, 12:15], mixc[0:HI, 6:9], vec("mean_0", HI, 3), ALU.mult), "prep")
            link(nc.vector.tensor_tensor(mixc[0:HI, 0:3], vec("beta_0", HI, 3), mixc[0:HI, 12:15], ALU.subtract), "prep")
            normalise_ln(1, n_sb)
            center(2, 2)
            for k in range(3):
                cw = w("conv", HI)[:, k * HI:(k + 1) * HI]
                link(nc.vector.tensor_scalar(convw[0:HI, k * HI:(k + 1) * HI], cw, mixc[0:HI, 9 + k:10 + k], None, ALU.mult),
                     "prep")
            normalise_ln(2, n_sb)
            shift(6)
            for t in range(BT):
                gram_blocks(t)
                if t == 1:
                    shift(7)
            qr_load(0)
            for j in range(D - 1):
                eliminate(j)
            qr_scale(0)
            signs(0)
            center(3, 2)
            signs(1)
            normalise_ln(3, n_sb)
            for j in range(2, D):
                signs(j)
            dve.wait_ge(S["cvec_mm"], 1)
            nc.vector.tensor_tensor(mixc[0:HI, 15:16], bank[4][0:HI, 508:509], vec("conv_b", HI), ALU.add).then_inc(S["cvec"], 1)
            signed_inverse(0)
            for t in range(BT, T2):
                gram_blocks(t)
                if t == BT + 1:
                    q_times_k(0)
                elif t == BT + 3:
                    block_m(0)

            dve.wait_ge(S["cvec"], 1)
            cvec = mixc[0:HI, 15:16]

            def keys_out(s, u, wait):
                dve.wait_ge(S["tr_s"], s + 1)
                if wait:
                    dve.wait_ge(S["av_s"], s - 1)
                nc.vector.tensor_copy(pts[u][0:64 + N, :].rearrange("p (h c i) -> p c h i", h=H, c=NC4),
                                      bank[3][0:64 + N, 0:NC4 * HI].rearrange("p (c h i) -> p c h i", c=NC4, h=H))\
                    .then_inc(S["pt_s"], 1)

            def row_max(s, u, wait):
                dve.wait_ge(S["mix"], s + 1)
                if wait:
                    dve.wait_ge(S["exp_s"], s - 1)
                a = bank[2][0:HI, 0:8 * N].rearrange("p (a n) -> p a n", n=N)
                nc.vector.reduce_max(rmax[u][0:HI, :], a, AX).then_inc(S["rmax_s"], 1)
                dve.wait_ge(S["rmax_s"], s + 1)
                nc.vector.tensor_scalar(rmaxc[u][0:HI, :], rmax[u][0:HI, :], cvec, None, ALU.add).then_inc(S["rmaxc_s"], 1)
                dve.wait_ge(S["rmaxc_s"], s + 1)
                nc.vector.scalar_tensor_tensor(tb[u][0:HI, :].rearrange("p (a n) -> p a n", n=N), a, cvec,
                                               rmaxc[u][0:HI, :].unsqueeze(2).to_broadcast([HI, 8, N]),
                                               ALU.add, ALU.subtract).then_inc(S["sub_s"], 1)

            def normalise(s, u, wait):
                dve.wait_ge(S["av_s"], s + 1)
                if wait:
                    dve.wait_ge(S["ot_s"], s - 1)
                o = bank[4][0:NC4 * NI, 0:H * 2 * (D + 1)].rearrange("p (h g d) -> p g h d", h=H, g=2)
                rv = rsum[u][0:NC4 * NI, :].rearrange("p (g h) -> p g h", g=2)
                nc.vector.reciprocal(rv, o[:, :, :, D]).then_inc(S["rsum_s"], 1)
                dve.wait_ge(S["rsum_s"], s + 1)
                nc.vector.tensor_tensor(on[u][0:NC4 * NI, :].rearrange("p (g h d) -> p g h d", g=2, h=H),
                                        o[:, :, :, 0:D], rv.unsqueeze(3).to_broadcast([NC4 * NI, 2, H, D]),
                                        ALU.mult).then_inc(S["on_s"], 1)

            def step(s, u, steady=False):
                if steady or 3 <= s < PAIRS + 3:
                    keys_out(s - 3, 1 - u, steady or s >= 5)
                if steady or 1 <= s < PAIRS + 1:
                    row_max(s - 1, 1 - u, steady or s >= 3)
                if steady or 3 <= s < PAIRS + 3:
                    normalise(s - 3, 1 - u, steady or s >= 5)

            def residual(b):
                for g in (2 * b, 2 * b + 1):
                    dve.wait_ge(S["proj_mm"], g + 1)
                    nc.vector.scalar_tensor_tensor(k_sb[:, gcols(g)], bank[6 + g % 2][:, 0:GN], vec("bproj"),
                                                   h_sb[:, gcols(g)], ALU.add, ALU.add).then_inc(S["h_attn"], 1)

            def v3(a):
                return a[0:TT, :].rearrange("p (t e) -> p t e", e=E)

            def bc(a):
                return a[0:TT, :].unsqueeze(2).to_broadcast([TT, 2 * BT, E])

            def link_r(ins):
                link(ins, "route")

            pv, rank, ge = v3(rt[2]), v3(rt[3]), v3(rt[6])

            def route_logits(b):
                lt = bank[6][0:TT, 0:NR].rearrange("p (t e) -> p t e", e=E)
                dve.wait_ge(S["lt_mm"], b + 1)
                link_r(nc.vector.reduce_max(r1[0][0:TT, :], lt, AX))
                link_r(nc.vector.tensor_tensor(v3(rt[0]), lt, bc(r1[0]), ALU.subtract))
                link_r(nc.vector.memset(rt[3][0:TT, :], 0.0))
                assert count["route"] == b * ROUTE_ALL + ROUTE_LOGITS

            def route_rank(b, part):
                if part == 1:
                    return route_top(b)
                dve.wait_ge(S["route_exp"], 2 * b + 1)
                link_r(nc.vector.reduce_sum(r1[1][0:TT, :], v3(rt[1]), AX))
                link_r(nc.vector.reciprocal(r1[1][0:TT, :], r1[1][0:TT, :]))
                link_r(nc.vector.tensor_tensor(v3(rt[2]), v3(rt[1]), bc(r1[1]), ALU.mult))
                rank_shifts(1, 3)

            def rank_shifts(lo, hi):
                for s in range(lo, hi):
                    link_r(nc.vector.tensor_tensor(ge[:, :, s:E], pv[:, :, 0:E - s], pv[:, :, s:E], ALU.is_ge))
                    link_r(nc.vector.tensor_tensor(rank[:, :, s:E], rank[:, :, s:E], ge[:, :, s:E], ALU.add))
                    link_r(nc.vector.scalar_tensor_tensor(rank[:, :, 0:E - s], rank[:, :, 0:E - s], 1.0,
                                                          ge[:, :, s:E], ALU.add, ALU.subtract))

            def route_top(b):
                rank_shifts(3, E)
                link_r(nc.vector.reduce_max(r1[2][0:TT, :], pv, AX))
                link_r(nc.vector.tensor_tensor(v3(rt[4]), pv, bc(r1[2]), ALU.subtract))
                assert count["route"] == b * ROUTE_ALL + ROUTE_TOP

            def route_weights(b):
                link_r(nc.vector.tensor_scalar(rt[3][0:TT, :], rt[3][0:TT, :], 2.0, None, ALU.is_lt))
                dve.wait_ge(S["route_exp"], 2 * b + 2)
                link_r(nc.vector.tensor_tensor(rt[6][0:TT, :], rt[5][0:TT, :], rt[3][0:TT, :], ALU.mult))
                link_r(nc.vector.reduce_sum(r1[3][0:TT, :], v3(rt[6]), AX))
                link_r(nc.vector.reciprocal(r1[0][0:TT, :], r1[3][0:TT, :]))
                dst = w7[0:TT, b * 2 * BT * E1:(b + 1) * 2 * BT * E1].rearrange("p (t e) -> p t e", e=E1)
                link_r(nc.vector.memset(dst[:, :, E:E1], 1.0))
                link_r(nc.vector.tensor_tensor(dst[:, :, 0:E], v3(rt[6]), bc(r1[0]), ALU.mult))
                assert count["route"] == (b + 1) * ROUTE_ALL

            def bias_and_residual(g):
                dve.wait_ge(S["b3_mm"], g + 1)
                if g >= 2:
                    dve.wait_ge(S["l3"], 8 * (g - 1))
                nc.vector.tensor_tensor(hb[g % 2], bank[6 + g % 2][:, 0:GN], k_sb[:, gcols(g)], ALU.add).then_inc(S["hb_done"], 1)

            def combine(i):
                n, t = divmod(i, 4)
                g, half = divmod(n, 2)
                tile = half * T2 + 4 * g + t
                dve.wait_ge(S["l3"], i + 1)
                if i >= 2:
                    dve.wait_ge(S["comb"], i - 1)
                col = ((4 * g + t) * 2 + half) * E1
                wo = wout[i % 2][0:TT, :].rearrange("p (e c) -> p e c", e=E1)
                nc.vector.tensor_tensor(wo, bank[4 + i % 2][0:TT, 0:E1 * C].rearrange("p (e c) -> p e c", e=E1),
                                        w7[0:TT, col:col + E1].unsqueeze(2).to_broadcast([TT, E1, C]),
                                        ALU.mult).then_inc(S["wout_done"], 1)
                dve.wait_ge(S["wout_done"], i + 1)
                nc.vector.tensor_reduce(osb[0:TT, tile * C:(tile + 1) * C], wo.rearrange("p e c -> p c e"),
                                        AX, ALU.add).then_inc(S["comb"], 1)

            for s in range(14):
                step(s, s % 2, s >= 6)
                if s == 0:
                    qr_load(1)
                if s < 4:
                    eliminate(2 * s)
                    if s < 3:
                        eliminate(2 * s + 1)
                elif s == 4:
                    qr_scale(1)
                elif s < 9:
                    signs(2 * (s - 5))
                    signs(2 * (s - 5) + 1)
                    if s == 8:
                        signed_inverse(1)
                elif s == 10:
                    q_times_k(1)
                elif s == 12:
                    block_m(1)
            pairs(dve, step, 14, 20)
            for s in range(20, PAIRS + 3):
                step(s, s % 2)
                if s == 20:
                    residual(0)
                elif s == 21:
                    center(0, 6, "2")
                    center(1, 6, "2")
                elif s == 22:
                    normalise_ln(0, q_sb, "2")
                elif s == 23:
                    normalise_ln(1, q_sb, "2")
                elif s == 26:
                    route_logits(0)
                elif s == 27:
                    route_rank(0, 0)
                elif s == 28:
                    route_rank(0, 1)
                elif s == 30:
                    route_weights(0)
                elif s == 32:
                    bias_and_residual(0)
                    bias_and_residual(1)
            residual(1)
            for i in range(2):
                combine(i)
            center(2, 6, "2")
            center(3, 6, "2")
            for i in range(2, 4):
                combine(i)
            normalise_ln(2, q_sb, "2")
            normalise_ln(3, q_sb, "2")
            for i in range(4, 12):
                combine(i)
            route_logits(1)
            for i in range(12, 14):
                combine(i)
            route_rank(1, 0)
            for i in range(14, 16):
                combine(i)
            route_rank(1, 1)
            route_weights(1)
            bias_and_residual(2)
            bias_and_residual(3)
            for i in range(16, 32):
                combine(i)

        @block.tensor
        def _(pe):
            def embed(e):
                pe.wait_ge(S["shifted0"], e + 1)
                pe.wait_ge(S["shifted1"], e + 1)
                g = e // 2
                if g >= 2:
                    pe.wait_ge(S["gelu_done"], g - 1)
                if g == 3:
                    pe.wait_ge(S["qk_tok_done"], BT)
                for v in range(WO):
                    for half in range(2):
                        src = pix[e % 4][half][:, :, 2 * v + half:2 * v + half + SW * (NW - 1) + 1:SW]
                        last = nc.tensor.matmul(bank[g % 2][64 * half:64 * half + 64, (e % 2) * SN:(e % 2 + 1) * SN],
                                                w("tok")[:, v * C:(v + 1) * C], src, start=(v == 0), stop=(v == WO - 1))
                last.then_inc(S["embed"], 1)

            def center(g, first_bank, ready, src, tag=""):
                pe.wait_ge(S[ready], g + 1)
                if g >= 2:
                    pe.wait_ge(S[f"xc{tag}_done"], g - 1)
                nc.tensor.matmul(bank[first_bank + g % 2][:, 0:GN], w("center"), src[:, gcols(g)],
                                 start=True, stop=True).then_inc(S[f"cen{tag}_mm"], 1)

            def variance(g, first_bank, tag=""):
                pe.wait_ge(S[f"sq{tag}_done"], g + 1)
                if g >= 2:
                    pe.wait_ge(S[f"std{tag}_done"], g - 1)
                nc.tensor.matmul(bank[first_bank + g % 2][:, 0:GN], w("avg"), slot(sq, g),
                                 start=True, stop=True).then_inc(S[f"var{tag}_mm"], 1)

            def q_and_k(g):
                pe.wait_ge(S["xn_done"], g + 1)
                if g >= 1:
                    pe.wait_ge(S["q_done"], g)
                if g == 2:
                    pe.wait_ge(S["gmask_done"], 2 * BT)
                nc.tensor.matmul(bank[6][:, 0:GN], w("wq"), n_sb[:, gcols(g)], start=True, stop=True).then_inc(S["q_mm"], 1)
                if g >= 1:
                    pe.wait_ge(S["k_done"], g)
                nc.tensor.matmul(bank[7][:, 0:GN], w("wk"), n_sb[:, gcols(g)], start=True, stop=True).then_inc(S["k_mm"], 1)

            def tokens(t):
                if t >= 2:
                    pe.wait_ge(S["qk_tok_done"], t - 1)
                for a in range(2):
                    c = slice((2 * t + a) * N, (2 * t + a + 1) * N)
                    for k, src in enumerate((q_sb, k_sb)):
                        last = nc.tensor.transpose(bank[t % 2][0:N, (2 * a + k) * 128:(2 * a + k + 1) * 128], src[:, c], ident)
                last.then_inc(S["tok_tr"], 1)
                if t >= 2:
                    pe.wait_ge(S["v_tok_done"], 2 * (t - 1))
                for a in range(2):
                    c = slice((2 * t + a) * N, (2 * t + a + 1) * N)
                    for half in range(2):
                        last = nc.tensor.matmul(bank[2 + t % 2][64 * half:64 * half + N, a * C:(a + 1) * C],
                                                n_sb[:, c], w("wv_a" if half == 0 else "wv_b"), start=True, stop=True)
                last.then_inc(S["v_mm"], 1)

            def gram(t):
                pe.wait_ge(S["qk_tok_done"], t + 1)
                if t >= 2:
                    pe.wait_ge(S["gmask_done"], 2 * (t - 1))
                for a in range(4):
                    blk = qk_tok[t % 2][:, a * 128:(a + 1) * 128]
                    last = nc.tensor.matmul(bank[6 + t % 2][:, a * 128:(a + 1) * 128], blk, blk, start=True, stop=True)
                last.then_inc(S["gram_mm"], 1)

            def tokens_and_grams(b, between={}):
                pe.wait_ge(S["q_done"], 2 * b + 2)
                pe.wait_ge(S["k_done"], 2 * b + 2)
                pe.wait_ge(S["gelu_done"], 3 + b)
                pe.wait_ge(S["xc_done"], 3 + b)
                for t in range(b * BT, (b + 1) * BT):
                    tokens(t)
                    if t > b * BT:
                        gram(t - 1)
                    if t in between:
                        between[t](0)
                gram((b + 1) * BT - 1)

            def to_rows(dst, src):
                for n in range(D):
                    for r0 in range(0, 128, 32):
                        last = nc.tensor.matmul(dst[r0:r0 + 32, n * 32:(n + 1) * 32], src[:, n * 32:(n + 1) * 32],
                                                ident[:, r0:r0 + 32], start=True, stop=True)
                return last

            def qr_operands(b):
                pe.wait_ge(S["atop_cp"], 2 * b + 2)
                pe.wait_ge(S["std_done"], 3 + b)
                if b == 1:
                    pe.wait_ge(S["gmask_done"], 2 * T2)
                to_rows(bank[5 + 2 * b], atop).then_inc(S["atop_mm"], 1)
                pe.wait_ge(S["cgram_done"], (b + 1) * BT)
                to_rows(bank[4 + 2 * b], cgram).then_inc(S["g_mm"], 1)

            def select_q_and_k(b):
                pe.wait_ge(S["linv_done"], b + 1)
                pe.wait_ge(S["cvec"], 1)
                li = linv.rearrange("p (h r) -> p h r", h=4)
                for k in range(2):
                    for jh in range(2):
                        last = nc.tensor.matmul(bank[4 + 2 * b][64 * jh:64 * jh + 64, k * 128:(k + 1) * 128], ident[:, k:128:2],
                                                li[:, :, jh * 32:(jh + 1) * 32], start=True, stop=True)
                last.then_inc(S["sel_mm"], 1)

            def m_to_columns(b):
                pe.wait_ge(S["mstep"], (D // 2 + 3) * (b + 1))
                for c in range(D):
                    for i in range(4):
                        last = nc.tensor.matmul(bank[5 + 2 * b][32 * i:32 * i + 32, c * BP:(c + 1) * BP], mmat[:, c * 32:(c + 1) * 32],
                                                w("eye64")[:, BP * i:BP * (i + 1)], start=True, stop=True)
                last.then_inc(S["z_mm"], 1)

            def grass_keys(b):
                for g in (2 * b, 2 * b + 1):
                    pe.wait_ge(S["bd_done"], 4 * b + 2 * (g % 2) + 2)
                    if g % 2 == 1:
                        pe.wait_ge(S["bd_done"], 4 * b + 4)
                    for a in range(GP):
                        p = g * GP + a
                        i = (g % 2) * GP + a
                        last = nc.tensor.matmul(bank[4 + 2 * b + g % 2][:, a * N:(a + 1) * N], bdm[:, i * 128:(i + 1) * 128],
                                                k_sb[:, p * N:(p + 1) * N], start=True, stop=True)
                    last.then_inc(S["kp_mm"], 1)

            pe.wait_ge(S["w_embed"], 16)
            embed(0)
            embed(1)
            embed(2)
            pe.wait_ge(S["w_rest"], 16)
            center(0, 2, "gelu_done", h_sb)
            embed(3)
            variance(0, 4)
            center(1, 2, "gelu_done", h_sb)
            embed(4)
            variance(1, 4)
            q_and_k(0)
            embed(5)
            center(2, 2, "gelu_done", h_sb)
            q_and_k(1)
            variance(2, 4)
            tokens_and_grams(0)
            qr_operands(0)
            embed(6)
            q_and_k(2)
            embed(7)
            pe.wait_ge(S["v_tok_done"], 2 * BT)
            center(3, 2, "gelu_done", h_sb)
            pe.wait_ge(S["aug_done"], 3)
            variance(3, 4)
            q_and_k(3)
            pe.wait_ge(S["prep"], 8)
            pe.wait_ge(S["std_done"], 4)
            for k in range(3):
                last = nc.tensor.matmul(bank[4][0:HI, 508:509], w("conv", HI)[:, k * HI:(k + 1) * HI], mixc[0:HI, k:k + 1],
                                        start=(k == 0), stop=(k == 2))
            last.then_inc(S["cvec_mm"], 1)
            tokens_and_grams(1, {BT + 2: select_q_and_k, BT + 4: m_to_columns, BT + 6: grass_keys})

            pe.wait_ge(S["kp_done"], 4)
            pe.wait_ge(S["kbd_k"], 2 * GROUPS)
            pe.wait_ge(S["v_tok_done"], 2 * T2)
            pe.wait_ge(S["qk_tok_done"], T2)

            def all_dots(s, u, wait):
                pe.wait_ge(S["qbd_ready"], s + 1)
                for b in range(2):
                    if wait:
                        pe.wait_ge(S["sq3"], 4 * s - (2 - 2 * b))
                    for c in range(2):
                        ch = 2 * b + c
                        last = nc.tensor.matmul(bank[b][0:HI, c * 4 * N:(c + 1) * 4 * N],
                                                qbd[u][:, ch * HI:(ch + 1) * HI], KBD[:, ds(s * 4 * N, 4 * N)],
                                                start=True, stop=True)
                    last.then_inc(S["dots"], 1)

            def mixing(s, u, wait):
                pe.wait_ge(S["sq3"], 4 * s + 4)
                if wait:
                    pe.wait_ge(S["sub_s"], s)
                r = er[u][0:HI, 8 * N:24 * N].rearrange("p (a k n) -> p a k n", a=8, k=2)
                for k, src in enumerate((er[u][0:HI, 0:8 * N], r[:, :, 0, :], r[:, :, 1, :])):
                    last = nc.tensor.matmul(bank[2][0:HI, 0:8 * N], convw[0:HI, k * HI:(k + 1) * HI], src,
                                            start=(k == 0), stop=(k == 2))
                last.then_inc(S["mix"], 1)

            def transposes(s, u, wait):
                pe.wait_ge(S["exp_s"], s + 1)
                if wait:
                    pe.wait_ge(S["pt_s"], s)
                for c in range(NC4):
                    last = nc.tensor.transpose(bank[3][0:64 + N, c * HI:(c + 1) * HI], pr[u][:, c * 128:c * 128 + 64 + N],
                                               ident[0:HI, 0:HI])
                last.then_inc(S["tr_s"], 1)

            def values(s, u, wait):
                pe.wait_ge(S["pt_s"], s + 1)
                if wait:
                    pe.wait_ge(S["on_s"], s)
                V9 = 2 * (D + 1)
                for h in range(H):
                    last = nc.tensor.matmul(bank[4][0:NC4 * NI, h * V9:(h + 1) * V9],
                                            pts[u][0:64 + N, h * NC4 * NI:(h + 1) * NC4 * NI],
                                            VBD[0:64 + N, ds(s * (H * V9) + h * V9, V9)], start=True, stop=True)
                last.then_inc(S["av_s"], 1)

            def out_transposes(s, u, wait):
                pe.wait_ge(S["on_s"], s + 1)
                if wait:
                    pe.wait_ge(S["o_done"], s)
                nc.tensor.transpose(bank[5][:, 0:96], on[u][:, :], ident[0:96, 0:96]).then_inc(S["ot_s"], 1)

            def step(s, u, steady=False):
                if steady or s < PAIRS:
                    all_dots(s, u, steady or s >= 1)
                if steady or 3 <= s < PAIRS + 3:
                    transposes(s - 3, 1 - u, steady or s >= 4)
                if steady or 1 <= s < PAIRS + 1:
                    mixing(s - 1, 1 - u, steady or s >= 2)
                if steady or 3 <= s < PAIRS + 3:
                    values(s - 3, 1 - u, steady or s >= 4)
                if steady or s >= 4:
                    out_transposes(s - 4, u, steady or s >= 5)

            def project(b):
                pe.wait_ge(S["o_done"], (b + 1) * BP)
                for g in (2 * b, 2 * b + 1):
                    if b == 1:
                        pe.wait_ge(S["hb_done"], g - 1)
                    nc.tensor.matmul(bank[6 + g % 2][:, 0:GN], w("wproj"), n_sb[:, gcols(g)],
                                     start=True, stop=True).then_inc(S["proj_mm"], 1)

            def center2(b):
                pe.wait_ge(S["h_attn"], 2 * b + 2)
                for g in (2 * b, 2 * b + 1):
                    center(g, 6, "h_attn", k_sb, "2")

            def variance2(b):
                for g in (2 * b, 2 * b + 1):
                    pe.wait_ge(S["xc2_done"], g + 1)
                    variance(g, 6, "2")

            def router_hidden(b):
                for g in (2 * b, 2 * b + 1):
                    pe.wait_ge(S["xn2_done"], g + 1)
                    nc.tensor.matmul(bank[6 + g % 2][0:2 * RH, 0:GN], w("wr1"), q_sb[:, gcols(g)],
                                     start=True, stop=True).then_inc(S["rh_mm"], 1)

            def router_logits(b):
                for g in (2 * b, 2 * b + 1):
                    pe.wait_ge(S["rh_done"], g + 1)
                    nc.tensor.matmul(bank[6 + g % 2][0:2 * E, 0:GN], w("wr2", 2 * RH), slot(rh, g)[0:2 * RH],
                                     start=True, stop=True).then_inc(S["lg_mm"], 1)

            def router_transposes(b):
                pe.wait_ge(S["lg_done"], 2 * b + 2)
                for t in range(BT):
                    last = nc.tensor.transpose(bank[6][0:TT, t * 2 * E:(t + 1) * 2 * E], lg[0:2 * E, t * TT:(t + 1) * TT],
                                               ident[0:2 * E, 0:2 * E])
                last.then_inc(S["lt_mm"], 1)

            def route_weights(b):
                pe.wait_ge(S["route"], (b + 1) * ROUTE_ALL)
                for g in (2 * b, 2 * b + 1):
                    for t in range(4):
                        tt = 4 * g + t
                        last = nc.tensor.transpose(bank[6 + g % 2][0:2 * E1, t * TT:(t + 1) * TT],
                                                   w7[0:TT, tt * 2 * E1:(tt + 1) * 2 * E1], ident[0:TT, 0:TT])
                    last.then_inc(S["wt_mm"], 1)

            def routed_bias(g):
                pe.wait_ge(S["wt_done"], g + 1)
                nc.tensor.matmul(bank[6 + g % 2][:, 0:GN], w("b3", 2 * E1), slot(wt, g)[0:2 * E1],
                                 start=True, stop=True).then_inc(S["b3_mm"], 1)

            def expert_part(n, j):
                g, half = divmod(n, 2)
                if j < 3:
                    m = 3 * n + j
                    if m >= 2:
                        pe.wait_ge(S["h1_done"], m - 1)
                    col = COL["w1"][0] + (3 * half + j) * 128
                    nc.tensor.matmul(bank[m % 2][:, 0:GN], W[:, col:col + 128], q_sb[:, gcols(g)],
                                     start=True, stop=True).then_inc(S["l1"], 1)
                if j >= 1:
                    m = 3 * n + j - 1
                    pe.wait_ge(S["h1_done"], m + 1)
                    if m >= 2:
                        pe.wait_ge(S["h2_done"], m - 1)
                    nc.tensor.matmul(bank[2 + m % 2][:, 0:GN], w("w2")[:, (j - 1) * 128:j * 128], h1[m % 2],
                                     start=True, stop=True).then_inc(S["l2"], 1)

            def third_layer(i):
                n, t = divmod(i, 4)
                g, half = divmod(n, 2)
                if t == 0:
                    pe.wait_ge(S["h2_done"], 3 * (n + 1))
                    pe.wait_ge(S["hb_done"], g + 1)
                bk = bank[4 + i % 2]
                if i >= 2:
                    pe.wait_ge(S["wout_done"], i - 1)
                for j in range(3):
                    nc.tensor.matmul(bk[0:TT, j * 128:(j + 1) * 128], h2[n % 2][:, j * GN + t * TT:j * GN + (t + 1) * TT],
                                     w("w3")[:, j * 128:(j + 1) * 128], start=True, stop=True)
                nc.tensor.matmul(bk[0:TT, 384:448], hb[g % 2][:, t * TT:(t + 1) * TT],
                                 ident[:, 64 * half:64 * half + 64], start=True, stop=True).then_inc(S["l3"], 1)

            step(0, 0)
            qr_operands(1)
            for s in range(1, 6):
                step(s, s % 2)
            pairs(pe, step, 6, 10)
            step(10, 0, True)
            select_q_and_k(1)
            step(11, 1, True)
            step(12, 0, True)
            m_to_columns(1)
            step(13, 1, True)
            grass_keys(1)
            step(14, 0, True)
            step(15, 1, True)
            pe.wait_ge(S["kp_done"], 8)
            pairs(pe, step, 16, 20)
            after = {20: project, 21: center2, 22: variance2, 24: router_hidden, 25: router_logits, 26: router_transposes,
                     31: route_weights}
            for s in range(20, PAIRS + 4):
                step(s, s % 2)
                if s in after:
                    after[s](0)
                elif s == 32:
                    routed_bias(0)
                    routed_bias(1)
                elif s == PAIRS + 2:
                    for j in range(4):
                        expert_part(0, j)
            project(1)
            between = {(1, 1): center2, (1, 3): variance2, (3, 1): router_hidden, (3, 2): router_logits,
                       (3, 3): router_transposes}
            for n in range(1, 5):
                for j in range(4):
                    expert_part(n, j)
                    third_layer(4 * (n - 1) + j)
                    if (n, j) in between:
                        between[n, j](1)
            for j in range(4):
                expert_part(5, j)
            route_weights(1)
            routed_bias(2)
            routed_bias(3)
            for n in range(6, 8):
                third_layer(4 * (n - 2))
                third_layer(4 * (n - 2) + 1)
                expert_part(n, 0)
                third_layer(4 * (n - 2) + 2)
                third_layer(4 * (n - 2) + 3)
                for j in range(1, 4):
                    expert_part(n, j)
            for i in range(24, 32):
                third_layer(i)


def _pack(np, f):
    P = np.zeros((128, NCOLS), np.float32)

    def at(name):
        a, b = COL[name]
        return P[:, a:b]

    tok = f["L0_tok_weight"].reshape(PH, PW, C)
    ta = at("tok").reshape(128, WO, C)
    for w in range(PW):
        v, par = divmod(w, 2)
        ta[64 * par:64 * par + 64, v] = tok[:, w]
    at("tok")[:] = ta.reshape(128, -1)

    V = at("vec")

    def rep(a, times):
        return np.concatenate([a] * times)

    bqkv = f["L0_attn_b_qkv"]
    V[:, VEC["tok_bias"]] = rep(f["L0_tok_bias"], 2)
    for i, n in enumerate(("bq", "bk", "bv")):
        V[:, VEC[n]] = rep(bqkv[i * C:(i + 1) * C], 2)
    V[:, VEC["bproj"]] = rep(f["L0_attn_b_proj"], 2)
    V[0:2 * RH, VEC["br1"]] = rep(f["L0_ffn_router_b1"], 2)
    V[0:2 * E, VEC["br2"]] = rep(f["L0_ffn_router_b2"], 2)
    for j in range(3):
        V[:, VEC[f"b1_{j}"]] = f["L0_ffn_expert_b1"][2 * j:2 * j + 2].reshape(-1)
        V[:, VEC[f"b2_{j}"]] = f["L0_ffn_expert_b2"][2 * j:2 * j + 2].reshape(-1)
    for k in range(3):
        for src, n in (("gamma", "gamma"), ("beta", "beta"), ("mean", "mean"), ("var", "var")):
            V[0:HI, VEC[f"{n}_{k}"]] = np.repeat(f[f"L0_attn_bn_{src}"][k * H:(k + 1) * H], NI)
        V[:, VEC[f"scale_{k}"]] = f[("L0_attn_scale", "L0_attn_riem_scale", "L0_attn_grassman_scale")[k]]
    V[0:HI, VEC["conv_b"]] = np.repeat(f["L0_attn_conv_b"], NI)
    V[:, VEC["eps"]] = EPS

    at("ident")[:] = np.eye(128)
    at("eye64")[0:64] = np.eye(64)
    at("eye64")[64:128] = np.eye(64)
    for half in range(2):
        s = slice(64 * half, 64 * half + 64)
        at("center")[s, s] = np.eye(64) - 1.0 / 64
        at("avg")[s, s] = 1.0 / 64
        for h in range(H):
            at("headmask")[64 * half + D * h:64 * half + D * h + D, h] = 1.0
        at("wq")[s, s] = f["L0_attn_w_qkv"][0:C].T
        at("wk")[s, s] = f["L0_attn_w_qkv"][C:2 * C].T
        at(("wv_a", "wv_b")[half])[s, :] = f["L0_attn_w_qkv"][2 * C:].T
        at("wproj")[s, s] = f["L0_attn_w_proj"].T
        at("wr1")[s, RH * half:RH * half + RH] = f["L0_ffn_router_w1"]
        at("wr2")[RH * half:RH * half + RH, E * half:E * half + E] = f["L0_ffn_router_w2"]
        at("b3")[E1 * half:E1 * half + E, s] = f["L0_ffn_expert_b3"]
        for e in range(E):
            c0 = (3 * half + e // 2) * 128 + 64 * (e % 2)
            at("w1")[s, c0:c0 + 64] = f["L0_ffn_expert_w1"][e]
    for e in range(E):
        r = 64 * (e % 2)
        c0 = (e // 2) * 128 + r
        at("w2")[r:r + 64, c0:c0 + 64] = f["L0_ffn_expert_w2"][e]
        at("w3")[r:r + 64, c0:c0 + 64] = f["L0_ffn_expert_w3"][e]
    at("eye8")[:] = np.eye(D).reshape(-1)
    for k in range(3):
        for i in range(NI):
            rows = at("conv")[i:HI:NI]
            rows[:, k * HI + i:(k + 1) * HI:NI] = f["L0_attn_conv_w"][:, k * H:(k + 1) * H].T
    return P


def kernel(**inputs):
    import numpy as _np
    import concourse.bacc as _bacc
    from concourse.bass_utils import run_bass_kernel_spmd as _run

    f = {k: _np.asarray(v) for k, v in inputs.items()}
    arrays = {"in_x_dram": _np.ascontiguousarray(f["x"]), "in_w_dram": _pack(_np, f)}
    nc = _bacc.Bacc("TRN2", target_bir_lowering=False, num_devices=1)
    f32 = mybir.dt.float32
    x = nc.dram_tensor("in_x_dram", (B, 1, IMG, IMG), f32, kind="ExternalInput").ap()
    wp = nc.dram_tensor("in_w_dram", (128, NCOLS), f32, kind="ExternalInput").ap()
    out = nc.dram_tensor("out_0_dram", (B, N, C), f32, kind="ExternalOutput").ap()
    vit_tower_kernel(nc, x, wp, out)
    r = _run(nc, [arrays], core_ids=[0])
    return r.results[0]["out_0_dram"]
```

```python
from contextlib import ExitStack

import concourse.bass as bass
from concourse import mybir

B, IMG = 64, 224
PH, PW, SH, SW = 64, 25, 64, 12
NH = (IMG - PH) // SH + 1
NW = (IMG - PW) // SW + 1
N = NH * NW
C, H = 64, 8
D = C // H
E, RH = 6, 32
EPS = 1e-5

PAIRS = B // 2
COLS = PAIRS * N
GROUPS = 4
GP = PAIRS // GROUPS
GN = GP * N
NC4 = 4
NI = 13
HI = H * NI
XW = SW * (NW - 1) + PW + 1
SP = GP // 2
SN = SP * N
STEPS = 2 * GROUPS
XG = SP * NH * XW
WO = (PW + 1) // 2
TT = 2 * N
T2 = PAIRS // 2
BP = PAIRS // 2
BT = T2 // 2
EW = 2 * E

ROUTE_LOGITS = 3
ROUTE_TOP = ROUTE_LOGITS + 3 + 3 * (E - 1) + 2
ROUTE_ALL = ROUTE_TOP + 9

def _columns():
    at, where = 0, {}
    for name, n in [("tok", WO * C), ("vec", 32),
                    ("ident", 128), ("eye64", 64), ("center", 128), ("avg", 128), ("headmask", H), ("eye8", D * D),
                    ("wq", 128), ("wk", 128), ("wv_a", C), ("wv_b", C),
                    ("conv", 3 * HI), ("wproj", 128), ("wr1", 2 * RH), ("wr2", 2 * E), ("b3", 128), ("erow", EW),
                    ("w1", 3 * 128), ("w2", 3 * 128), ("w3", 3 * C)]:
        where[name] = (at, at + n)
        at += n
    return where, at


COL, NCOLS = _columns()
VEC = {n: i for i, n in enumerate(
    ["tok_bias", "bq", "bk", "bv", "bproj", "br1", "br2", "b1_0", "b1_1", "b1_2", "b2_0", "b2_1", "b2_2",
     "gamma_0", "gamma_1", "gamma_2", "beta_0", "beta_1", "beta_2", "mean_0", "mean_1", "mean_2",
     "var_0", "var_1", "var_2", "conv_b", "scale_0", "scale_1", "scale_2", "eps"])}


def vit_tower_kernel(nc, x, wpack, out):
    f32 = mybir.dt.float32
    f32r = mybir.dt.float32r
    ALU = mybir.AluOpType
    ACT = mybir.ActivationFunctionType
    AX = mybir.AxisListType.X
    ds = bass.ds

    with ExitStack() as ctx:
        def sb(name, shape, dtype=f32):
            return ctx.enter_context(nc.sbuf_tensor(name, shape, dtype))

        bank = [ctx.enter_context(nc.psum_tensor(f"bank{i}", [128, 512], f32)) for i in range(8)]

        W = sb("weights", [128, NCOLS])

        def w(name, rows=128):
            a, b = COL[name]
            return W[0:rows, a:b]

        def vec(name, rows=128, n=1):
            a = COL["vec"][0] + VEC[name]
            return W[0:rows, a:a + n]

        ident = w("ident")
        h_sb = sb("h", [128, COLS])
        q_sb = sb("q", [128, COLS + 4])
        k_sb = sb("k", [128, COLS])
        n_sb = sb("normed", [128, COLS])
        KBD = sb("kbd", [128, PAIRS * 4 * N])
        VBD = sb("vbd", [128, PAIRS * H * 2 * (D + 1)])
        xc = sb("centered", [128, 2 * GN])
        sq = sb("square", [128, 2 * GN])
        rstd = sb("rstd", [128, 2 * GN])
        convw = sb("convw", [HI, 3 * HI])
        mixc = sb("mixc", [HI, 16])
        qbd = [sb(f"qbd{u}", [128, NC4 * HI]) for u in range(2)]
        on = [sb(f"heads{u}", [96, 128]) for u in range(2)]
        pr = [sb(f"probs{u}", [HI, NC4 * 128]) for u in range(2)]
        pixels_sb = [sb(f"pixels{b}", [128, 4 * XG]) for b in range(2)]
        wt = sb("weights_t", [2 * EW, 2 * GN], f32r)
        erows = sb("erows", [2 * EW, EW * C], f32r)
        xhl = sb("x_parts", [128, 2 * 2 * GN], f32r)
        w1h, w1l = sb("w1_high", [128, 3 * 128], f32r), sb("w1_low", [128, 3 * 128], f32r)
        kbd = KBD[:, :].rearrange("p (a g k n) -> p a g k n", a=PAIRS, g=2, k=2)
        vbd = VBD[:, :].rearrange("p (a h g d) -> p a h g d", a=PAIRS, h=H, g=2)
        pix = [[pixels_sb[i // 2][:, (2 * (i % 2) + half) * XG:(2 * (i % 2) + half + 1) * XG]
                .rearrange("p (a c) -> p a c", c=XW) for half in range(2)] for i in range(4)]

        at = [0]

        def part(b, n):
            a = at[0]
            at[0] += n
            assert at[0] <= 4 * XG
            return pixels_sb[b][:, a:a + n]

        qk_tok = [part(0, 4 * 128) for _ in range(2)]
        gmask = [part(0, 4 * C) for _ in range(2)]
        cgram = part(0, D * 32)
        atop = part(0, D * 32)
        aug = part(0, 4 * D * 3 * D)
        etmp = part(0, 4 * D * 2 * D)
        small = part(0, 256)
        linv = part(0, 4 * D * D)
        ik = part(0, 2 * D * D)
        prods = part(0, D // 2 * 4 * D * D)
        mmat = part(0, 4 * D * D)
        bdm = part(0, BP * 128)
        at[0] = 0
        h1 = [part(0, GN) for _ in range(2)]
        h2 = [part(0, 3 * GN) for _ in range(4)]
        outt = [part(0, GN) for _ in range(2)]
        osb = part(0, T2 * 2 * C)
        at[0] = 0
        er = [part(1, 3 * 2 * NC4 * N) for _ in range(2)]
        tb = [part(1, 2 * NC4 * N) for _ in range(2)]
        pts = [part(1, NC4 * HI) for _ in range(2)]
        rmax = [part(1, 8) for _ in range(2)]
        rmaxc = [part(1, 8) for _ in range(2)]
        rsum = [part(1, 16) for _ in range(2)]
        rh = part(1, 2 * GN)
        lg = part(1, 2 * GN)
        whl = part(1, T2 * 2 * EW)
        NR = 2 * E * BT
        rt = [part(1, NR) for _ in range(7)]
        r1 = [part(1, 2 * BT) for _ in range(4)]

        S = {n: ctx.enter_context(nc.semaphore(n)) for n in """
            w_embed w_rest pix0 pix1 pix2 pix3 pix4 pix5 pix6 pix7 shifted0 shifted1 embed gelu_done prep sqv
            xc_done sq_done cen_mm var_mm std_done rcp_done xn_done
            zero_kbd zero_vbd zero_tok zero_bdm pads
            q_mm k_mm q_done k_done kbd_k tok_tr v_mm qk_tok_done v_tok_done
            gram_mm gmask_done cgram_done atop_cp atop_mm g_mm aug_done elim pivots sqrt_done lu linv_done sel_mm
            mstep z_mm bd_done kp_mm kp_done cvec_mm cvec
            qbd_ready dots sq3 mix rmax_s rmaxc_s sub_s exp_s tr_s pt_s av_s rsum_s on_s ot_s o_done
            proj_mm h_attn xc2_done sq2_done cen2_mm var2_mm std2_done rcp2_done xn2_done
            rh_mm rh_done lg_mm lg_done lt_mm route route_exp wt_mm wt_done
            erows_done w1h_done w1l_done x_high x_low l1 h1_done l2 h2_done spread scaled third outt_done out_tr tiles_out stored
            """.split()}

        block = ctx.enter_context(nc.Block())
        outf = out[:, :, :].rearrange("b n c -> (b n) c")

        def gcols(g):
            return slice(g * GN, (g + 1) * GN)

        def spread_bank(n, j):
            return bank[(4, 6, 7)[j] if n >= 4 else 4]

        def output_bank(g):
            return bank[0 if g == GROUPS - 1 else 5]

        def x_parts(g, half):
            a = (2 * (g % 2) + half) * GN
            return xhl[:, a:a + GN]

        def slot(buf, g):
            return buf[:, (g % 2) * GN:(g % 2 + 1) * GN]

        @block.sync
        def _(sp):
            b = COL["vec"][1]
            sp.dma_start(W[:, 0:b], wpack[:, 0:b]).then_inc(S["w_embed"], 16)
            for e in range(STEPS):
                if e >= 4:
                    sp.wait_ge(S["embed"], e - 3)
                for half in range(2):
                    dst = pix[e % 4][half][64 * half:64 * half + 64, :, :]
                    b0 = half * PAIRS + e * SP
                    for i in range(NH):
                        src = x[b0:b0 + SP, 0, i * SH:i * SH + PH, 0:XW].rearrange("b r c -> r b c")
                        sp.dma_start(dst[:, i:SP * NH:NH, :], src).then_inc(S[f"pix{e}"], 16)
                if e == 2:
                    sp.dma_start(W[:, b:NCOLS], wpack[:, b:NCOLS]).then_inc(S["w_rest"], 16)
            for g in range(GROUPS):
                sp.wait_ge(S["tiles_out"], g + 1)
                tiles = osb[0:TT, g * 4 * 2 * C:(g + 1) * 4 * 2 * C].rearrange("p (t h c) -> p h t c", h=2, c=C)
                for half in range(2):
                    r0 = half * COLS + g * GN
                    sp.dma_start(outf[r0:r0 + GN, :].rearrange("(t p) c -> p t c", p=TT),
                                 tiles[:, half]).then_inc(S["stored"], 16)
            sp.wait_ge(S["stored"], 16 * 2 * GROUPS)

        @block.gpsimd
        def _(pool):
            pool.memset(VBD[:, :], 0.0).then_inc(S["zero_vbd"], 1)
            pool.memset(KBD[:, :], 0.0).then_inc(S["zero_kbd"], 1)
            for u in range(2):
                pool.memset(pr[u][:, :], 0.0).then_inc(S["pads"], 1)
                pool.memset(on[u][:, :], 0.0).then_inc(S["pads"], 1)
            pool.memset(q_sb[:, COLS:COLS + 4], 0.0).then_inc(S["pads"], 1)
            pool.wait_ge(S["pads"], 5)
            for half in range(2):
                pool.wait_ge(S["zero_vbd"], 1 + half)
                pool.memset(vbd[64 * half:64 * half + N, :, :, half, D:D + 1], 1.0).then_inc(S["zero_vbd"], 1)
            pool.wait_ge(S["zero_vbd"], 3)
            pool.wait_ge(S["embed"], 6)
            for u in range(2):
                pool.memset(qk_tok[u], 0.0).then_inc(S["zero_tok"], 1)
            pool.memset(bdm, 0.0).then_inc(S["zero_bdm"], 1)

            def keys(b):
                for g in (2 * b, 2 * b + 1):
                    pool.wait_ge(S["k_done"], g + 1)
                pool.wait_ge(S["q_done"], 2 * b + 2)
                pool.wait_ge(S["zero_kbd"], 1)
                pool.wait_ge(S["zero_bdm"], 1)
                if b == 1:
                    pool.wait_ge(S["kbd_k"], 4)
                    pool.wait_ge(S["atop_mm"], 1)
                for k, src in enumerate((q_sb, k_sb)):
                    pool.tensor_copy(atop.rearrange("p (n a k) -> p a n k", n=D, k=2)[:, :, :, k],
                                     src[:, b * 2 * GN:(b + 1) * 2 * GN].rearrange("p (a n) -> p a n", n=N)[:, :, 0:D])\
                        .then_inc(S["atop_cp"], 1)
                pool.wait_ge(S["atop_cp"], 2 * b + 2)
                for g in (2 * b, 2 * b + 1):
                    for half in range(2):
                        if g + half > 0:
                            pool.wait_ge(S["kbd_k"], 2 * g + half)
                        pool.tensor_copy(kbd[64 * half:64 * half + 64, g * GP:(g + 1) * GP, half, 0, :],
                                         k_sb[64 * half:64 * half + 64, gcols(g)]
                                         .rearrange("p (a n) -> p a n", n=N)).then_inc(S["kbd_k"], 1)

            def block_queries(s, u, wait):
                if wait:
                    pool.wait_ge(S["dots"], 2 * s - 2)
                qv = q_sb[:, ds(s * N, NC4 * NI)].rearrange("p (c i) -> p c i", i=NI)
                pool.tensor_tensor(qbd[u][:, :].rearrange("p (c h i) -> p c h i", c=NC4, h=H),
                                   qv.unsqueeze(2).to_broadcast([128, NC4, H, NI]),
                                   w("headmask").unsqueeze(1).unsqueeze(3).to_broadcast([128, NC4, H, NI]),
                                   ALU.mult).then_inc(S["qbd_ready"], 1)

            keys(0)
            keys(1)
            pool.wait_ge(S["kbd_k"], 2 * GROUPS)
            pool.wait_ge(S["w_rest"], 16)
            for s in range(2):
                block_queries(s, s, False)
            with pool.Fori(0, 4) as i:
                for u in range(2):
                    block_queries(2 * i + (2 + u), u, True)
            pool.tensor_copy(erows[:, :].rearrange("p (e c) -> p e c", e=EW),
                             w("erow", 2 * EW).unsqueeze(2).to_broadcast([2 * EW, EW, C])).then_inc(S["erows_done"], 1)
            pool.tensor_copy(w1h[:, :], w("w1")).then_inc(S["w1h_done"], 1)
            pool.wait_ge(S["w1h_done"], 1)
            pool.tensor_tensor(w1l[:, :], w("w1"), w1h[:, :].bitcast(f32), ALU.subtract).then_inc(S["w1l_done"], 1)
            pool.wait_ge(S["erows_done"], 1)
            pool.wait_ge(S["w1l_done"], 1)
            with pool.Fori(0, (PAIRS - 10) // 2) as i:
                for u in range(2):
                    block_queries(2 * i + (10 + u), u, True)

        def pairs(eng, step, lo, hi):
            assert (hi - lo) % 2 == 0 and lo % 2 == 0
            with eng.Fori(0, (hi - lo) // 2) as i:
                for u in range(2):
                    step(2 * i + (lo + u), u, True)

        @block.scalar
        def _(act):
            def squares_ln(g, tag=""):
                act.wait_ge(S[f"xc{tag}_done"], g + 1)
                if g >= 2:
                    act.wait_ge(S[f"var{tag}_mm"], g - 1)
                nc.scalar.activation(slot(sq, g), slot(xc, g), ACT.Square).then_inc(S[f"sq{tag}_done"], 1)

            def std_ln(g, first_bank, tag=""):
                act.wait_ge(S[f"var{tag}_mm"], g + 1)
                if g >= 2:
                    act.wait_ge(S[f"xn{tag}_done"], g - 1)
                nc.scalar.activation(slot(rstd, g), bank[first_bank + g % 2][:, 0:GN], ACT.Sqrt,
                                     bias=vec("eps")).then_inc(S[f"std{tag}_done"], 1)

            def shift(e):
                act.wait_ge(S[f"pix{e}"], 16 * 2 * NH)
                nc.scalar.activation(pix[e % 4][1][0:64, :, 1:XW:2], pix[e % 4][1][64:128, :, 0:XW - 1:2],
                                     ACT.Copy).then_inc(S["shifted1"], 1)

            def gelu(g):
                act.wait_ge(S["embed"], 2 * g + 2)
                nc.scalar.activation(h_sb[:, gcols(g)], bank[g % 2][:, 0:GN], ACT.Gelu,
                                     bias=vec("tok_bias")).then_inc(S["gelu_done"], 1)

            def q_and_k(g):
                act.wait_ge(S["q_mm"], g + 1)
                nc.scalar.activation(q_sb[:, gcols(g)], bank[6][:, 0:GN], ACT.Identity,
                                     bias=vec("bq")).then_inc(S["q_done"], 1)
                act.wait_ge(S["k_mm"], g + 1)
                nc.scalar.activation(k_sb[:, gcols(g)], bank[7][:, 0:GN], ACT.Identity,
                                     bias=vec("bk")).then_inc(S["k_done"], 1)

            def tokens(t):
                act.wait_ge(S["tok_tr"], t + 1)
                if t >= 2:
                    act.wait_ge(S["gram_mm"], t - 1)
                nc.scalar.activation(qk_tok[t % 2][0:N, :], bank[t % 2][0:N, :], ACT.Copy).then_inc(S["qk_tok_done"], 1)
                act.wait_ge(S["v_mm"], t + 1)
                for half in range(2):
                    r = slice(64 * half, 64 * half + N)
                    nc.scalar.activation(vbd[r, 2 * t:2 * t + 2, :, half, 0:D],
                                         bank[2 + t % 2][r, 0:2 * C].rearrange("p (a h d) -> p a h d", a=2, d=D),
                                         ACT.Copy).then_inc(S["v_tok_done"], 1)

            def pivot_roots(b):
                act.wait_ge(S["pivots"], b + 1)
                nc.scalar.activation(small[:, 32:64], small[:, 0:32], ACT.Sqrt).then_inc(S["sqrt_done"], 1)

            def grass_keys(b):
                for g in (2 * b, 2 * b + 1):
                    act.wait_ge(S["kp_mm"], g + 1)
                    for half in range(2):
                        r = slice(64 * half, 64 * half + 64)
                        nc.scalar.activation(kbd[r, g * GP:(g + 1) * GP, half, 1, :],
                                             bank[4 + 2 * b + g % 2][r, 0:GN].rearrange("p (a n) -> p a n", n=N),
                                             ACT.Copy).then_inc(S["kp_done"], 1)

            act.wait_ge(S["w_embed"], 16)
            nc.scalar.activation(mixc[0:HI, 0:3], vec("var_0", HI, 3), ACT.Sqrt, bias=vec("eps", HI)).then_inc(S["sqv"], 1)
            shift(0)
            shift(1)
            shift(2)
            gelu(0)
            shift(3)
            squares_ln(0)
            shift(4)
            gelu(1)
            std_ln(0, 4)
            squares_ln(1)
            shift(5)
            std_ln(1, 4)
            q_and_k(0)
            shift(6)
            gelu(2)
            shift(7)
            squares_ln(2)
            q_and_k(1)
            act.wait_ge(S["zero_vbd"], 3)
            act.wait_ge(S["zero_tok"], 2)
            for t in range(BT):
                tokens(t)
                if t == 1:
                    std_ln(2, 4)
            pivot_roots(0)
            gelu(3)
            q_and_k(2)
            squares_ln(3)
            tokens(BT)
            tokens(BT + 1)
            std_ln(3, 4)
            for t in range(BT + 2, T2):
                tokens(t)
                if t == BT + 3:
                    q_and_k(3)
                if t == BT + 7:
                    grass_keys(0)

            def squares(s, u, wait):
                if wait:
                    act.wait_ge(S["mix"], s - 1)
                for b in range(2):
                    act.wait_ge(S["dots"], 2 * s + (b + 1))
                    src = bank[b][0:HI, 0:8 * N].rearrange("p (a k n) -> p a k n", a=4, k=2)
                    e = er[u][0:HI, 4 * b * N:4 * (b + 1) * N].rearrange("p (a n) -> p a n", a=4)
                    r = er[u][0:HI, (8 + 8 * b) * N:(16 + 8 * b) * N]
                    nc.scalar.activation(e, src[:, :, 0, :], ACT.Copy).then_inc(S["sq3"], 1)
                    nc.scalar.activation(r, bank[b][0:HI, 0:8 * N], ACT.Square).then_inc(S["sq3"], 1)

            def exponentials(s, u, wait):
                act.wait_ge(S["sub_s"], s + 1)
                if wait:
                    act.wait_ge(S["tr_s"], s - 1)
                dst = pr[u][:, :].rearrange("p (c g n) -> p (c g) n", g=2, n=64)[:, :, 0:N]
                nc.scalar.activation(dst, tb[u][0:HI, :].rearrange("p (a n) -> p a n", n=N),
                                     ACT.Exp).then_inc(S["exp_s"], 1)

            def heads_out(s):
                act.wait_ge(S["ot_s"], s + 1)
                nc.scalar.activation(n_sb[:, ds(s * N, N)], bank[5][:, 0:N], ACT.Identity,
                                     bias=vec("bv")).then_inc(S["o_done"], 1)

            def step(s, u, steady=False):
                if steady or 2 <= s < PAIRS + 2:
                    exponentials(s - 2, u, steady or s >= 4)
                if steady or s < PAIRS:
                    squares(s, u, steady or s >= 2)
                if steady or s >= 4:
                    heads_out(s - 4)

            def x_high(g):
                act.wait_ge(S["xn2_done"], g + 1)
                if g >= 2:
                    act.wait_ge(S["l1"], 6 * (g - 1))
                for half in range(2):
                    r = slice(64 * half, 64 * half + 64)
                    nc.scalar.activation(x_parts(g, half)[r], q_sb[r, gcols(g)], ACT.Copy).then_inc(S["x_high"], 1)

            def router_hidden(b):
                for g in (2 * b, 2 * b + 1):
                    act.wait_ge(S["rh_mm"], g + 1)
                    nc.scalar.activation(slot(rh, g)[0:2 * RH], bank[6 + g % 2][0:2 * RH, 0:GN], ACT.Relu,
                                         bias=vec("br1", 2 * RH)).then_inc(S["rh_done"], 1)

            def router_logits(b):
                for g in (2 * b, 2 * b + 1):
                    act.wait_ge(S["lg_mm"], g + 1)
                    if g >= 2:
                        act.wait_ge(S["lt_mm"], 1)
                    nc.scalar.activation(slot(lg, g)[0:2 * E], bank[6 + g % 2][0:2 * E, 0:GN], ACT.Identity,
                                         bias=vec("br2", 2 * E)).then_inc(S["lg_done"], 1)

            def router_exp(b, k):
                act.wait_ge(S["route"], b * ROUTE_ALL + (ROUTE_LOGITS, ROUTE_TOP)[k])
                nc.scalar.activation(rt[(1, 5)[k]][0:TT, :], rt[(0, 4)[k]][0:TT, :], ACT.Exp).then_inc(S["route_exp"], 1)

            def weights_out(b):
                for g in (2 * b, 2 * b + 1):
                    act.wait_ge(S["wt_mm"], g + 1)
                    if g >= 2:
                        act.wait_ge(S["third"], 3 * (g - 1))
                    nc.scalar.activation(slot(wt, g), bank[6 + g % 2][0:2 * EW, 0:GN],
                                         ACT.Copy).then_inc(S["wt_done"], 1)

            def expert_part(n, j):
                if j < 3:
                    m = 3 * n + j
                    act.wait_ge(S["l1"], m + 1)
                    if m >= 2:
                        act.wait_ge(S["l2"], m - 1)
                    nc.scalar.activation(h1[m % 2], bank[m % 2][:, 0:GN], ACT.Relu,
                                         bias=vec(f"b1_{j}")).then_inc(S["h1_done"], 1)
                if j >= 1:
                    m = 3 * n + j - 1
                    act.wait_ge(S["l2"], m + 1)
                    if n >= 4:
                        act.wait_ge(S["third"], 3 * (n // 2 - 1))
                    nc.scalar.activation(h2[n % 4][:, (j - 1) * GN:j * GN], bank[2 + m % 2][:, 0:GN], ACT.Relu,
                                         bias=vec(f"b2_{j - 1}")).then_inc(S["h2_done"], 1)

            def tiles_out(g):
                act.wait_ge(S["out_tr"], g + 1)
                nc.scalar.activation(osb[0:TT, g * 8 * C:(g + 1) * 8 * C], output_bank(g)[0:TT, 0:8 * C],
                                     ACT.Copy).then_inc(S["tiles_out"], 1)

            for s in range(6):
                step(s, s % 2)
                if s == 4:
                    pivot_roots(1)
            pairs(act, step, 6, 14)
            grass_keys(1)
            pairs(act, step, 14, 20)
            for s in range(20, PAIRS + 4):
                step(s, s % 2)
                if s == 21:
                    squares_ln(0, "2")
                    squares_ln(1, "2")
                elif s == 22:
                    std_ln(0, 6, "2")
                    std_ln(1, 6, "2")
                elif s == 26:
                    x_high(0)
                    x_high(1)
                    router_hidden(0)
                elif s == 27:
                    router_logits(0)
                elif s == 28:
                    router_exp(0, 0)
                elif s == 30:
                    router_exp(0, 1)
                elif s == 32:
                    weights_out(0)
                elif s == PAIRS + 2:
                    for j in range(4):
                        expert_part(0, j)

            for n in range(1, 8):
                for j in range(4):
                    expert_part(n, j)
                    if (n, j) == (1, 1):
                        squares_ln(2, "2")
                        squares_ln(3, "2")
                    elif (n, j) == (1, 3):
                        std_ln(2, 6, "2")
                        std_ln(3, 6, "2")
                    elif (n, j) == (2, 3):
                        x_high(2)
                        router_hidden(1)
                    elif (n, j) == (3, 2):
                        x_high(3)
                    elif (n, j) in ((3, 1), (5, 1)):
                        tiles_out(n // 2 - 1)
                    elif (n, j) == (3, 0):
                        router_logits(1)
                    elif (n, j) == (4, 0):
                        router_exp(1, 0)
                    elif (n, j) == (4, 3):
                        router_exp(1, 1)
                    elif (n, j) == (6, 0):
                        weights_out(1)
            tiles_out(2)
            tiles_out(3)

        @block.vector
        def _(dve):
            count = {}

            def link(ins, name):
                count[name] = count.get(name, 0) + 1
                ins.then_inc(S[name], 1)
                dve.wait_ge(S[name], count[name])

            def shift(e):
                dve.wait_ge(S[f"pix{e}"], 16 * 2 * NH)
                nc.vector.tensor_copy(pix[e % 4][0][64:128, :, 0:XW:2], pix[e % 4][0][0:64, :, 1:XW:2])\
                    .then_inc(S["shifted0"], 1)

            def center(g, first_bank, tag=""):
                dve.wait_ge(S[f"cen{tag}_mm"], g + 1)
                if g >= 2:
                    dve.wait_ge(S[f"xn{tag}_done"], g - 1)
                    dve.wait_ge(S[f"sq{tag}_done"], g - 1)
                nc.vector.tensor_copy(slot(xc, g), bank[first_bank + g % 2][:, 0:GN]).then_inc(S[f"xc{tag}_done"], 1)

            def reciprocal_ln(g, tag="", parts=(0, 1)):
                if parts[0] == 0:
                    dve.wait_ge(S[f"std{tag}_done"], g + 1)
                r = slot(rstd, g)[:, parts[0] * SN:(parts[-1] + 1) * SN]
                nc.vector.reciprocal(r, r).then_inc(S[f"rcp{tag}_done"], len(parts))

            def scale_ln(g, dst, tag=""):
                dve.wait_ge(S[f"rcp{tag}_done"], 2 * (g + 1))
                nc.vector.tensor_tensor(dst[:, gcols(g)], slot(xc, g), slot(rstd, g), ALU.mult).then_inc(S[f"xn{tag}_done"], 1)

            def normalise_ln(g, dst, tag=""):
                reciprocal_ln(g, tag)
                scale_ln(g, dst, tag)

            def gram_blocks(t):
                dve.wait_ge(S["gram_mm"], t + 1)
                gm = gmask[t % 2][:, :].rearrange("p (a h d) -> p a h d", a=4, h=H)
                if t >= 2:
                    dve.wait_ge(S["cgram_done"], t - 1)
                nc.vector.tensor_tensor(gm, bank[6 + t % 2][:, 0:4 * C].rearrange("p (a h d) -> p a h d", a=4, d=D),
                                        w("headmask").unsqueeze(1).unsqueeze(3).to_broadcast([128, 4, H, D]),
                                        ALU.mult).then_inc(S["gmask_done"], 1)
                dve.wait_ge(S["gmask_done"], t + 1)
                if t == BT:
                    dve.wait_ge(S["g_mm"], 1)
                c = 4 * (t % BT)
                nc.vector.tensor_reduce(cgram.rearrange("p (d a) -> p a d", d=D)[:, c:c + 4, :],
                                        gm.rearrange("p a h d -> p a d h"), AX, ALU.add).then_inc(S["cgram_done"], 1)

            A = aug.rearrange("p (h d c) -> p h d c", h=4, d=D)
            rc = small[:, 64:68]
            lrow = small[:, 68:96].rearrange("p (h i) -> p h i", h=4)
            u_ = small[:, 96:128].rearrange("p (h d) -> p h d", h=4)
            npv = small[:, 128:132]
            nrc = small[:, 132:136]
            lc = small[:, 136:164].rearrange("p (h i) -> p h i", h=4)
            sg = small[:, 164:196]

            def qr_load(b):
                if b == 0:
                    dve.wait_ge(S["w_rest"], 16)
                nc.vector.tensor_copy(A[:, :, :, 2 * D:3 * D],
                                      w("eye8").rearrange("p (d c) -> p d c", d=D).unsqueeze(1)
                                      .to_broadcast([128, 4, D, D])).then_inc(S["aug_done"], 1)
                dve.wait_ge(S["atop_mm"], b + 1)
                nc.vector.tensor_copy(A[:, :, :, D:2 * D],
                                      bank[5 + 2 * b][:, 0:256].rearrange("p (n h d) -> p h d n", n=D, h=4)).then_inc(S["aug_done"], 1)
                dve.wait_ge(S["g_mm"], b + 1)
                nc.vector.tensor_copy(A[:, :, :, 0:D],
                                      bank[4 + 2 * b][:, 0:256].rearrange("p (n h d) -> p h d n", n=D, h=4)).then_inc(S["aug_done"], 1)
                dve.wait_ge(S["aug_done"], 3 * (b + 1))

            def eliminate(j):
                m = D - 1 - j
                link(nc.vector.reciprocal(rc, A[:, :, j, j]), "elim")
                link(nc.vector.tensor_tensor(lrow[:, :, 0:m], A[:, :, j, j + 1:D],
                                             rc.unsqueeze(2).to_broadcast([128, 4, m]), ALU.mult), "elim")
                tmp = etmp[:, 0:4 * m * 16].rearrange("p (h i c) -> p h i c", h=4, i=m)
                link(nc.vector.tensor_tensor(tmp, lrow[:, :, 0:m].unsqueeze(3).to_broadcast([128, 4, m, 16]),
                                             A[:, :, j:j + 1, j + 1:j + 17].to_broadcast([128, 4, m, 16]), ALU.mult), "elim")
                rows = A[:, :, j + 1:D, j + 1:j + 17]
                link(nc.vector.tensor_tensor(rows, rows, tmp, ALU.subtract), "elim")

            def qr_scale(b):
                diag = aug.rearrange("p (h r) -> p h r", h=4)[:, :, 0:D * 3 * D:3 * D + 1]
                piv = small[:, 0:32].rearrange("p (h d) -> p h d", h=4)
                nc.vector.tensor_copy(piv, diag).then_inc(S["pivots"], 1)
                dve.wait_ge(S["sqrt_done"], b + 1)
                link(nc.vector.reciprocal(small[:, 32:64], small[:, 32:64]), "elim")
                rs = small[:, 32:64].rearrange("p (h d) -> p h d", h=4)
                both = A[:, :, :, D:3 * D]
                link(nc.vector.tensor_tensor(both, both, rs.unsqueeze(3).to_broadcast([128, 4, D, 2 * D]), ALU.mult), "elim")

            def signs(j):
                tjj = A[:, :, j, D + j]
                link(nc.vector.tensor_scalar(u_[:, :, j], tjj, 0.0, -2.0, ALU.is_ge, ALU.mult), "lu")
                if j == D - 1:
                    return
                m = D - 1 - j
                link(nc.vector.scalar_tensor_tensor(npv, u_[:, :, j], 1.0, tjj, ALU.add, ALU.subtract), "lu")
                link(nc.vector.reciprocal(nrc, npv), "lu")
                link(nc.vector.tensor_tensor(lc[:, :, 0:m], A[:, :, j, D + j + 1:2 * D],
                                             nrc.unsqueeze(2).to_broadcast([128, 4, m]), ALU.mult), "lu")
                tmp = etmp[:, 0:4 * m * m].rearrange("p (h k i) -> p h k i", h=4, k=m)
                link(nc.vector.tensor_tensor(tmp, A[:, :, j + 1:D, D + j].unsqueeze(3).to_broadcast([128, 4, m, m]),
                                             lc[:, :, 0:m].unsqueeze(2).to_broadcast([128, 4, m, m]), ALU.mult), "lu")
                tr = A[:, :, j + 1:D, D + j + 1:2 * D]
                link(nc.vector.tensor_tensor(tr, tr, tmp, ALU.add), "lu")

            def signed_inverse(b):
                link(nc.vector.tensor_scalar(sg, small[:, 96:128], 1.0, None, ALU.add), "lu")
                if b == 1:
                    dve.wait_ge(S["sel_mm"], 1)
                nc.vector.tensor_tensor(linv.rearrange("p (h j c) -> p h j c", h=4, j=D), A[:, :, :, 2 * D:3 * D],
                                        sg.rearrange("p (h d) -> p h d", h=4).unsqueeze(3).to_broadcast([128, 4, D, D]),
                                        ALU.mult).then_inc(S["linv_done"], 1)

            def q_times_k(b):
                dve.wait_ge(S["sel_mm"], b + 1)
                if b == 1:
                    dve.wait_ge(S["z_mm"], 1)
                J = D // 2
                link(nc.vector.tensor_copy(ik, bank[4 + 2 * b][:, 128:256]), "mstep")
                iqv = bank[4 + 2 * b][:, 0:128].rearrange("p (h j c) -> p h j c", h=4, j=J)
                ikv = ik.rearrange("p (h j c) -> p h j c", h=4, j=J)
                for j in range(J):
                    nc.vector.tensor_tensor(prods[:, j * 256:(j + 1) * 256].rearrange("p (h c a) -> p h c a", h=4, c=D),
                                            iqv[:, :, j, :].unsqueeze(3).to_broadcast([128, 4, D, D]),
                                            ikv[:, :, j, :].unsqueeze(2).to_broadcast([128, 4, D, D]),
                                            ALU.mult).then_inc(S["mstep"], 1)
                count["mstep"] += J
                dve.wait_ge(S["mstep"], count["mstep"])
                link(nc.vector.tensor_tensor(prods[:, 0:512], prods[:, 0:512], prods[:, 512:1024], ALU.add), "mstep")
                link(nc.vector.tensor_tensor(mmat.rearrange("p (c h a) -> p h c a", c=D, h=4),
                                             prods[:, 0:256].rearrange("p (h c a) -> p h c a", h=4, c=D),
                                             prods[:, 256:512].rearrange("p (h c a) -> p h c a", h=4, c=D),
                                             ALU.add), "mstep")

            def block_m(b):
                dve.wait_ge(S["z_mm"], b + 1)
                dve.wait_ge(S["zero_bdm"], 1)
                if b == 1:
                    dve.wait_ge(S["kp_mm"], 2)
                z = bank[5 + 2 * b][:, 0:D * BP].rearrange("p (c a) -> p a c", c=D)
                for g in range(2):
                    for half in range(2):
                        r = slice(64 * half, 64 * half + 64)
                        dst = bdm[r, g * GP * 128:(g + 1) * GP * 128].rearrange("p (a c) -> p a c", c=128)
                        nc.vector.tensor_tensor(dst[:, :, 64 * half:64 * half + 64].rearrange("p a (h c) -> p a h c", c=D),
                                                z[r, g * GP:(g + 1) * GP, :].unsqueeze(2).to_broadcast([64, GP, H, D]),
                                                w("headmask")[r].unsqueeze(1).unsqueeze(3).to_broadcast([64, GP, H, D]),
                                                ALU.mult).then_inc(S["bd_done"], 1)

            shift(0)
            shift(1)
            shift(2)
            shift(3)
            center(0, 2)
            shift(4)
            normalise_ln(0, n_sb)
            center(1, 2)
            shift(5)
            dve.wait_ge(S["sqv"], 1)
            dve.wait_ge(S["w_rest"], 16)
            link(nc.vector.reciprocal(mixc[0:HI, 3:6], mixc[0:HI, 0:3]), "prep")
            link(nc.vector.tensor_tensor(mixc[0:HI, 6:9], mixc[0:HI, 3:6], vec("gamma_0", HI, 3), ALU.mult), "prep")
            link(nc.vector.tensor_tensor(mixc[0:HI, 9:12], mixc[0:HI, 6:9], vec("scale_0", HI, 3), ALU.mult), "prep")
            link(nc.vector.tensor_tensor(mixc[0:HI, 12:15], mixc[0:HI, 6:9], vec("mean_0", HI, 3), ALU.mult), "prep")
            link(nc.vector.tensor_tensor(mixc[0:HI, 0:3], vec("beta_0", HI, 3), mixc[0:HI, 12:15], ALU.subtract), "prep")
            normalise_ln(1, n_sb)
            shift(6)
            shift(7)
            center(2, 2)
            for k in range(3):
                cw = w("conv", HI)[:, k * HI:(k + 1) * HI]
                link(nc.vector.tensor_scalar(convw[0:HI, k * HI:(k + 1) * HI], cw, mixc[0:HI, 9 + k:10 + k], None, ALU.mult),
                     "prep")
            for t in range(BT):
                gram_blocks(t)
                if t == 0:
                    normalise_ln(2, n_sb)
            qr_load(0)
            for j in range(D - 1):
                eliminate(j)
            qr_scale(0)
            signs(0)
            center(3, 2)
            signs(1)
            gram_blocks(BT)
            signs(2)
            signs(3)
            normalise_ln(3, n_sb)
            gram_blocks(BT + 1)
            signs(4)
            gram_blocks(BT + 2)
            signs(5)
            signs(6)
            signs(7)
            dve.wait_ge(S["cvec_mm"], 1)
            nc.vector.tensor_tensor(mixc[0:HI, 15:16], bank[4][0:HI, 508:509], vec("conv_b", HI), ALU.add).then_inc(S["cvec"], 1)
            signed_inverse(0)
            gram_blocks(BT + 3)
            q_times_k(0)
            gram_blocks(BT + 4)
            gram_blocks(BT + 5)
            block_m(0)
            gram_blocks(BT + 6)
            gram_blocks(BT + 7)

            dve.wait_ge(S["cvec"], 1)
            cvec = mixc[0:HI, 15:16]

            def keys_out(s, u, wait):
                dve.wait_ge(S["tr_s"], s + 1)
                if wait:
                    dve.wait_ge(S["av_s"], s - 1)
                nc.vector.tensor_copy(pts[u][0:64 + N, :].rearrange("p (h c i) -> p c h i", h=H, c=NC4),
                                      bank[3][0:64 + N, 0:NC4 * HI].rearrange("p (c h i) -> p c h i", c=NC4, h=H))\
                    .then_inc(S["pt_s"], 1)

            def row_max(s, u, wait):
                dve.wait_ge(S["mix"], s + 1)
                if wait:
                    dve.wait_ge(S["exp_s"], s - 1)
                a = bank[2][0:HI, 0:8 * N].rearrange("p (a n) -> p a n", n=N)
                nc.vector.reduce_max(rmax[u][0:HI, :], a, AX).then_inc(S["rmax_s"], 1)
                dve.wait_ge(S["rmax_s"], s + 1)
                nc.vector.tensor_scalar(rmaxc[u][0:HI, :], rmax[u][0:HI, :], cvec, None, ALU.add).then_inc(S["rmaxc_s"], 1)
                dve.wait_ge(S["rmaxc_s"], s + 1)
                nc.vector.scalar_tensor_tensor(tb[u][0:HI, :].rearrange("p (a n) -> p a n", n=N), a, cvec,
                                               rmaxc[u][0:HI, :].unsqueeze(2).to_broadcast([HI, 8, N]),
                                               ALU.add, ALU.subtract).then_inc(S["sub_s"], 1)

            def normalise(s, u, wait):
                dve.wait_ge(S["av_s"], s + 1)
                if wait:
                    dve.wait_ge(S["ot_s"], s - 1)
                o = bank[4][0:NC4 * NI, 0:H * 2 * (D + 1)].rearrange("p (h g d) -> p g h d", h=H, g=2)
                rv = rsum[u][0:NC4 * NI, :].rearrange("p (g h) -> p g h", g=2)
                nc.vector.reciprocal(rv, o[:, :, :, D]).then_inc(S["rsum_s"], 1)
                dve.wait_ge(S["rsum_s"], s + 1)
                nc.vector.tensor_tensor(on[u][0:NC4 * NI, :].rearrange("p (g h d) -> p g h d", g=2, h=H),
                                        o[:, :, :, 0:D], rv.unsqueeze(3).to_broadcast([NC4 * NI, 2, H, D]),
                                        ALU.mult).then_inc(S["on_s"], 1)

            def step_keys(s, u, steady=False):
                if steady or 3 <= s < PAIRS + 3:
                    keys_out(s - 3, 1 - u, steady or s >= 5)

            def step_rows(s, u, steady=False):
                if steady or 1 <= s < PAIRS + 1:
                    row_max(s - 1, 1 - u, steady or s >= 3)
                if steady or 3 <= s < PAIRS + 3:
                    normalise(s - 3, 1 - u, steady or s >= 5)

            def step(s, u, steady=False):
                step_keys(s, u, steady)
                step_rows(s, u, steady)

            def x_low(g):
                for half in range(2):
                    r, other = slice(64 * half, 64 * half + 64), slice(64 * (1 - half), 64 * (1 - half) + 64)
                    dve.wait_ge(S["x_high"], 2 * g + half + 1)
                    nc.vector.tensor_tensor(x_parts(g, half)[other], q_sb[r, gcols(g)],
                                            x_parts(g, half)[r].bitcast(f32), ALU.subtract).then_inc(S["x_low"], 1)

            def residual(b):
                for g in (2 * b, 2 * b + 1):
                    dve.wait_ge(S["proj_mm"], g + 1)
                    nc.vector.scalar_tensor_tensor(k_sb[:, gcols(g)], bank[6 + g % 2][:, 0:GN], vec("bproj"),
                                                   h_sb[:, gcols(g)], ALU.add, ALU.add).then_inc(S["h_attn"], 1)

            def v3(a):
                return a[0:TT, :].rearrange("p (t e) -> p t e", e=E)

            def bc(a):
                return a[0:TT, :].unsqueeze(2).to_broadcast([TT, 2 * BT, E])

            def link_r(ins):
                link(ins, "route")

            pv, rank, ge = v3(rt[2]), v3(rt[3]), v3(rt[6])

            def route_logits(b):
                lt = bank[6][0:TT, 0:NR].rearrange("p (t e) -> p t e", e=E)
                dve.wait_ge(S["lt_mm"], b + 1)
                link_r(nc.vector.reduce_max(r1[0][0:TT, :], lt, AX))
                link_r(nc.vector.tensor_tensor(v3(rt[0]), lt, bc(r1[0]), ALU.subtract))
                link_r(nc.vector.memset(rt[3][0:TT, :], 0.0))
                assert count["route"] == b * ROUTE_ALL + ROUTE_LOGITS

            def route_rank(b):
                dve.wait_ge(S["route_exp"], 2 * b + 1)
                link_r(nc.vector.reduce_sum(r1[1][0:TT, :], v3(rt[1]), AX))
                link_r(nc.vector.reciprocal(r1[1][0:TT, :], r1[1][0:TT, :]))
                link_r(nc.vector.tensor_tensor(v3(rt[2]), v3(rt[1]), bc(r1[1]), ALU.mult))
                rank_shifts(1, 3)

            def rank_shifts(lo, hi):
                for s in range(lo, hi):
                    link_r(nc.vector.tensor_tensor(ge[:, :, s:E], pv[:, :, 0:E - s], pv[:, :, s:E], ALU.is_ge))
                    link_r(nc.vector.tensor_tensor(rank[:, :, s:E], rank[:, :, s:E], ge[:, :, s:E], ALU.add))
                    link_r(nc.vector.scalar_tensor_tensor(rank[:, :, 0:E - s], rank[:, :, 0:E - s], 1.0,
                                                          ge[:, :, s:E], ALU.add, ALU.subtract))

            def route_top(b):
                rank_shifts(3, E)
                link_r(nc.vector.reduce_max(r1[2][0:TT, :], pv, AX))
                link_r(nc.vector.tensor_tensor(v3(rt[4]), pv, bc(r1[2]), ALU.subtract))
                assert count["route"] == b * ROUTE_ALL + ROUTE_TOP

            def route_weights(b):
                link_r(nc.vector.tensor_scalar(rt[3][0:TT, :], rt[3][0:TT, :], 2.0, None, ALU.is_lt))
                dve.wait_ge(S["route_exp"], 2 * b + 2)
                link_r(nc.vector.tensor_tensor(rt[6][0:TT, :], rt[5][0:TT, :], rt[3][0:TT, :], ALU.mult))
                link_r(nc.vector.reduce_sum(r1[3][0:TT, :], v3(rt[6]), AX))
                link_r(nc.vector.reciprocal(r1[0][0:TT, :], r1[3][0:TT, :]))
                link_r(nc.vector.tensor_tensor(v3(rt[0]), v3(rt[6]), bc(r1[0]), ALU.mult))
                dst = whl[0:TT, b * BT * 2 * EW:(b + 1) * BT * 2 * EW].rearrange("p (t k e) -> p t k e", k=2, e=EW)
                wv = rt[0][0:TT, :].rearrange("p (t e) -> p t e", e=EW)
                tv = rt[1][0:TT, :].rearrange("p (t e) -> p t e", e=EW)
                dv = rt[2][0:TT, :].rearrange("p (t e) -> p t e", e=EW)
                link_r(nc.vector.tensor_scalar(tv, wv, 4097.0, None, ALU.mult))
                link_r(nc.vector.tensor_tensor(dv, tv, wv, ALU.subtract))
                link_r(nc.vector.tensor_tensor(dst[:, :, 0, :], tv, dv, ALU.subtract))
                link_r(nc.vector.tensor_tensor(dst[:, :, 1, :], wv, dst[:, :, 0, :], ALU.subtract))
                assert count["route"] == (b + 1) * ROUTE_ALL

            def scale(n, j):
                dve.wait_ge(S["spread"], 3 * n + j + 1)
                dve.wait_ge(S["h2_done"], 3 * n + j + 1)
                a = h2[n % 4][:, j * GN:(j + 1) * GN]
                nc.vector.tensor_tensor(a, a, spread_bank(n, j)[:, 0:GN], ALU.mult).then_inc(S["scaled"], 1)

            def add_residual(g):
                dve.wait_ge(S["third"], 3 * (g + 1))
                if g >= 2:
                    dve.wait_ge(S["out_tr"], g - 1)
                nc.vector.tensor_tensor(outt[g % 2], output_bank(g)[:, 0:GN], k_sb[:, gcols(g)], ALU.add).then_inc(S["outt_done"], 1)

            step(0, 0)
            qr_load(1)
            eliminate(0)
            eliminate(1)
            for s in range(1, 14):
                step_keys(s, s % 2, s >= 6)
                if s in (2, 3):
                    eliminate(2 * s - 1)
                elif s == 5:
                    signs(0)
                elif 6 <= s < 10:
                    signs(2 * s - 11)
                step_rows(s, s % 2, s >= 6)
                if s <= 3:
                    eliminate(2 * s)
                elif s == 4:
                    qr_scale(1)
                elif 6 <= s < 9:
                    signs(2 * s - 10)
                elif s == 9:
                    signed_inverse(1)
                elif s == 10:
                    q_times_k(1)
                elif s == 12:
                    block_m(1)
            pairs(dve, step, 14, 20)
            for s in range(20, PAIRS + 3):
                step_keys(s, s % 2)
                if s == 23:
                    reciprocal_ln(0, "2", (1,))
                elif s == 24:
                    reciprocal_ln(1, "2", (0,))
                elif s == 25:
                    reciprocal_ln(1, "2", (1,))
                elif s == 29:
                    route_rank(0)
                elif s == 30:
                    route_top(0)
                elif s == 32:
                    route_weights(0)
                step_rows(s, s % 2)
                if s == 20:
                    residual(0)
                elif s == 21:
                    center(0, 6, "2")
                    center(1, 6, "2")
                elif s == 22:
                    reciprocal_ln(0, "2", (0,))
                elif s == 23:
                    scale_ln(0, q_sb, "2")
                elif s == 25:
                    scale_ln(1, q_sb, "2")
                elif s == 27:
                    x_low(0)
                    x_low(1)
                elif s == 28:
                    route_logits(0)
            for j in range(3):
                scale(0, j)
            residual(1)
            scale(1, 0)
            center(2, 6, "2")
            center(3, 6, "2")
            scale(1, 1)
            scale(1, 2)
            normalise_ln(2, q_sb, "2")
            scale(2, 0)
            reciprocal_ln(3, "2")
            scale(2, 1)
            scale_ln(3, q_sb, "2")
            scale(2, 2)
            add_residual(0)
            x_low(2)
            scale(3, 0)
            scale(3, 1)
            scale(3, 2)
            route_logits(1)
            x_low(3)
            route_rank(1)
            route_top(1)
            add_residual(1)
            route_weights(1)
            for n in range(4, 8):
                for j in range(3):
                    scale(n, j)
            add_residual(2)
            add_residual(3)

        @block.tensor
        def _(pe):
            def embed(e):
                pe.wait_ge(S["shifted0"], e + 1)
                pe.wait_ge(S["shifted1"], e + 1)
                g = e // 2
                if g >= 2:
                    pe.wait_ge(S["gelu_done"], g - 1)
                if g == 3:
                    pe.wait_ge(S["qk_tok_done"], BT)
                for v in range(WO):
                    for half in range(2):
                        src = pix[e % 4][half][:, :, 2 * v + half:2 * v + half + SW * (NW - 1) + 1:SW]
                        last = nc.tensor.matmul(bank[g % 2][64 * half:64 * half + 64, (e % 2) * SN:(e % 2 + 1) * SN],
                                                w("tok")[:, v * C:(v + 1) * C], src, start=(v == 0), stop=(v == WO - 1))
                last.then_inc(S["embed"], 1)

            def center(g, first_bank, ready, src, tag=""):
                pe.wait_ge(S[ready], g + 1)
                if g >= 2:
                    pe.wait_ge(S[f"xc{tag}_done"], g - 1)
                nc.tensor.matmul(bank[first_bank + g % 2][:, 0:GN], w("center"), src[:, gcols(g)],
                                 start=True, stop=True).then_inc(S[f"cen{tag}_mm"], 1)

            def variance(g, first_bank, tag=""):
                pe.wait_ge(S[f"sq{tag}_done"], g + 1)
                if g >= 2:
                    pe.wait_ge(S[f"std{tag}_done"], g - 1)
                nc.tensor.matmul(bank[first_bank + g % 2][:, 0:GN], w("avg"), slot(sq, g),
                                 start=True, stop=True).then_inc(S[f"var{tag}_mm"], 1)

            def q_and_k(g):
                pe.wait_ge(S["xn_done"], g + 1)
                if g >= 1:
                    pe.wait_ge(S["q_done"], g)
                if g >= 2:
                    pe.wait_ge(S["gmask_done"], BT if g == 2 else BT + 3)
                nc.tensor.matmul(bank[6][:, 0:GN], w("wq"), n_sb[:, gcols(g)], start=True, stop=True).then_inc(S["q_mm"], 1)
                if g >= 1:
                    pe.wait_ge(S["k_done"], g)
                nc.tensor.matmul(bank[7][:, 0:GN], w("wk"), n_sb[:, gcols(g)], start=True, stop=True).then_inc(S["k_mm"], 1)

            def tokens(t):
                if t >= 2:
                    pe.wait_ge(S["qk_tok_done"], t - 1)
                for a in range(2):
                    c = slice((2 * t + a) * N, (2 * t + a + 1) * N)
                    for k, src in enumerate((q_sb, k_sb)):
                        last = nc.tensor.transpose(bank[t % 2][0:N, (2 * a + k) * 128:(2 * a + k + 1) * 128], src[:, c], ident)
                last.then_inc(S["tok_tr"], 1)
                if t >= 2:
                    pe.wait_ge(S["v_tok_done"], 2 * (t - 1))
                for a in range(2):
                    c = slice((2 * t + a) * N, (2 * t + a + 1) * N)
                    for half in range(2):
                        last = nc.tensor.matmul(bank[2 + t % 2][64 * half:64 * half + N, a * C:(a + 1) * C],
                                                n_sb[:, c], w("wv_a" if half == 0 else "wv_b"), start=True, stop=True)
                last.then_inc(S["v_mm"], 1)

            def gram(t):
                pe.wait_ge(S["qk_tok_done"], t + 1)
                if t >= 2:
                    pe.wait_ge(S["gmask_done"], t - 1)
                for a in range(4):
                    for half in range(2):
                        blk = qk_tok[t % 2][:, a * 128 + 64 * half:a * 128 + 64 * half + 64]
                        last = nc.tensor.matmul(bank[6 + t % 2][64 * half:64 * half + 64, a * C:(a + 1) * C], blk, blk,
                                                start=True, stop=True)
                last.then_inc(S["gram_mm"], 1)

            def first_tokens(b, t):
                if t == b * BT:
                    pe.wait_ge(S["q_done"], 2 * b + 1)
                    pe.wait_ge(S["k_done"], 2 * b + 1)
                    pe.wait_ge(S["gelu_done"], 3 + b)
                pe.wait_ge(S["xc_done"], 3 + (b if t > b * BT else 0))
                tokens(t)

            def tokens_and_grams(b):
                for t in range(b * BT + 2, (b + 1) * BT):
                    if t == b * BT + BT // 2:
                        pe.wait_ge(S["q_done"], 2 * b + 2)
                        pe.wait_ge(S["k_done"], 2 * b + 2)
                    tokens(t)
                    gram(t - 1)
                    if t == BT + 3:
                        q_and_k(3)
                    elif t == BT + 4:
                        select_q_and_k(0)
                    elif t == BT + 6:
                        m_to_columns(0)
                    elif t == BT + 7:
                        grass_keys(0)
                gram((b + 1) * BT - 1)

            def to_rows(dst, src):
                for n in range(D):
                    for r0 in range(0, 128, 32):
                        last = nc.tensor.matmul(dst[r0:r0 + 32, n * 32:(n + 1) * 32], src[:, n * 32:(n + 1) * 32],
                                                ident[:, r0:r0 + 32], start=True, stop=True)
                return last

            def qr_operands(b):
                pe.wait_ge(S["atop_cp"], 2 * b + 2)
                pe.wait_ge(S["std_done"], 3 + b)
                if b == 1:
                    pe.wait_ge(S["gmask_done"], T2)
                to_rows(bank[5 + 2 * b], atop).then_inc(S["atop_mm"], 1)
                pe.wait_ge(S["cgram_done"], (b + 1) * BT)
                to_rows(bank[4 + 2 * b], cgram).then_inc(S["g_mm"], 1)

            def select_q_and_k(b):
                pe.wait_ge(S["linv_done"], b + 1)
                pe.wait_ge(S["cvec"], 1)
                li = linv.rearrange("p (h r) -> p h r", h=4)
                for k in range(2):
                    for jh in range(2):
                        last = nc.tensor.matmul(bank[4 + 2 * b][64 * jh:64 * jh + 64, k * 128:(k + 1) * 128], ident[:, k:128:2],
                                                li[:, :, jh * 32:(jh + 1) * 32], start=True, stop=True)
                last.then_inc(S["sel_mm"], 1)

            def m_to_columns(b):
                pe.wait_ge(S["mstep"], (D // 2 + 3) * (b + 1))
                for c in range(D):
                    for i in range(4):
                        last = nc.tensor.matmul(bank[5 + 2 * b][32 * i:32 * i + 32, c * BP:(c + 1) * BP], mmat[:, c * 32:(c + 1) * 32],
                                                w("eye64")[:, BP * i:BP * (i + 1)], start=True, stop=True)
                last.then_inc(S["z_mm"], 1)

            def grass_keys(b):
                for g in (2 * b, 2 * b + 1):
                    pe.wait_ge(S["bd_done"], 4 * b + 2 * (g % 2) + 2)
                    if g % 2 == 1:
                        pe.wait_ge(S["bd_done"], 4 * b + 4)
                    for a in range(GP):
                        p = g * GP + a
                        i = (g % 2) * GP + a
                        for half in range(2):
                            last = nc.tensor.matmul(bank[4 + 2 * b + g % 2][64 * half:64 * half + 64, a * N:(a + 1) * N],
                                                    bdm[:, i * 128 + 64 * half:i * 128 + 64 * half + 64],
                                                    k_sb[:, p * N:(p + 1) * N], start=True, stop=True)
                    last.then_inc(S["kp_mm"], 1)

            pe.wait_ge(S["w_embed"], 16)
            for _ in range(4):
                nc.tensor.matmul(bank[7][:, 0:GN], w("tok")[:, 0:128], w("tok")[:, 0:GN], start=True, stop=True)
            embed(0)
            embed(1)
            embed(2)
            pe.wait_ge(S["w_rest"], 16)
            center(0, 2, "gelu_done", h_sb)
            embed(3)
            variance(0, 4)
            center(1, 2, "gelu_done", h_sb)
            embed(4)
            variance(1, 4)
            q_and_k(0)
            embed(5)
            center(2, 2, "gelu_done", h_sb)
            q_and_k(1)
            variance(2, 4)
            first_tokens(0, 0)
            first_tokens(0, 1)
            pe.wait_ge(S["q_done"], 2)
            pe.wait_ge(S["k_done"], 2)
            gram(0)
            tokens_and_grams(0)
            qr_operands(0)
            embed(6)
            embed(7)
            q_and_k(2)
            pe.wait_ge(S["v_tok_done"], 2 * BT)
            center(3, 2, "gelu_done", h_sb)
            first_tokens(1, BT)
            first_tokens(1, BT + 1)
            pe.wait_ge(S["aug_done"], 3)
            variance(3, 4)
            pe.wait_ge(S["q_done"], 3)
            pe.wait_ge(S["k_done"], 3)
            gram(BT)
            pe.wait_ge(S["prep"], 8)
            pe.wait_ge(S["std_done"], 4)
            for k in range(3):
                last = nc.tensor.matmul(bank[4][0:HI, 508:509], w("conv", HI)[:, k * HI:(k + 1) * HI], mixc[0:HI, k:k + 1],
                                        start=(k == 0), stop=(k == 2))
            last.then_inc(S["cvec_mm"], 1)
            tokens_and_grams(1)

            pe.wait_ge(S["kp_done"], 4)
            pe.wait_ge(S["kbd_k"], 2 * GROUPS)
            pe.wait_ge(S["v_tok_done"], 2 * T2)
            pe.wait_ge(S["qk_tok_done"], T2)

            def all_dots(s, u, wait):
                pe.wait_ge(S["qbd_ready"], s + 1)
                for b in range(2):
                    if wait:
                        pe.wait_ge(S["sq3"], 4 * s - (2 - 2 * b))
                    for c in range(2):
                        ch = 2 * b + c
                        last = nc.tensor.matmul(bank[b][0:HI, c * 4 * N:(c + 1) * 4 * N],
                                                qbd[u][:, ch * HI:(ch + 1) * HI], KBD[:, ds(s * 4 * N, 4 * N)],
                                                start=True, stop=True)
                    last.then_inc(S["dots"], 1)

            def mixing(s, u, wait):
                pe.wait_ge(S["sq3"], 4 * s + 4)
                if wait:
                    pe.wait_ge(S["sub_s"], s)
                r = er[u][0:HI, 8 * N:24 * N].rearrange("p (a k n) -> p a k n", a=8, k=2)
                for k, src in enumerate((er[u][0:HI, 0:8 * N], r[:, :, 0, :], r[:, :, 1, :])):
                    last = nc.tensor.matmul(bank[2][0:HI, 0:8 * N], convw[0:HI, k * HI:(k + 1) * HI], src,
                                            start=(k == 0), stop=(k == 2))
                last.then_inc(S["mix"], 1)

            def transposes(s, u, wait):
                pe.wait_ge(S["exp_s"], s + 1)
                if wait:
                    pe.wait_ge(S["pt_s"], s)
                for c in range(NC4):
                    last = nc.tensor.transpose(bank[3][0:64 + N, c * HI:(c + 1) * HI], pr[u][:, c * 128:c * 128 + 64 + N],
                                               ident[0:HI, 0:HI])
                last.then_inc(S["tr_s"], 1)

            def values(s, u, wait):
                pe.wait_ge(S["pt_s"], s + 1)
                if wait:
                    pe.wait_ge(S["on_s"], s)
                V9 = 2 * (D + 1)
                for h in range(H):
                    last = nc.tensor.matmul(bank[4][0:NC4 * NI, h * V9:(h + 1) * V9],
                                            pts[u][0:64 + N, h * NC4 * NI:(h + 1) * NC4 * NI],
                                            VBD[0:64 + N, ds(s * (H * V9) + h * V9, V9)], start=True, stop=True)
                last.then_inc(S["av_s"], 1)

            def out_transposes(s, u, wait):
                pe.wait_ge(S["on_s"], s + 1)
                if wait:
                    pe.wait_ge(S["o_done"], s)
                nc.tensor.transpose(bank[5][:, 0:96], on[u][:, :], ident[0:96, 0:96]).then_inc(S["ot_s"], 1)

            def step(s, u, steady=False):
                if steady or s < PAIRS:
                    all_dots(s, u, steady or s >= 1)
                if steady or 3 <= s < PAIRS + 3:
                    transposes(s - 3, 1 - u, steady or s >= 4)
                if steady or 1 <= s < PAIRS + 1:
                    mixing(s - 1, 1 - u, steady or s >= 2)
                if steady or 3 <= s < PAIRS + 3:
                    values(s - 3, 1 - u, steady or s >= 4)
                if steady or s >= 4:
                    out_transposes(s - 4, u, steady or s >= 5)

            def project(b):
                pe.wait_ge(S["o_done"], (b + 1) * BP)
                for g in (2 * b, 2 * b + 1):
                    if b == 1:
                        pe.wait_ge(S["wt_done"], 2)
                    nc.tensor.matmul(bank[6 + g % 2][:, 0:GN], w("wproj"), n_sb[:, gcols(g)],
                                     start=True, stop=True).then_inc(S["proj_mm"], 1)

            def center2(b):
                pe.wait_ge(S["h_attn"], 2 * b + 2)
                for g in (2 * b, 2 * b + 1):
                    center(g, 6, "h_attn", k_sb, "2")

            def variance2(b):
                for g in (2 * b, 2 * b + 1):
                    pe.wait_ge(S["xc2_done"], g + 1)
                    variance(g, 6, "2")

            def router_hidden(b):
                for g in (2 * b, 2 * b + 1):
                    pe.wait_ge(S["xn2_done"], g + 1)
                    nc.tensor.matmul(bank[6 + g % 2][0:2 * RH, 0:GN], w("wr1"), q_sb[:, gcols(g)],
                                     start=True, stop=True).then_inc(S["rh_mm"], 1)

            def router_logits(b):
                for g in (2 * b, 2 * b + 1):
                    pe.wait_ge(S["rh_done"], g + 1)
                    nc.tensor.matmul(bank[6 + g % 2][0:2 * E, 0:GN], w("wr2", 2 * RH), slot(rh, g)[0:2 * RH],
                                     start=True, stop=True).then_inc(S["lg_mm"], 1)

            def router_transposes(b):
                pe.wait_ge(S["lg_done"], 2 * b + 2)
                for t in range(BT):
                    last = nc.tensor.transpose(bank[6][0:TT, t * 2 * E:(t + 1) * 2 * E], lg[0:2 * E, t * TT:(t + 1) * TT],
                                               ident[0:2 * E, 0:2 * E])
                last.then_inc(S["lt_mm"], 1)

            def route_weights(b):
                pe.wait_ge(S["route"], (b + 1) * ROUTE_ALL)
                for g in (2 * b, 2 * b + 1):
                    for t in range(4):
                        tt = 4 * g + t
                        last = nc.tensor.transpose(bank[6 + g % 2][0:2 * EW, t * TT:(t + 1) * TT],
                                                   whl[0:TT, tt * 2 * EW:(tt + 1) * 2 * EW], ident[0:TT, 0:TT])
                    last.then_inc(S["wt_mm"], 1)

            def expert_part(n, j):
                g, half = divmod(n, 2)
                if j < 3:
                    m = 3 * n + j
                    if m >= 2:
                        pe.wait_ge(S["h1_done"], m - 1)
                    if j == 0:
                        pe.wait_ge(S["w1l_done"], 1)
                        pe.wait_ge(S["x_low"], 2 * g + half + 1)
                    for k, wk in enumerate((w1h, w1l)):
                        last = nc.tensor.matmul(bank[m % 2][:, 0:GN], wk[:, j * 128:(j + 1) * 128], x_parts(g, half),
                                                start=(k == 0), stop=(k == 1))
                    last.then_inc(S["l1"], 1)
                if j >= 1:
                    m = 3 * n + j - 1
                    pe.wait_ge(S["h1_done"], m + 1)
                    if m >= 2:
                        pe.wait_ge(S["h2_done"], m - 1)
                    nc.tensor.matmul(bank[2 + m % 2][:, 0:GN], w("w2")[:, (j - 1) * 128:j * 128], h1[m % 2],
                                     start=True, stop=True).then_inc(S["l2"], 1)

            def spread(n, j):
                g, half = divmod(n, 2)
                if j == 0:
                    pe.wait_ge(S["wt_done"], 4 if n >= 4 else g + 1)
                    pe.wait_ge(S["erows_done"], 1)
                if n > 4:
                    pe.wait_ge(S["scaled"], 3 * (n - 1) + j + 1)
                elif 3 * n + j > 0:
                    pe.wait_ge(S["scaled"], min(3 * n + j, 12))
                else:
                    pe.wait_ge(S["on_s"], PAIRS)
                col = (E * half + 2 * j) * C
                nc.tensor.matmul(spread_bank(n, j)[:, 0:GN], erows[:, col:col + 128], slot(wt, g), start=True, stop=True).then_inc(S["spread"], 1)

            def third_layer(g, j):
                if j == 0:
                    if g in (1, 2):
                        pe.wait_ge(S["tiles_out"], g)
                    nc.tensor.matmul(output_bank(g)[:, 0:GN], w("b3", 2 * EW), slot(wt, g).bitcast(f32), start=True, stop=False)
                pe.wait_ge(S["scaled"], 3 * (2 * g + 1) + j + 1)
                for half in range(2):
                    last = nc.tensor.matmul(output_bank(g)[64 * half:64 * half + 64, 0:GN], w("w3")[:, j * C:(j + 1) * C],
                                            h2[(2 * g + half) % 4][:, j * GN:(j + 1) * GN], start=False, stop=(j == 2))
                last.then_inc(S["third"], 1)

            def output_tiles(g):
                pe.wait_ge(S["outt_done"], g + 1)
                for t in range(4):
                    last = nc.tensor.transpose(output_bank(g)[0:TT, t * 2 * C:(t + 1) * 2 * C], outt[g % 2][:, t * TT:(t + 1) * TT], ident)
                last.then_inc(S["out_tr"], 1)

            step(0, 0)
            qr_operands(1)
            for s in range(1, 6):
                step(s, s % 2)
            pairs(pe, step, 6, 10)
            step(10, 0, True)
            select_q_and_k(1)
            step(11, 1, True)
            step(12, 0, True)
            m_to_columns(1)
            step(13, 1, True)
            grass_keys(1)
            step(14, 0, True)
            step(15, 1, True)
            pe.wait_ge(S["kp_done"], 8)
            pairs(pe, step, 16, 20)
            for s in range(20, PAIRS + 4):
                step(s, s % 2)
                if s == 20:
                    project(0)
                elif s == 21:
                    center2(0)
                elif s == 22:
                    variance2(0)
                elif s == 26:
                    router_hidden(0)
                elif s == 27:
                    router_logits(0)
                elif s == 28:
                    router_transposes(0)
                elif s == 32:
                    route_weights(0)
                elif s == PAIRS + 2:
                    for j in range(4):
                        expert_part(0, j)
                        if j >= 1:
                            spread(0, j - 1)
            project(1)
            for n in range(1, 8):
                for j in range(4):
                    expert_part(n, j)
                    if n <= 3 and j >= 1:
                        spread(n, j - 1)
                    elif n >= 6 and j >= 1:
                        spread(n - 2, j - 1)
                    if n in (2, 4) and j >= 1:
                        third_layer(n // 2 - 1, j - 1)
                    elif n in (3, 5) and j == 0:
                        output_tiles(n // 2 - 1)
                    if (n, j) == (1, 1):
                        center2(1)
                    elif (n, j) == (1, 3):
                        variance2(1)
                    elif (n, j) == (2, 3):
                        router_hidden(1)
                    elif (n, j) == (3, 0):
                        router_logits(1)
                    elif (n, j) == (3, 1):
                        router_transposes(1)
                    elif (n, j) == (5, 2):
                        route_weights(1)
            for j in range(3):
                spread(6, j)
            for j in range(3):
                third_layer(2, j)
                spread(7, j)
            third_layer(3, 0)
            output_tiles(2)
            third_layer(3, 1)
            third_layer(3, 2)
            output_tiles(3)


def _pack(np, f):
    P = np.zeros((128, NCOLS), np.float32)

    def at(name):
        a, b = COL[name]
        return P[:, a:b]

    tok = f["L0_tok_weight"].reshape(PH, PW, C)
    ta = at("tok").reshape(128, WO, C)
    for w in range(PW):
        v, par = divmod(w, 2)
        ta[64 * par:64 * par + 64, v] = tok[:, w]
    at("tok")[:] = ta.reshape(128, -1)

    V = at("vec")

    def rep(a, times):
        return np.concatenate([a] * times)

    bqkv = f["L0_attn_b_qkv"]
    V[:, VEC["tok_bias"]] = rep(f["L0_tok_bias"], 2)
    for i, n in enumerate(("bq", "bk", "bv")):
        V[:, VEC[n]] = rep(bqkv[i * C:(i + 1) * C], 2)
    V[:, VEC["bproj"]] = rep(f["L0_attn_b_proj"], 2)
    V[0:2 * RH, VEC["br1"]] = rep(f["L0_ffn_router_b1"], 2)
    V[0:2 * E, VEC["br2"]] = rep(f["L0_ffn_router_b2"], 2)
    for j in range(3):
        V[:, VEC[f"b1_{j}"]] = f["L0_ffn_expert_b1"][2 * j:2 * j + 2].reshape(-1)
        V[:, VEC[f"b2_{j}"]] = f["L0_ffn_expert_b2"][2 * j:2 * j + 2].reshape(-1)
    for k in range(3):
        for src, n in (("gamma", "gamma"), ("beta", "beta"), ("mean", "mean"), ("var", "var")):
            V[0:HI, VEC[f"{n}_{k}"]] = np.repeat(f[f"L0_attn_bn_{src}"][k * H:(k + 1) * H], NI)
        V[:, VEC[f"scale_{k}"]] = f[("L0_attn_scale", "L0_attn_riem_scale", "L0_attn_grassman_scale")[k]]
    V[0:HI, VEC["conv_b"]] = np.repeat(f["L0_attn_conv_b"], NI)
    V[:, VEC["eps"]] = EPS

    at("ident")[:] = np.eye(128)
    at("eye64")[0:64] = np.eye(64)
    at("eye64")[64:128] = np.eye(64)
    for half in range(2):
        s = slice(64 * half, 64 * half + 64)
        at("center")[s, s] = np.eye(64) - 1.0 / 64
        at("avg")[s, s] = 1.0 / 64
        for h in range(H):
            at("headmask")[64 * half + D * h:64 * half + D * h + D, h] = 1.0
        at("wq")[s, s] = f["L0_attn_w_qkv"][0:C].T
        at("wk")[s, s] = f["L0_attn_w_qkv"][C:2 * C].T
        at(("wv_a", "wv_b")[half])[s, :] = f["L0_attn_w_qkv"][2 * C:].T
        at("wproj")[s, s] = f["L0_attn_w_proj"].T
        at("wr1")[s, RH * half:RH * half + RH] = f["L0_ffn_router_w1"]
        at("wr2")[RH * half:RH * half + RH, E * half:E * half + E] = f["L0_ffn_router_w2"]
        for part in range(2):
            r = EW * part + E * half
            at("b3")[r:r + E, s] = f["L0_ffn_expert_b3"]
            at("erow")[r:r + E, E * half:E * half + E] = np.eye(E)
        for e in range(E):
            c0 = (e // 2) * 128 + 64 * (e % 2)
            at("w1")[s, c0:c0 + 64] = f["L0_ffn_expert_w1"][e]
    for e in range(E):
        r = 64 * (e % 2)
        c0 = (e // 2) * 128 + r
        at("w2")[r:r + 64, c0:c0 + 64] = f["L0_ffn_expert_w2"][e]
        at("w3")[r:r + 64, (e // 2) * C:(e // 2 + 1) * C] = f["L0_ffn_expert_w3"][e]
    at("eye8")[:] = np.eye(D).reshape(-1)
    for k in range(3):
        for i in range(NI):
            rows = at("conv")[i:HI:NI]
            rows[:, k * HI + i:(k + 1) * HI:NI] = f["L0_attn_conv_w"][:, k * H:(k + 1) * H].T
    return P


def kernel(**inputs):
    import numpy as _np
    import concourse.bacc as _bacc
    from concourse.bass_utils import run_bass_kernel_spmd as _run

    f = {k: _np.asarray(v) for k, v in inputs.items()}
    arrays = {"in_x_dram": _np.ascontiguousarray(f["x"]), "in_w_dram": _pack(_np, f)}
    nc = _bacc.Bacc("TRN2", target_bir_lowering=False, num_devices=1)
    f32 = mybir.dt.float32
    x = nc.dram_tensor("in_x_dram", (B, 1, IMG, IMG), f32, kind="ExternalInput").ap()
    wp = nc.dram_tensor("in_w_dram", (128, NCOLS), f32, kind="ExternalInput").ap()
    out = nc.dram_tensor("out_0_dram", (B, N, C), f32, kind="ExternalOutput").ap()
    vit_tower_kernel(nc, x, wp, out)
    r = _run(nc, [arrays], core_ids=[0])
    return r.results[0]["out_0_dram"]
```
